# Optimizing a Trainium2 kernel written in Bass

```python
import numpy as np
import jax
import jax.numpy as jnp

def _softmax(x, axis=-1):
    return jax.nn.softmax(x, axis=axis)
def _gelu(x):
    return jax.nn.gelu(x, approximate=True)
def _silu(x):
    return jax.nn.silu(x)
def _sigmoid(x):
    return jax.nn.sigmoid(x)
def _layernorm(x, axis=-1, eps=1e-5):
    m = jnp.mean(x, axis=axis, keepdims=True)
    v = jnp.var(x, axis=axis, keepdims=True)
    return (x - m) / jnp.sqrt(v + eps)
def _scatter_add(tgt, idx, src, axis=0):
    return tgt.at[idx].add(src)
def _segment_sum(src, seg, n):
    return jax.ops.segment_sum(src, seg, n)

kernel_name = 'mk_conv_preact_d2_conv_nchw64_c01b0d'

def setup_inputs(seed: int = 0):
    np.random.seed(seed)
    _w = jnp.asarray
    def _rec_inputs():
        import jax
        import jax.numpy as jnp
        _gk = jax.random.key(seed)
        x = -0.0003929 + 0.9999 * jax.random.normal(jax.random.fold_in(_gk, 1), (4, 64, 256, 256), jnp.float32)
        return x
    x = _rec_inputs()
    def _L0_conv_setup():
        import jax, jax.numpy as jnp
        import numpy as np
        PATCH = 8

        def _to_patches(t):
            b, c, H, W = t.shape
            t = t.reshape(b, c, H // PATCH, PATCH, W // PATCH, PATCH)
            return t.transpose(0, 1, 2, 4, 3, 5)

        def _from_patches(t):
            b, c, h, w, p1, p2 = t.shape
            return t.transpose(0, 1, 2, 4, 3, 5).reshape(b, c, h * p1, w * p2)
        key = jax.random.key(seed)
        ks = jax.random.split(key, 8)
        dim = 64
        hid = dim * 6
        x = jax.random.normal(ks[0], (4, dim, 256, 256), dtype=jnp.float32)
        w_hidden = jax.random.normal(ks[1], (hid, dim), dtype=jnp.float32) * 0.05
        b_hidden = jax.random.normal(ks[2], (hid,), dtype=jnp.float32) * 0.02
        w_dw = jax.random.normal(ks[3], (hid, 3, 3), dtype=jnp.float32) * 0.1
        b_dw = jax.random.normal(ks[4], (hid,), dtype=jnp.float32) * 0.02
        w_proj = jax.random.normal(ks[5], (dim, dim * 2), dtype=jnp.float32) * 0.05
        b_proj = jax.random.normal(ks[6], (dim,), dtype=jnp.float32) * 0.02
        ln_w = jnp.ones((dim * 2,), dtype=jnp.float32)
        ln_b = jnp.zeros((dim * 2,), dtype=jnp.float32)
        return {'x': x, 'w_hidden': w_hidden, 'b_hidden': b_hidden, 'w_dw': w_dw, 'b_dw': b_dw, 'w_proj': w_proj, 'b_proj': b_proj, 'ln_w': ln_w, 'ln_b': ln_b}
    _L0_conv_all = _L0_conv_setup()
    _L0_conv_in = {k: v for k, v in _L0_conv_all.items() if k in ('w_hidden', 'b_hidden', 'w_dw', 'b_dw', 'w_proj', 'b_proj', 'ln_w', 'ln_b', )}
    del _L0_conv_all

    def _L1_conv_setup():
        import jax, jax.numpy as jnp
        import numpy as np
        BN_EPS = 1e-05

        def _involution(x, w_reduce, b_reduce, bn_gamma, bn_beta, w_span, b_span):
            B, C, H, W = x.shape
            xp = jnp.pad(x, ((0, 0), (0, 0), (1, 1), (1, 1)))
            patches = jnp.stack([xp[:, :, i:i + H, j:j + W] for i in range(3) for j in range(3)], axis=2)
            r = jnp.einsum('oc,bchw->bohw', w_reduce, x) + b_reduce[None, :, None, None]
            mu = r.mean(axis=(0, 2, 3), keepdims=True)
            var = r.var(axis=(0, 2, 3), keepdims=True)
            rn = (r - mu) * jax.lax.rsqrt(var + BN_EPS)
            rn = jax.nn.relu(rn * bn_gamma[None, :, None, None] + bn_beta[None, :, None, None])
            kern = jnp.einsum('kc,bchw->bkhw', w_span, rn) + b_span[None, :, None, None]
            return jnp.einsum('bkhw,bckhw->bchw', kern, patches)
        key = jax.random.key(seed)
        ks = jax.random.split(key, 4)
        B, C, H, W = (8, 64, 128, 128)
        return {'x': jax.random.normal(ks[0], (B, C, H, W), jnp.float32), 'w_reduce': jax.random.normal(ks[1], (C, C), jnp.float32) * 0.05, 'b_reduce': jnp.zeros((C,), jnp.float32), 'bn_gamma': jnp.ones((C,), jnp.float32), 'bn_beta': jnp.zeros((C,), jnp.float32), 'w_span': jax.random.normal(ks[2], (9, C), jnp.float32) * 0.05, 'b_span': jnp.zeros((9,), jnp.float32), 'w_conv2': jax.random.normal(ks[3], (C, C, 3, 3), jnp.float32) * 0.02, 'b_conv2': jnp.zeros((C,), jnp.float32)}
    _L1_conv_all = _L1_conv_setup()
    _L1_conv_in = {k: v for k, v in _L1_conv_all.items() if k in ('w_reduce', 'b_reduce', 'bn_gamma', 'bn_beta', 'w_span', 'b_span', 'w_conv2', 'b_conv2', )}
    del _L1_conv_all

    return {
        "x": x,
        "L0_conv_w_hidden": _L0_conv_in["w_hidden"],
        "L0_conv_b_hidden": _L0_conv_in["b_hidden"],
        "L0_conv_w_dw": _L0_conv_in["w_dw"],
        "L0_conv_b_dw": _L0_conv_in["b_dw"],
        "L0_conv_w_proj": _L0_conv_in["w_proj"],
        "L0_conv_b_proj": _L0_conv_in["b_proj"],
        "L0_conv_ln_w": _L0_conv_in["ln_w"],
        "L0_conv_ln_b": _L0_conv_in["ln_b"],
        "L1_conv_w_reduce": _L1_conv_in["w_reduce"],
        "L1_conv_b_reduce": _L1_conv_in["b_reduce"],
        "L1_conv_bn_gamma": _L1_conv_in["bn_gamma"],
        "L1_conv_bn_beta": _L1_conv_in["bn_beta"],
        "L1_conv_w_span": _L1_conv_in["w_span"],
        "L1_conv_b_span": _L1_conv_in["b_span"],
        "L1_conv_w_conv2": _L1_conv_in["w_conv2"],
        "L1_conv_b_conv2": _L1_conv_in["b_conv2"],
    }

def reference(x, L0_conv_w_hidden, L0_conv_b_hidden, L0_conv_w_dw, L0_conv_b_dw, L0_conv_w_proj, L0_conv_b_proj, L0_conv_ln_w, L0_conv_ln_b, L1_conv_w_reduce, L1_conv_b_reduce, L1_conv_bn_gamma, L1_conv_bn_beta, L1_conv_w_span, L1_conv_b_span, L1_conv_w_conv2, L1_conv_b_conv2):
    import jax
    import jax.numpy as jnp
    def _L0_conv_ref(x, w_hidden, b_hidden, w_dw, b_dw, w_proj, b_proj, ln_w, ln_b):
        import jax, jax.numpy as jnp
        import numpy as np
        PATCH = 8

        def _to_patches(t):
            b, c, H, W = t.shape
            t = t.reshape(b, c, H // PATCH, PATCH, W // PATCH, PATCH)
            return t.transpose(0, 1, 2, 4, 3, 5)

        def _from_patches(t):
            b, c, h, w, p1, p2 = t.shape
            return t.transpose(0, 1, 2, 4, 3, 5).reshape(b, c, h * p1, w * p2)
        hidden = jnp.einsum('bchw,oc->bohw', x, w_hidden) + b_hidden[None, :, None, None]
        hid = hidden.shape[1]
        hidden = jax.lax.conv_general_dilated(hidden, w_dw[:, None, :, :], window_strides=(1, 1), padding='SAME', feature_group_count=hid, dimension_numbers=('NCHW', 'OIHW', 'NCHW')) + b_dw[None, :, None, None]
        q, k, v = jnp.split(hidden, 3, axis=1)
        q_fft = jnp.fft.rfft2(_to_patches(q))
        k_fft = jnp.fft.rfft2(_to_patches(k))
        out = jnp.fft.irfft2(q_fft * k_fft, s=(PATCH, PATCH))
        out = _from_patches(out).astype(x.dtype)
        mu = jnp.mean(out, axis=1, keepdims=True)
        var = jnp.var(out, axis=1, keepdims=True)
        out = (out - mu) / jnp.sqrt(var + 1e-05) * ln_w[None, :, None, None] + ln_b[None, :, None, None]
        output = v * out
        return jnp.einsum('bchw,oc->bohw', output, w_proj) + b_proj[None, :, None, None]

    def _L1_conv_ref(x, w_reduce, b_reduce, bn_gamma, bn_beta, w_span, b_span, w_conv2, b_conv2):
        import jax, jax.numpy as jnp
        import numpy as np
        BN_EPS = 1e-05

        def _involution(x, w_reduce, b_reduce, bn_gamma, bn_beta, w_span, b_span):
            B, C, H, W = x.shape
            xp = jnp.pad(x, ((0, 0), (0, 0), (1, 1), (1, 1)))
            patches = jnp.stack([xp[:, :, i:i + H, j:j + W] for i in range(3) for j in range(3)], axis=2)
            r = jnp.einsum('oc,bchw->bohw', w_reduce, x) + b_reduce[None, :, None, None]
            mu = r.mean(axis=(0, 2, 3), keepdims=True)
            var = r.var(axis=(0, 2, 3), keepdims=True)
            rn = (r - mu) * jax.lax.rsqrt(var + BN_EPS)
            rn = jax.nn.relu(rn * bn_gamma[None, :, None, None] + bn_beta[None, :, None, None])
            kern = jnp.einsum('kc,bchw->bkhw', w_span, rn) + b_span[None, :, None, None]
            return jnp.einsum('bkhw,bckhw->bchw', kern, patches)
        z = jax.nn.softplus(_involution(x, w_reduce, b_reduce, bn_gamma, bn_beta, w_span, b_span))
        y = jax.lax.conv_general_dilated(z, w_conv2, window_strides=(1, 1), padding=((1, 1), (1, 1)))
        y = y + b_conv2[None, :, None, None]
        return jax.nn.softplus(y)

    def _gn(v, G=32, eps=1e-5):
        B_, C_, H_, W_ = v.shape
        g = v.reshape(B_, G, C_ // G, H_, W_)
        m = jnp.mean(g, axis=(2, 3, 4), keepdims=True)
        s = jnp.var(g, axis=(2, 3, 4), keepdims=True)
        return ((g - m) / jnp.sqrt(s + eps)).reshape(v.shape)

    def _ln_c(v, eps=1e-6):
        m = jnp.mean(v, axis=1, keepdims=True)
        s = jnp.var(v, axis=1, keepdims=True)
        return (v - m) / jnp.sqrt(s + eps)

    def _ln_t(v, eps=1e-5):
        m = jnp.mean(v, axis=-1, keepdims=True)
        s = jnp.var(v, axis=-1, keepdims=True)
        return (v - m) / jnp.sqrt(s + eps)

    def _to_tokens(v):
        B_, C_, H_, W_ = v.shape
        return v.reshape(B_, C_, H_ * W_).transpose(0, 2, 1)
    def _from_tokens(t, like):
        B_, C_, H_, W_ = like.shape
        return t.transpose(0, 2, 1).reshape(B_, C_, H_, W_)

    x = x + _L0_conv_ref(_gn(x), L0_conv_w_hidden, L0_conv_b_hidden, L0_conv_w_dw, L0_conv_b_dw, L0_conv_w_proj, L0_conv_b_proj, L0_conv_ln_w, L0_conv_ln_b)
    x = x + _L1_conv_ref(_gn(x), L1_conv_w_reduce, L1_conv_b_reduce, L1_conv_bn_gamma, L1_conv_bn_beta, L1_conv_w_span, L1_conv_b_span, L1_conv_w_conv2, L1_conv_b_conv2)
    return x


_drawn_inputs = setup_inputs


def setup_inputs(seed=0):
    import zlib

    import numpy as np

    out = dict(_drawn_inputs(seed))
    spreads = {'L0_conv_ln_w': (1.0, 0.6),
     'L0_conv_ln_b': (0.0, 0.8),
     'L1_conv_b_reduce': (0.0, 0.8),
     'L1_conv_bn_gamma': (1.0, 0.6),
     'L1_conv_bn_beta': (0.0, 0.8),
     'L1_conv_b_span': (0.0, 0.479),
     'L1_conv_b_conv2': (0.0, 0.1)}
    factors = {'L0_conv_b_hidden': 8.0, 'L0_conv_b_proj': 3.08}
    for name, (base, spread) in spreads.items():
        noise = np.random.default_rng([zlib.crc32(name.encode()), seed]).standard_normal(out[name].shape)
        drawn = base * np.exp(spread * noise) if base else spread * noise
        out[name] = jnp.asarray(drawn.astype(out[name].dtype))
    for name, factor in factors.items():
        out[name] = (out[name] * factor).astype(out[name].dtype)
    return out
```

```python
from contextlib import ExitStack

import numpy as np

import concourse.bass as bass
from concourse import mybir

ALU = mybir.AluOpType
ACT = mybir.ActivationFunctionType
AX_X = mybir.AxisListType.X
F32 = mybir.dt.float32
F16 = mybir.dt.float16
RMAX = bass.bass_isa.ReduceOp.max

P = 128
C = 64
W = 256
WP = W + 2
PATCH = 8
R = 8
HID = 6 * C
KQ = 256
XTRA = 9
GN_EPS = 1e-5
LN_EPS = 1e-5
BN_EPS = 1e-5
WSCALE = 256.0
GCOL = 64
ORDER = [0, 2, 1, 3]
TAPS = [(dr, dc) for dr in (-1, 0, 1) for dc in (-1, 0, 1)]


def strips_of_layer1(strips):
    return (strips + 1 + 3) // 4 * 4


def build_program(nc, A, NI, S):
    NS = NI * S
    ROWS = NS * R
    NG = NS * 4
    NB = NS // 2
    N1 = strips_of_layer1(NS)
    Y1R = R * (N1 + 1) + 10
    y1 = nc.dram_tensor("y1_scratch", (C, Y1R, W), F32, kind="Internal").ap()
    y1_by_parity = y1.rearrange("c (r two) w -> c two r w", two=2)
    out_by_parity = A["out"].rearrange("c (r two) w -> c two r w", two=2)

    with ExitStack() as ctx:
        def sb(name, shape, dt=F32):
            return ctx.enter_context(nc.sbuf_tensor(name, shape, dt))

        def sem(name):
            return ctx.enter_context(nc.semaphore(name))

        bank = [ctx.enter_context(nc.psum_tensor(f"bank{i}", [P, 512], F32)) for i in range(8)]

        gn_scale = sb("gn_scale", [P, 2, NI])
        gn_bias = sb("gn_bias", [P, 2, NI])
        pair_avg = sb("pair_avg", [P, P])
        bn_alpha = sb("bn_alpha", [P, 1])
        bn_shift = sb("bn_shift", [P, 1])
        small = sb("small", [P, 64])

        w_hi = sb("w_hi", [P, 9, HID], F16)
        w_lo_pair = sb("w_lo_pair", [P, 3, HID], F16)
        w_lo_one = sb("w_lo_one", [P, 3, HID], F16)
        inv_wscale = sb("inv_wscale", [P, 1])
        dft_q = sb("dft_q", [P, P])
        dft_kr = sb("dft_kr", [P, P])
        dft_ki = sb("dft_ki", [P, P])
        idft_r = sb("idft_r", [P, P])
        idft_i = sb("idft_i", [P, P])
        center = sb("center", [P, P])
        mean_w = sb("mean_w", [P, C])
        proj_w = sb("proj_w", [P, C])
        proj_b = sb("proj_b", [P, C])
        b_proj = sb("b_proj", [P, 1])
        tab0 = sb("tab0", [P, NS + 2, 6])

        with ExitStack() as ph:
            def tsb(name, shape, dt=F32):
                return ph.enter_context(nc.sbuf_tensor(name, shape, dt))

            wh = tsb("wh", [P, HID])
            w_dw = tsb("w_dw", [P, 9, HID])
            w_all = tsb("w_all", [P, 9, HID])
            bh = tsb("bh", [P, HID])
            bdw = tsb("bdw", [P, HID])
            bd = tsb("bd", [P, HID])
            btap = tsb("btap", [P, HID])
            b_hi = tsb("b_hi", [P, HID], F16)
            b_sel = tsb("b_sel", [P, 2])
            lnwb = tsb("lnwb", [P, 2])
            wpT = tsb("wpT", [P, C])
            zrow = tsb("zrow", [C, 18, W])
            wmax = tsb("wmax", [P, 4])
            loaded = ph.enter_context(nc.semaphore("weights_loaded"))
            step = ph.enter_context(nc.semaphore("weight_step"))
            maxed = ph.enter_context(nc.semaphore("weight_max"))
            zeroed = ph.enter_context(nc.semaphore("zeros_made"))
            stored = ph.enter_context(nc.semaphore("zeros_stored"))
            blk = ph.enter_context(nc.Block())
            loads = [(wh[:], "wh"), (w_dw[:], "w_dw"), (bh[:], "b_hidden_rows"), (bdw[:], "w_dw_rows"),
                     (bd[:], "b_dw_rows"), (b_sel[:], "b_sel"), (lnwb[:], "ln_wb"), (wpT[:], "w_projT"),
                     (dft_q[:], "dft_q"), (dft_kr[:], "dft_kr"), (dft_ki[:], "dft_ki"),
                     (idft_r[:], "idft_r"), (idft_i[:], "idft_i"), (center[:], "center"),
                     (mean_w[:], "mean_w"), (b_proj[:], "b_proj"), (tab0[:], "tab0"), (pair_avg[:], "pair_avg")]

            @blk.sync
            def _(sp):
                for dst, name in loads:
                    sp.dma_start(dst, A[name]).then_inc(loaded, 16)
                sp.wait_ge(zeroed, 1)
                sp.dma_start(y1[:, 0:R, :], zrow[:, 0:R, :]).then_inc(stored, 16)
                n = 16
                for r0 in range(R + ROWS, Y1R, 18):
                    k = min(18, Y1R - r0)
                    sp.dma_start(y1[:, r0:r0 + k, :], zrow[:, 0:k, :]).then_inc(stored, 16)
                    n += 16
                sp.wait_ge(stored, n)

            @blk.gpsimd
            def _(pool):
                nc.gpsimd.memset(zrow[:], 0.0).then_inc(zeroed, 1)
                pool.wait_ge(maxed, 1)
                nc.gpsimd.partition_all_reduce(wmax[:, 2:3], wmax[:, 1:2], P, RMAX).then_inc(maxed, 1)

            @blk.vector
            def _(v):
                count = [0]

                def then(ins):
                    count[0] += 1
                    ins.then_inc(step, 1)
                    v.wait_ge(step, count[0])

                v.wait_ge(loaded, 16 * len(loads))
                for t in range(9):
                    then(v.tensor_tensor(w_all[:, t, :], w_dw[:, t, :], wh[:], ALU.mult))
                then(v.tensor_tensor(btap[:], bh[:], bdw[:], ALU.mult))
                then(v.tensor_tensor(btap[:], btap[:], bd[:], ALU.add))
                then(v.scalar_tensor_tensor(w_dw[:], w_all[:], -1.0, w_all[:], ALU.mult, ALU.max))
                then(v.tensor_reduce(wmax[:, 0:1], w_dw[:].rearrange("p t o -> p (t o)"), AX_X, ALU.max))
                then(v.scalar_tensor_tensor(bh[:], btap[:], -1.0, btap[:], ALU.mult, ALU.max))
                then(v.tensor_reduce(wmax[:, 3:4], bh[:], AX_X, ALU.max))
                v.tensor_tensor(wmax[:, 1:2], wmax[:, 0:1], wmax[:, 3:4], ALU.max).then_inc(maxed, 1)
                v.wait_ge(maxed, 2)
                then(v.tensor_scalar(wmax[:, 2:3], wmax[:, 2:3], 1e-30, None, ALU.max))
                then(v.tensor_scalar(inv_wscale[:], wmax[:, 2:3], 1.0 / WSCALE, None, ALU.mult))
                then(v.reciprocal(wmax[:, 0:1], inv_wscale[:]))
                then(v.tensor_scalar(w_all[:], w_all[:], wmax[:, 0:1], None, ALU.mult))
                then(v.tensor_copy(w_hi[:], w_all[:]))
                then(v.tensor_tensor(w_dw[:], w_all[:], w_hi[:], ALU.subtract))
                then(v.memset(w_lo_one[:], 0.0))
                then(v.tensor_copy(w_lo_pair[0:C], w_dw[0:C, 0:3, :]))
                then(v.tensor_copy(w_lo_pair[C:P], w_dw[C:P, 3:6, :]))
                then(v.tensor_copy(w_lo_one[0:C], w_dw[0:C, 6:9, :]))
                then(v.tensor_scalar(btap[:], btap[:], wmax[:, 0:1], None, ALU.mult))
                then(v.tensor_copy(b_hi[:], btap[:]))
                then(v.tensor_tensor(btap[:], btap[:], b_hi[:], ALU.subtract))
                then(v.tensor_scalar(btap[:], btap[:], b_sel[:, 1:2], None, ALU.mult))
                then(v.scalar_tensor_tensor(btap[:], b_hi[:], b_sel[:, 0:1], btap[:], ALU.mult, ALU.add))
                then(v.tensor_copy(w_lo_one[C:P, 1, :], btap[C:P]))
                then(v.tensor_scalar(proj_w[:], wpT[:], lnwb[:, 0:1], None, ALU.mult))
                then(v.tensor_scalar(proj_b[:], wpT[:], lnwb[:, 1:2], None, ALU.mult))

        def group_norm_params(blk_sems, v, layer, mv, tmp):
            step, asked, answered, count = blk_sems

            def then(ins):
                count[0] += 1
                ins.then_inc(step, 1)
                v.wait_ge(step, count[0])

            mean, var = mv[:, :, 0], mv[:, :, 1]
            then(v.tensor_tensor(tmp[:, 0, :], mean, mean, ALU.mult))
            then(v.tensor_tensor(tmp[:, 1, :], tmp[:, 0, :], var, ALU.add))
            then(v.tensor_copy(tmp[:, 0, :], mean))
            v.tensor_copy(tmp[:, 2, :], mean).then_inc(asked, 1)
            v.wait_ge(answered, 1)
            then(v.tensor_copy(tmp[:, 0:2, :], bank[0][:, 0:2 * NI].rearrange("p (a i) -> p a i", i=NI)))
            then(v.tensor_tensor(tmp[:, 2, :], tmp[:, 0, :], tmp[:, 0, :], ALU.mult))
            then(v.tensor_tensor(tmp[:, 2, :], tmp[:, 1, :], tmp[:, 2, :], ALU.subtract))
            v.tensor_scalar(tmp[:, 2, :], tmp[:, 2, :], 0.0, GN_EPS, ALU.max, ALU.add).then_inc(asked, 1)
            v.wait_ge(answered, 2)
            then(v.reciprocal(gn_scale[:, layer, :], tmp[:, 2, :]))
            then(v.scalar_tensor_tensor(gn_bias[:, layer, :], tmp[:, 0, :], -1.0, gn_scale[:, layer, :],
                                        ALU.mult, ALU.mult))
            return then

        def group_norm_root(act, asked, answered, tmp):
            act.wait_ge(asked, 2)
            act.activation(tmp[:, 2, :], tmp[:, 2, :], ACT.Sqrt).then_inc(answered, 1)

        with ExitStack() as ph:
            CH = 2 * R
            NC = ROWS // (2 * CH)
            PER = NC // NI
            NST = CH * W // 512
            xc = ph.enter_context(nc.sbuf_tensor("xc", [P, 2, CH * W], F32))
            st = ph.enter_context(nc.sbuf_tensor("st", [P, NC, NST * 6], F32))
            mv = ph.enter_context(nc.sbuf_tensor("mv", [P, NI, 2], F32))
            tmp = ph.enter_context(nc.sbuf_tensor("tmp", [P, 3, NI], F32))
            loaded = [ph.enter_context(nc.semaphore(f"chunk_loaded{i}")) for i in range(2)]
            used = ph.enter_context(nc.semaphore("chunk_used"))
            step = ph.enter_context(nc.semaphore("gn0_step"))
            asked = ph.enter_context(nc.semaphore("gn0_asked"))
            answered = ph.enter_context(nc.semaphore("gn0_answered"))
            blk = ph.enter_context(nc.Block())

            @blk.sync
            def _(sp):
                def load(i, b, first):
                    rows = [1 + (2 * CH) * (i * 2 + b) + CH * h for h in range(2)]
                    if not first:
                        rows = [sp.snap(row) for row in rows]
                        sp.wait_ge(used, i * 2 + b - 1)
                    for h, row in enumerate(rows):
                        sp.dma_start(xc[C * h:C * h + C, b, :].rearrange("p (r w) -> p r w", w=W),
                                     A["x"][:, bass.ds(row, CH), :]).then_inc(loaded[b], 16)

                load(0, 0, True)
                load(0, 1, True)
                if NC > 2:
                    with sp.Fori(1, NC // 2) as i:
                        load(i, 0, False)
                        load(i, 1, False)

            @blk.vector
            def _(v):
                with v.Fori(0, NC // 2) as i:
                    for b in range(2):
                        v.wait_ge(loaded[b], i * 32 + 32)
                        for n in range(NST):
                            last = v.bn_stats(st[:, bass.ds(i * 2 + b, 1), 6 * n:6 * n + 6].rearrange("p a k -> p (a k)"),
                                              xc[:, b, 512 * n:512 * n + 512])
                        last.then_inc(used, 1)
                v.wait_ge(used, NC)
                for i in range(NI):
                    last = v.bn_aggr(mv[:, i, :], st[:, PER * i:PER * i + PER, :].rearrange("p a k -> p (a k)"))
                last.then_inc(step, 1)
                v.wait_ge(step, 1)
                then = group_norm_params((step, asked, answered, [1]), v, 0, mv, tmp)
                for i in range(NI):
                    then(v.tensor_copy(tab0[:, S * i:S * i + S, 0:1],
                                       gn_scale[:, 0:1, i:i + 1].to_broadcast([P, S, 1])))
                    then(v.tensor_copy(tab0[:, S * i:S * i + S, 1:2],
                                       gn_bias[:, 0:1, i:i + 1].to_broadcast([P, S, 1])))

            @blk.scalar
            def _(act):
                group_norm_root(act, asked, answered, tmp)

            @blk.tensor
            def _(pe):
                pe.wait_ge(asked, 1)
                pe.matmul(bank[0][:, 0:2 * NI], pair_avg[:], tmp[:, 0:2, :].rearrange("p a i -> p (a i)"),
                          start=True, stop=True).then_inc(answered, 1)

        y_stats = sb("y_stats", [P, NS * 2, 6])

        with ExitStack() as ph:
            def tsb(name, shape, dt=F32):
                return ph.enter_context(nc.sbuf_tensor(name, shape, dt))

            def tsem(name):
                return ph.enter_context(nc.semaphore(name))

            SL = R + 3
            SLP = R + 4
            xr = [tsb(f"xr{b}", [P, SL, W]) for b in range(2)]
            xn = tsb("xn", [P, W, SLP])
            hi_all = tsb("hi_all", [P, WP, SLP], F16)
            hl_all = tsb("hl_all", [P, WP, SLP], F16)
            hi_lo = [[tsb(f"hi_lo{b}_{d}", [P, WP, R], F16) for d in range(3)] for b in range(2)]
            hi_pair = [tsb(f"hi_pair{b}", [P, WP, R], F16) for b in range(2)]
            hi_ind = [tsb(f"hi_ind{b}", [P, WP, R], F16) for b in range(2)]
            par = [tsb(f"par{b}", [P, 6]) for b in range(2)]
            ind = tsb("ind", [P, W, R], F16)
            qk = tsb("qk", [P, 4, KQ])
            qf = tsb("qf", [P, 4 * P])
            u1 = tsb("u1", [P, 4, P])
            u2 = tsb("u2", [P, 4, P])
            o_s = tsb("o_s", [P, 512])
            v_s = [tsb(f"v_s{i}", [P, 512]) for i in range(4)]
            vd = [tsb(f"vd{i}", [P, 512]) for i in range(4)]
            sq = [tsb(f"sq{i}", [P, 512]) for i in range(4)]
            rs = tsb("rs", [P, 512])
            rt = tsb("rt", [P, 512])
            eps = tsb("eps", [P, 1])
            yt = tsb("yt", [P, 512])
            ys = [tsb(f"ys{b}", [P, R, 2 * GCOL]) for b in range(2)]

            x_loaded = [tsem(f"x_loaded{b}") for b in range(2)]
            ind_loaded = tsem("ind_loaded")
            buffers_zeroed = tsem("buffers_zeroed")
            par_ready = tsem("par_ready")
            xn_made = tsem("xn_made")
            xn_masked = tsem("xn_masked")
            hi_made = tsem("hi_made")
            low_made = tsem("low_made")
            stacks_ready = tsem("stacks_ready")
            qk_conv = tsem("qk_conv")
            qk_copied = tsem("qk_copied")
            q_freq = tsem("q_freq")
            k_freq = tsem("k_freq")
            qf_copied = tsem("qf_copied")
            u_ready = tsem("u_ready")
            inv_done = tsem("inv_done")
            o_copied = tsem("o_copied")
            v_conv = tsem("v_conv")
            v_copied = tsem("v_copied")
            d_done = tsem("d_done")
            sq_ready = tsem("sq_ready")
            vd_ready = tsem("vd_ready")
            fin_done = tsem("fin_done")
            rs_ready = tsem("rs_ready")
            rt_ready = tsem("rt_ready")
            t_ready = tsem("t_ready")
            fin_read = tsem("fin_read")
            pair_ready = tsem("pair_ready")
            y_stored = [tsem(f"y_stored{b}") for b in range(2)]
            blk = ph.enter_context(nc.Block())

            b_qk, b_v, b_q, b_kr, b_ki, b_o, b_d = (bank[0], bank[1]), bank[2], bank[3], bank[4], bank[5], bank[6], bank[7]
            b_var, b_a, b_b = b_q, b_kr, b_ki

            def run(eng, body, tail=None):
                body(0, True)
                if NB > 1:
                    with eng.Fori(1, NB) as i:
                        body(i, False)
                if tail:
                    tail()

            @blk.sync
            def _(sp):
                def load(row, b):
                    sp.dma_start(xr[b][0:C, 1:SL, :], A["x"][:, bass.ds(row, R + 2), :]).then_inc(x_loaded[b], 16)
                    sp.dma_start(xr[b][C:P, 0:SL - 1, :], A["x"][:, bass.ds(row, R + 2), :]).then_inc(x_loaded[b], 16)

                def store(row, b):
                    for h in range(2):
                        sp.dma_start(y1[:, bass.ds(row, R), 2 * GCOL * h:2 * GCOL * h + 2 * GCOL],
                                     ys[b][C * h:C * h + C]).then_inc(y_stored[b], 16)

                def body(i, first):
                    for b in range(2):
                        if not (first and b == 0):
                            to, of = i * 2 * R + b * R, i * 2 * R + (b + 1) * R
                            if not first:
                                to, of = sp.snap(to), sp.snap(of)
                            sp.wait_ge(pair_ready, i * 4 + 2 * b)
                            store(to, 1 - b)
                            load(of, 1 - b)

                sp.dma_start(ind[:], A["ind"]).then_inc(ind_loaded, 16)
                sp.wait_ge(buffers_zeroed, 1)
                load(0, 0)
                load(R, 1)
                run(sp, body)
                sp.wait_ge(pair_ready, 2 * NS)
                store(NS * R, 1)
                sp.wait_ge(y_stored[0], 16 * NS)
                sp.wait_ge(y_stored[1], 16 * NS)
                sp.wait_ge(x_loaded[0], 32 * (NS // 2) + 32)

            @blk.gpsimd
            def _(pool):
                nc.gpsimd.memset(eps[:], LN_EPS)
                for t in xr + [xn, hi_all, hl_all] + hi_ind:
                    last = nc.gpsimd.memset(t[:], 0.0)
                last.then_inc(buffers_zeroed, 1)

            @blk.tensor
            def _(pe):
                def conv(b, out, o0, o1, tile=None, group=None):
                    n = 0
                    def one(src, dc, w):
                        nonlocal n
                        c0, cols = (16 * tile, 16) if tile is not None else (GCOL * group, GCOL)
                        px = src[:, c0 + dc + 1:c0 + dc + 1 + cols, :].rearrange("p c r -> p (c r)")
                        a, m = (px, w[:, o0:o1]) if tile is not None else (w[:, o0:o1], px)
                        r = pe.matmul(out, a, m, start=n == 0, stop=n == 14)
                        n += 1
                        return r
                    for t, (dr, dc) in enumerate(TAPS):
                        one(hi_lo[b][dr + 1], dc, w_hi[:, t, :])
                    for j, dc in enumerate((-1, 0, 1)):
                        one(hi_pair[b], dc, w_lo_pair[:, j, :])
                        last = one(hi_ind[b], dc, w_lo_one[:, j, :])
                    return last

                def final(i, k):
                    g3 = 8 * i + (k - 3) if isinstance(i, int) else i * 8 + (k - 3)
                    pe.wait_ge(vd_ready, g3 + 2)
                    pe.wait_ge(sq_ready, g3 + 2)
                    pe.wait_ge(u_ready, i * 8 + k)
                    pe.wait_ge(qf_copied, i * 8 + k)
                    for h in range(2):
                        r = (k - 3 + h) % 4
                        lo, hi = C * h, C * h + C
                        pe.matmul(b_var[lo:hi, :], mean_w[:], sq[r][:], start=True, stop=True)
                        pe.matmul(b_a[lo:hi, :], proj_w[:], vd[r][:], start=True, stop=True)
                        last = pe.matmul(b_b[lo:hi, :], proj_b[:], v_s[r][:], start=True, stop=True)
                    last.then_inc(fin_done, 1)

                def inverse(i, k, any_before):
                    pe.wait_ge(u_ready, i * 8 + k)
                    if any_before:
                        pe.wait_ge(o_copied, i * 8 + (k - 1))
                    o4 = b_o[:].rearrange("p (t m) -> p t m", t=4)
                    for t in range(4):
                        pe.matmul(o4[:, t], u1[:, t, :], idft_r[:], start=True, stop=False)
                        last = pe.matmul(o4[:, t], u2[:, t, :], idft_i[:], start=False, stop=True)
                    last.then_inc(inv_done, 1)

                def centered(i, k, any_before):
                    pe.wait_ge(o_copied, i * 8 + k)
                    if any_before:
                        pe.wait_ge(vd_ready, i * 8 + (k - 1))
                        pe.wait_ge(sq_ready, i * 8 + (k - 1))
                    pe.matmul(b_d[:], center[:], o_s[:], start=True, stop=True).then_inc(d_done, 1)

                def body(i, first):
                    for k in range(8):
                        b = k // 4
                        cg = ORDER[k % 4]
                        if k % 4 == 0:
                            pe.wait_ge(stacks_ready, i * 2 + (b + 1))
                            pe.wait_ge(hi_made, i * 2 + (b + 1))
                        for t in range(4):
                            if t % 2 == 0 and not (first and k == 0):
                                pe.wait_ge(qk_copied, i * 16 + (2 * k - 1 + t // 2))
                            last = conv(b, b_qk[t // 2][:, KQ * (t % 2):KQ * (t % 2) + KQ], 0, KQ, tile=4 * cg + t)
                            if t % 2:
                                last.then_inc(qk_conv, 1)
                        if k % 2 and not (first and k < 3):
                            final(i, k)
                        if not (first and k == 0):
                            inverse(i, k, not (first and k == 1))
                            pe.wait_ge(v_copied, i * 8 + k)
                        conv(b, b_v[:], KQ, HID, group=cg).then_inc(v_conv, 1)
                        if not (first and k == 0):
                            centered(i, k, not (first and k == 1))
                        pe.wait_ge(qk_copied, i * 16 + (2 * k + 2))
                        if not (first and k == 0):
                            pe.wait_ge(u_ready, i * 8 + k)
                            pe.wait_ge(qf_copied, i * 8 + k)
                        if not (first and k < 3):
                            pe.wait_ge(fin_read, i * 4 + (k - 1) // 2)
                        pe.matmul(b_q[:], dft_q[:], qk[:, :, 0:P], start=True, stop=True).then_inc(q_freq, 1)
                        pe.matmul(b_kr[:], dft_kr[:], qk[:, :, P:KQ], start=True, stop=True)
                        pe.matmul(b_ki[:], dft_ki[:], qk[:, :, P:KQ], start=True, stop=True).then_inc(k_freq, 1)

                def tail():
                    inverse(NB, 0, True)
                    centered(NB, 0, True)
                    pe.wait_ge(fin_read, NB * 4 - 1)
                    for nm, val in ((vd_ready, NG), (sq_ready, NG), (u_ready, NG), (qf_copied, NG)):
                        pe.wait_ge(nm, val)
                    for h in range(2):
                        lo, hi = C * h, C * h + C
                        pe.matmul(b_var[lo:hi, :], mean_w[:], sq[2 + h][:], start=True, stop=True)
                        pe.matmul(b_a[lo:hi, :], proj_w[:], vd[2 + h][:], start=True, stop=True)
                        last = pe.matmul(b_b[lo:hi, :], proj_b[:], v_s[2 + h][:], start=True, stop=True)
                    last.then_inc(fin_done, 1)

                run(pe, body, tail)

            @blk.scalar
            def _(act):
                def normed(s, b):
                    act.wait_ge(x_loaded[b], (s - b) * 16 + 32)
                    act.wait_ge(par_ready, s + 1)
                    if not isinstance(s, int) or s >= 1:
                        act.wait_ge(stacks_ready, s + 0)
                        act.wait_ge(hi_made, s + 0)
                    act.activation(xn[:, :, 0:SL], xr[b][:].rearrange("p s w -> p w s"), ACT.Identity, bias=par[b][:, 1:2],
                                   scale=par[b][:, 0:1]).then_inc(xn_made, 1)

                def high_parts(s):
                    act.wait_ge(xn_masked, s + 1)
                    act.copy(hi_all[:, 1:W + 1, :], xn[:]).then_inc(hi_made, 1)

                def freq_copy(i, k, any_before):
                    act.wait_ge(q_freq, i * 8 + k)
                    if any_before:
                        act.wait_ge(u_ready, i * 8 + (k - 1))
                    act.copy(qf[:], b_q[:]).then_inc(qf_copied, 1)

                def o_copy(i, k, any_before):
                    act.wait_ge(inv_done, i * 8 + k)
                    if any_before:
                        act.wait_ge(d_done, i * 8 + (k - 1))
                    act.copy(o_s[:], b_o[:]).then_inc(o_copied, 1)

                def std(i, k):
                    act.wait_ge(fin_done, i * 4 + (k - 1) // 2)
                    if not (isinstance(i, int) and i == 0 and k < 5):
                        act.wait_ge(fin_read, i * 4 + (k - 1) // 2 - 1)
                    act.activation(rs[:], b_var[:], ACT.Sqrt, bias=eps[:, 0:1]).then_inc(rs_ready, 1)

                def square(i, k, ring_used):
                    act.wait_ge(vd_ready, i * 8 + k)
                    if ring_used:
                        act.wait_ge(fin_done, i * 4 + (k - 5) // 2 + 1)
                    act.activation(sq[(k - 1) % 4][:], b_d[:], ACT.Square).then_inc(sq_ready, 1)

                def body(i, first):
                    for k in range(8):
                        if k % 4 == 3:
                            normed(i * 2 + (k // 4 + 1), (k // 4 + 1) % 2)
                        if not (first and k == 0):
                            freq_copy(i, k, not (first and k == 1))
                        if k % 4 == 3:
                            high_parts(i * 2 + (k // 4 + 1))
                        for h in range(2):
                            act.wait_ge(qk_conv, i * 16 + (2 * k + h + 1))
                            if not (first and k == 0):
                                act.wait_ge(k_freq, i * 8 + k)
                            act.activation(qk[:, 2 * h:2 * h + 2, :], b_qk[h][:].rearrange("p (t c) -> p t c", t=2),
                                           ACT.Copy, scale=inv_wscale[:, 0:1]).then_inc(qk_copied, 1)
                        if k % 2 and not (first and k < 3):
                            std(i, k)
                        if not (first and k == 0):
                            o_copy(i, k, not (first and k == 1))
                        act.wait_ge(v_conv, i * 8 + (k + 1))
                        if not (first and k < 4):
                            act.wait_ge(fin_done, i * 4 + (k - 4) // 2 + 1)
                            act.wait_ge(vd_ready, i * 8 + (k - 3))
                        act.activation(v_s[k % 4][:], b_v[:], ACT.Copy,
                                       scale=inv_wscale[:, 0:1]).then_inc(v_copied, 1)
                        if not (first and k == 0):
                            square(i, k, not (first and k < 5))

                def tail():
                    freq_copy(NB, 0, True)
                    o_copy(NB, 0, True)
                    square(NB, 0, True)
                    std(NB, 1)

                act.wait_ge(buffers_zeroed, 1)
                normed(0, 0)
                high_parts(0)
                run(act, body, tail)

            @blk.vector
            def _(v):
                def params(s, b):
                    if not isinstance(s, int) or s >= 2:
                        v.wait_ge(xn_masked, s - 1)
                    v.tensor_copy(par[b][:], tab0[:, bass.ds(s, 1), :].rearrange("p a k -> p (a k)")).then_inc(par_ready, 1)

                def masks(s, b):
                    v.wait_ge(xn_made, s + 1)
                    v.wait_ge(par_ready, s + 1)
                    for p0, top, bottom in ((0, 1, SL - 1), (C, 0, SL - 2)):
                        for slot, col in ((top, 2), (bottom, 3)):
                            last = v.tensor_scalar(xn[p0:p0 + C, :, slot], xn[p0:p0 + C, :, slot],
                                                   par[b][p0:p0 + C, col:col + 1], None, ALU.mult)
                    last.then_inc(xn_masked, 1)

                def stacks(s, b):
                    if not isinstance(s, int) or s >= 2:
                        v.wait_ge(qk_conv, s * 8 - 8)
                        v.wait_ge(v_conv, s * 4 - 4)
                    for row, col in ((0, 4), (R - 1, 5)):
                        v.tensor_scalar(hi_ind[b][C:P, 1:W + 1, row], ind[C:P, :, row], par[b][C:P, col:col + 1], None, ALU.mult)
                    if isinstance(s, int) and s < 2:
                        v.tensor_copy(hi_ind[b][C:P, 1:W + 1, 1:R - 1], ind[C:P, :, 1:R - 1])
                    v.wait_ge(hi_made, s + 1)
                    v.tensor_copy(hl_all[0:C, 1:W + 1, 0:SL], hi_all[0:C, 1:W + 1, 0:SL])
                    v.tensor_tensor(hl_all[C:P, 1:W + 1, 1:SL], xn[C:P, :, 0:SL - 1], hi_all[C:P, 1:W + 1, 0:SL - 1],
                                    ALU.subtract).then_inc(low_made, 1)
                    v.tensor_copy(hi_pair[b][:], hi_all[:, :, 1:1 + R])
                    v.tensor_copy(hi_ind[b][0:C], hi_all[0:C, :, 3:3 + R])
                    v.wait_ge(low_made, s + 1)
                    for d in range(3):
                        last = v.tensor_copy(hi_lo[b][d][:], hl_all[:, :, 1 + d:1 + d + R])
                    last.then_inc(stacks_ready, 1)

                def products(i, k, any_before):
                    v.wait_ge(qf_copied, i * 8 + k)
                    v.wait_ge(k_freq, i * 8 + k)
                    if any_before:
                        v.wait_ge(inv_done, i * 8 + (k - 1))
                    flat = lambda t: t[:].rearrange("p t c -> p (t c)")
                    v.tensor_tensor(flat(u1), qf[:], b_kr[:], ALU.mult)
                    v.tensor_tensor(flat(u2), qf[:], b_ki[:], ALU.mult).then_inc(u_ready, 1)

                def times_v(i, k, ring_used):
                    v.wait_ge(d_done, i * 8 + k)
                    v.wait_ge(v_copied, i * 8 + k)
                    if ring_used:
                        v.wait_ge(fin_done, i * 4 + (k - 5) // 2 + 1)
                    v.tensor_tensor(vd[(k - 1) % 4][:], v_s[(k - 1) % 4][:], b_d[:], ALU.mult).then_inc(vd_ready, 1)

                def finish(i, k):
                    m = ((k - 3) % 4) // 2
                    sb_ = ((k - 3) // 4) % 2
                    done = i * 4 + (k - 1) // 2
                    v.wait_ge(fin_done, done)
                    v.wait_ge(rs_ready, done)
                    v.reciprocal(rt[:], rs[:]).then_inc(rt_ready, 1)
                    v.wait_ge(rt_ready, done)
                    v.tensor_tensor(rt[:], rt[:], b_a[:], ALU.mult).then_inc(t_ready, 1)
                    v.wait_ge(t_ready, i * 8 + 2 * ((k - 1) // 2) - 1)
                    v.scalar_tensor_tensor(yt[:], b_b[:], b_proj[:, 0:1], rt[:], ALU.add, ALU.add).then_inc(fin_read, 1)
                    v.wait_ge(fin_read, done)
                    strip_less_2 = i * 2 + ((k - 3) // 4 - 2)
                    if m == 0 and not (isinstance(i, int) and strip_less_2 < 0):
                        v.wait_ge(y_stored[sb_], (strip_less_2 - sb_) * 16 + 32)
                    y3 = yt[:].rearrange("p (c r) -> p r c", r=R)
                    for h in range(2):
                        c0 = GCOL * (m + 2 * h)
                        slot = 2 - h
                        last = v.tensor_tensor(ys[sb_][C * h:C * h + C, :, GCOL * m:GCOL * m + GCOL], y3[C * h:C * h + C],
                                               xr[sb_][C * h:C * h + C, slot:slot + R, c0:c0 + GCOL], ALU.add)
                    last.then_inc(t_ready, 1)
                    v.wait_ge(t_ready, i * 8 + 2 * ((k - 1) // 2))
                    v.bn_stats(y_stats[:, bass.ds(i * 4 + ((k - 1) // 2 - 1), 1), :].rearrange("p a k -> p (a k)"),
                               ys[sb_][:, :, GCOL * m:GCOL * m + GCOL]).then_inc(pair_ready, 1)

                def body(i, first):
                    for k in range(8):
                        s, b = i * 2 + (k // 4 + 1), (k // 4 + 1) % 2
                        if k % 4 == 2:
                            params(s, b)
                        if not (first and k == 0):
                            products(i, k, not (first and k == 1))
                        if k % 4 == 3:
                            masks(s, b)
                        if k % 2 and not (first and k < 3):
                            finish(i, k)
                        if k % 4 == 3:
                            stacks(s, b)
                        if not (first and k == 0):
                            times_v(i, k, not (first and k < 5))

                def tail():
                    products(NB, 0, True)
                    times_v(NB, 0, True)
                    finish(NB, 1)

                v.wait_ge(buffers_zeroed, 1)
                v.wait_ge(ind_loaded, 16)
                params(0, 0)
                masks(0, 0)
                stacks(0, 0)
                run(v, body, tail)

        tab1 = sb("tab1", [P, N1 + 2, 10])
        wr = sb("wr", [P, P])
        with ExitStack() as ph:
            def tsb(name, shape, dt=F32):
                return ph.enter_context(nc.sbuf_tensor(name, shape, dt))

            def tsem(name):
                return ph.enter_context(nc.semaphore(name))

            mv = tsb("mv1", [P, NI, 2])
            tmp = tsb("tmp1", [P, 3, NI])
            wrs = tsb("wrs", [P, NI, P])
            yc = [tsb(f"yc{b}", [P, 4, W]) for b in range(4)]
            rst = tsb("rst", [P, NS, 12])
            rmv = tsb("rmv", [P, NI, 2])
            half_avg = tsb("half_avg", [P, P])
            const = tsb("const", [P, NI])
            vecs = tsb("vecs", [P, 3])
            acc = tsb("acc", [P, 8])
            w_loaded = tsem("w_loaded")
            y_loaded = [tsem(f"y_loaded{b}") for b in range(4)]
            r_made = tsem("r_made")
            r_read = tsem("r_read")
            step = tsem("gn1_step")
            asked = tsem("gn1_asked")
            answered = tsem("gn1_answered")
            scaled = tsem("wr_scaled")
            blk = ph.enter_context(nc.Block())
            NQ = NS // 4

            @blk.sync
            def _(sp):
                for dst, name in ((wr[:], "w_reduceT"), (half_avg[:], "half_avg"), (vecs[:], "bn_vecs"),
                                  (tab1[:], "tab1")):
                    sp.dma_start(dst, A[name]).then_inc(w_loaded, 16)

                def load(i, b, first):
                    rows = [(i * 4 + b) * R + (R + 4 * h) for h in range(2)]
                    if not first:
                        rows = [sp.snap(row) for row in rows]
                        sp.wait_ge(r_made, i * 8 + 2 * (b - 3))
                    for h, row in enumerate(rows):
                        sp.dma_start(yc[b][C * h:C * h + C], y1[:, bass.ds(row, 4), :]).then_inc(y_loaded[b], 16)

                for b in range(4):
                    load(0, b, True)
                if NQ > 1:
                    with sp.Fori(1, NQ) as i:
                        for b in range(4):
                            load(i, b, False)

            @blk.scalar
            def _(act):
                group_norm_root(act, asked, answered, tmp)
                act.wait_ge(asked, 4)
                act.activation(acc[:, 7:8], acc[:, 7:8], ACT.Sqrt).then_inc(answered, 1)

            @blk.tensor
            def _(pe):
                pe.wait_ge(asked, 1)
                pe.matmul(bank[0][:, 0:2 * NI], pair_avg[:], tmp[:, 0:2, :].rearrange("p a i -> p (a i)"),
                          start=True, stop=True).then_inc(answered, 1)
                pe.wait_ge(scaled, 1)
                pe.matmul(bank[1][:, 0:NI], wr[:], gn_bias[:, 1, :], start=True, stop=True).then_inc(answered, 1)

                def products(img, j, b, first):
                    i = img * (NQ // NI) + j
                    pe.wait_ge(y_loaded[b], i * 32 + 32)
                    for h in range(2):
                        bk = 2 + 2 * (b % 2) + h
                        if not (first and b < 2):
                            pe.wait_ge(r_read, i * 8 + (2 * b + h - 3))
                        last = pe.matmul(bank[bk][:], wrs[:, img, :], yc[b][:, 2 * h:2 * h + 2, :].rearrange("p r w -> p (r w)"),
                                         start=True, stop=True)
                        last.then_inc(r_made, 1)

                for img in range(NI):
                    if img == 0:
                        for b in range(4):
                            products(0, 0, b, True)
                    j0 = 1 if img == 0 else 0
                    if NQ // NI > j0:
                        with pe.Fori(j0, NQ // NI) as j:
                            for b in range(4):
                                products(img, j, b, False)
                pe.wait_ge(asked, 3)
                pe.matmul(bank[1][:, 0:2], half_avg[:], acc[:, 0:2], start=True, stop=True).then_inc(answered, 1)

            @blk.vector
            def _(v):
                PERI = 2 * NS // NI
                for i in range(NI):
                    last = v.bn_aggr(mv[:, i, :], y_stats[:, PERI * i:PERI * i + PERI, :].rearrange("p a k -> p (a k)"))
                last.then_inc(step, 1)
                v.wait_ge(step, 1)
                count = [1]
                then = group_norm_params((step, asked, answered, count), v, 1, mv, tmp)
                v.wait_ge(w_loaded, 64)
                for i in range(NI):
                    last = v.tensor_scalar(wrs[:, i, :], wr[:], gn_scale[:, 1, i:i + 1], None, ALU.mult)
                last.then_inc(scaled, 1)
                with v.Fori(0, NQ) as i:
                    for b in range(4):
                        for h in range(2):
                            v.wait_ge(r_made, i * 8 + (2 * b + h + 1))
                            v.bn_stats(rst[:, bass.ds(i * 4 + b, 1), 6 * h:6 * h + 6].rearrange("p a k -> p (a k)"),
                                       bank[2 + 2 * (b % 2) + h][:]).then_inc(r_read, 1)
                v.wait_ge(r_read, 2 * NS)
                for i in range(NI):
                    last = v.bn_aggr(rmv[:, i, :], rst[:, S * i:S * i + S, :].rearrange("p a k -> p (a k)"))
                then(last)
                v.wait_ge(answered, 3)
                then(v.tensor_copy(const[:], bank[1][:, 0:NI]))
                then(v.tensor_tensor(rmv[:, :, 0], rmv[:, :, 0], const[:], ALU.add))
                then(v.tensor_scalar(rmv[:, :, 0], rmv[:, :, 0], vecs[:, 0:1], None, ALU.add))
                then(v.tensor_tensor(const[:], rmv[:, :, 0], rmv[:, :, 0], ALU.mult))
                then(v.tensor_tensor(rmv[:, :, 1], rmv[:, :, 1], const[:], ALU.add))
                then(v.tensor_reduce(acc[:, 0:2], rmv[:].rearrange("p i k -> p k i"), AX_X, ALU.add))
                v.tensor_copy(acc[:, 2:4], acc[:, 0:2]).then_inc(asked, 1)
                v.wait_ge(answered, 4)
                then(v.tensor_scalar(acc[:, 4:6], bank[1][:, 0:2], 1.0 / NI, None, ALU.mult))
                then(v.tensor_tensor(acc[:, 6:7], acc[:, 4:5], acc[:, 4:5], ALU.mult))
                then(v.tensor_tensor(acc[:, 7:8], acc[:, 5:6], acc[:, 6:7], ALU.subtract))
                v.tensor_scalar(acc[:, 7:8], acc[:, 7:8], 0.0, BN_EPS, ALU.max, ALU.add).then_inc(asked, 1)
                v.wait_ge(answered, 5)
                then(v.reciprocal(acc[:, 7:8], acc[:, 7:8]))
                then(v.tensor_tensor(bn_alpha[:], acc[:, 7:8], vecs[:, 1:2], ALU.mult))
                then(v.tensor_tensor(acc[:, 6:7], vecs[:, 0:1], acc[:, 4:5], ALU.subtract))
                then(v.scalar_tensor_tensor(bn_shift[:], acc[:, 6:7], bn_alpha[:, 0:1], vecs[:, 2:3], ALU.mult, ALU.add))
                for kind, src in ((0, gn_scale), (4, gn_bias)):
                    for i in range(NI):
                        lo = S * i + 1
                        then(v.tensor_copy(tab1[:, lo:lo + S, kind:kind + 4],
                                           src[:, 1:2, i:i + 1].to_broadcast([P, S, 4])))
                    nxt = tab1[C:P, 0:S * (NI - 1) + 1:S, :] if NI > 1 else tab1[C:P, 0:1, :]
                    for col in (1, 3):
                        then(v.tensor_copy(nxt[:, :, kind + col], src[C:P, 1, :]))
                    then(v.memset(tab1[C:P, S:NS + 1:S, kind + 2:kind + 3], 0.0))
                    then(v.memset(tab1[0:C, S:NS + 1:S, kind + 3:kind + 4], 0.0))

        with ExitStack() as ph:
            def tsb(name, shape, dt=F32):
                return ph.enter_context(nc.sbuf_tensor(name, shape, dt))

            def tsem(name):
                return ph.enter_context(nc.semaphore(name))

            xa = [tsb(f"xa{b}", [P, 4, W]) for b in range(2)]
            xb = [tsb(f"xb{b}", [P, 5, W]) for b in range(4)]
            x_mid = [tsb(f"x_mid{b}", [P, 4, WP]) for b in range(2)]
            x_up = [tsb(f"x_up{b}", [P, 4, WP]) for b in range(2)]
            x_down = [tsb(f"x_down{b}", [P, 4, WP]) for b in range(2)]
            par = [tsb(f"par1_{b}", [P, 10]) for b in range(2)]
            rn = tsb("rn", [P, 1024])
            prod = [tsb(f"prod{k}", [P, 1024]) for k in range(9)]
            inv = tsb("inv", [P, 1024])
            ab = tsb("ab", [P, 1024])
            z = [tsb(f"z{b}", [P, 5, WP]) for b in range(2)]
            pre = tsb("pre", [P, 1024])
            ab2 = tsb("ab2", [P, 1024])
            res = [tsb(f"res{b}", [P, 1024]) for b in range(2)]
            span_w = tsb("span_w", [P, 9, P])
            span_b = tsb("span_b", [P, 9])
            conv_w = tsb("conv_w", [P, 6, P])
            conv_b = tsb("conv_b", [P, 1])

            w_loaded = tsem("w1_loaded")
            xa_loaded = [tsem(f"xa_loaded{b}") for b in range(2)]
            xb_loaded = [tsem(f"xb_loaded{b}") for b in range(4)]
            zeroed = tsem("zeroed1")
            par_ready = tsem("par1_ready")
            normed = tsem("normed")
            r_done = tsem("r_done")
            rn_ready = tsem("rn_ready")
            kern_done = tsem("kern_done")
            prod_ready = tsem("prod_ready")
            half_sum = tsem("half_sum")
            pool_step = tsem("pool_step")
            sum_step = tsem("sum_step")
            exp_step = tsem("exp_step")
            log_ready = tsem("log_ready")
            z_written = tsem("z_written")
            z_ready = tsem("z_ready")
            conv_done = tsem("conv_done")
            pre_ready = tsem("pre_ready")
            exp2_step = tsem("exp2_step")
            log2_ready = tsem("log2_ready")
            soft_ready = tsem("soft_ready")
            out_ready = tsem("out_ready")
            out_stored = [tsem(f"out_stored{b}") for b in range(2)]
            blk = ph.enter_context(nc.Block())

            b_kern = ((bank[0], bank[1]), (bank[2], bank[3]))
            b_r = (bank[4], bank[5])
            b_c = (bank[6], bank[7])
            NB1 = N1 // 4

            def run1(eng, body):
                body(0, True)
                if NB1 > 1:
                    with eng.Fori(1, NB1) as i:
                        body(i, False)

            @blk.sync
            def _(sp):
                def load(r, r1, b):
                    sp.dma_start(xa[b % 2][0:C], y1_by_parity[:, 1, bass.ds(r, 4), :]).then_inc(xa_loaded[b % 2], 16)
                    sp.dma_start(xa[b % 2][C:P], y1_by_parity[:, 0, bass.ds(r1, 4), :]).then_inc(xa_loaded[b % 2], 16)
                    sp.dma_start(xb[b][0:C], y1_by_parity[:, 0, bass.ds(r, 5), :]).then_inc(xb_loaded[b], 16)
                    sp.dma_start(xb[b][C:P], y1_by_parity[:, 1, bass.ds(r, 5), :]).then_inc(xb_loaded[b], 16)

                def store(r, b):
                    for h in range(2):
                        sp.dma_start(out_by_parity[:, h, bass.ds(r, 4), :],
                                     res[b % 2][C * h:C * h + C].rearrange("p (r w) -> p r w", w=W)).then_inc(out_stored[b % 2], 16)

                def body(i, first):
                    for k in range(4):
                        to, of, of1 = (i * 16 + n for n in (4 * (k - 2), 4 * (k + 2), 4 * (k + 2) + 1))
                        strips_normed, strips_out = i * 4 + (k + 1), i * 4 + (k - 1)
                        if not first:
                            to, of, of1 = sp.snap(to), sp.snap(of), sp.snap(of1)
                            strips_normed, strips_out = sp.snap(strips_normed), sp.snap(strips_out)
                        if not (first and k < 2):
                            sp.wait_ge(out_ready, strips_out)
                            store(to, (k - 2) % 4)
                        sp.wait_ge(normed, strips_normed)
                        load(of, of1, (k + 2) % 4)

                for dst, name in ((span_w[:], "span_w"), (span_b[:], "span_b"), (conv_w[:], "conv_w"), (conv_b[:], "conv_b")):
                    sp.dma_start(dst, A[name]).then_inc(w_loaded, 16)
                load(0, 1, 0)
                load(4, 5, 1)
                run1(sp, body)
                for b in range(2):
                    sp.wait_ge(out_stored[b], 32 * ((N1 - 2) // 2))
                sp.wait_ge(xa_loaded[1], 32 * (N1 // 2 + 1))
                sp.wait_ge(xb_loaded[0], 32 * (N1 // 4 + 1))
                sp.wait_ge(xb_loaded[1], 32 * (N1 // 4 + 1))

            @blk.gpsimd
            def _(pool):
                for t in x_mid + x_up + x_down + z:
                    last = nc.gpsimd.memset(t[:], 0.0)
                last.then_inc(zeroed, 1)

                def body(i, first):
                    for k in range(4):
                        for n in range(3):
                            pool.wait_ge(prod_ready, i * 36 + (9 * k + n + 2))
                            if n:
                                pool.wait_ge(pool_step, i * 8 + (2 * k + n))
                            ins = nc.gpsimd.tensor_tensor(prod[0][:], prod[0][:], prod[n + 1][:], ALU.add)
                            ins.then_inc(pool_step if n < 2 else half_sum, 1)

                run1(pool, body)

            @blk.tensor
            def _(pe):
                def r_product(u, b, before):
                    pe.wait_ge(normed, u + 1)
                    if before:
                        pe.wait_ge(rn_ready, u + 0)
                    for h in range(2):
                        last = pe.matmul(b_r[h][:], wr[:], x_mid[b][:, 2 * h:2 * h + 2, 1:W + 1], start=True, stop=True)
                    last.then_inc(r_done, 1)

                def body(i, first):
                    for k in range(4):
                        pe.wait_ge(rn_ready, i * 4 + (k + 1))
                        for n in range(9):
                            if not (first and 9 * k + n < 2):
                                pe.wait_ge(prod_ready, i * 36 + (9 * k + n - 1))
                            for h in range(2):
                                last = pe.matmul(b_kern[(9 * k + n) % 2][h][:], span_w[:, n, :],
                                                 rn[:, 512 * h:512 * h + 512], start=True, stop=True)
                            last.then_inc(kern_done, 1)
                        r_product(i * 4 + (k + 1), (k + 1) % 2, True)
                        if not (first and k == 0):
                            pe.wait_ge(z_ready, i * 4 + k)
                            if not (first and k == 1):
                                pe.wait_ge(pre_ready, i * 4 + (k - 1))
                            zb = z[(k - 1) % 2]
                            for h in range(2):
                                for n in range(6):
                                    j, dc = n // 3, n % 3
                                    last = pe.matmul(b_c[h][:], conv_w[:, n, :], zb[:, 2 * h + j:2 * h + j + 2, dc:dc + W],
                                                     start=n == 0, stop=n == 5)
                            last.then_inc(conv_done, 1)

                r_product(0, 0, False)
                run1(pe, body)

            @blk.scalar
            def _(act):
                def norm(u, b, before):
                    act.wait_ge(xa_loaded[b % 2], (u - b % 2) * 16 + 32)
                    act.wait_ge(xb_loaded[b], (u - b) * 8 + 32)
                    act.wait_ge(par_ready, u + 1)
                    if before:
                        act.wait_ge(prod_ready, (u - 1) * 9)
                        act.wait_ge(r_done, u - 1)
                    p = par[b % 2]
                    for src, s0, dst, col in ((xa[b % 2], 0, x_mid, 1), (xb[b], 0, x_up, 2), (xb[b], 1, x_down, 3)):
                        act.activation(dst[b % 2][:, 0:3, 1:W + 1], src[:, s0:s0 + 3, :], ACT.Identity,
                                       bias=p[:, 4:5], scale=p[:, 0:1])
                        last = act.activation(dst[b % 2][:, 3, 1:W + 1], src[:, s0 + 3, :], ACT.Identity,
                                              bias=p[:, 4 + col:5 + col], scale=p[:, col:col + 1])
                    last.then_inc(normed, 1)

                def bn_relu(u, before):
                    act.wait_ge(r_done, u + 1)
                    if before:
                        act.wait_ge(kern_done, u * 9)
                    for h in range(2):
                        last = act.activation(rn[:, 512 * h:512 * h + 512], b_r[h][:], ACT.Relu, bias=bn_shift[:, 0:1],
                                              scale=bn_alpha[:, 0:1])
                    last.then_inc(rn_ready, 1)

                def soft(buf, steps, sem_log, i, strips):
                    act.wait_ge(steps, i * 8 + (2 * strips - 1))
                    act.activation(buf[:], buf[:], ACT.Exp, scale=-1.0).then_inc(steps, 1)
                    act.wait_ge(steps, i * 8 + 2 * strips)
                    act.activation(buf[:], buf[:], ACT.Ln, bias=1.0).then_inc(sem_log, 1)

                def body(i, first):
                    for k in range(4):
                        if not (first and k == 0):
                            act.wait_ge(sum_step, i * 20 + 5 * k)
                            if not (first and k == 1):
                                act.wait_ge(z_written, i * 8 + (2 * k - 3))
                            act.activation(ab[:], inv[:], ACT.Abs).then_inc(exp_step, 1)
                            soft(ab, exp_step, log_ready, i, k)
                        norm(i * 4 + (k + 1), (k + 1) % 4, not (first and k == 0))
                        if not (first and k < 2):
                            act.wait_ge(conv_done, i * 4 + (k - 1))
                            if not (first and k == 2):
                                act.wait_ge(soft_ready, i * 4 + (k - 2))
                            for h in range(2):
                                last = act.activation(ab2[:, 512 * h:512 * h + 512], b_c[h][:], ACT.Abs, bias=conv_b[:, 0:1])
                            last.then_inc(exp2_step, 1)
                            for h in range(2):
                                last = act.activation(pre[:, 512 * h:512 * h + 512], b_c[h][:], ACT.Relu, bias=conv_b[:, 0:1])
                            last.then_inc(pre_ready, 1)
                            soft(ab2, exp2_step, log2_ready, i, k - 1)
                        bn_relu(i * 4 + (k + 1), True)

                act.wait_ge(zeroed, 1)
                act.wait_ge(w_loaded, 64)
                norm(0, 0, False)
                bn_relu(0, False)
                run1(act, body)

            @blk.vector
            def _(v):
                def params(u, b):
                    if not isinstance(u, int) or u >= 2:
                        v.wait_ge(normed, u - 1)
                        v.wait_ge(z_ready, u - 1)
                    v.tensor_copy(par[b % 2][:], tab1[:, bass.ds(u, 1), :].rearrange("p a k -> p (a k)")).then_inc(par_ready, 1)

                def z_finish(i, k, third):
                    b = (k - 1) % 2
                    v.wait_ge(log_ready, i * 4 + k)
                    if third:
                        v.wait_ge(conv_done, i * 4 + (k - 2))
                    v.scalar_tensor_tensor(z[b][:, 1:5, 1:W + 1], inv[:].rearrange("p (r w) -> p r w", w=W), 0.0,
                                           ab[:].rearrange("p (r w) -> p r w", w=W), ALU.max, ALU.add).then_inc(z_written, 1)
                    v.wait_ge(z_written, i * 8 + 2 * k - 1)
                    v.tensor_scalar(z[1 - b][:, 0, 1:W + 1], z[b][:, 4, 1:W + 1], par_m[b][:, 0:1], None, ALU.mult)\
                        .then_inc(z_written, 1)
                    v.wait_ge(z_written, i * 8 + 2 * k)
                    v.tensor_scalar(z[b][:, 4, 1:W + 1], z[b][:, 4, 1:W + 1], par_m[b][:, 1:2], None, ALU.mult).then_inc(z_ready, 1)

                def out_finish(i, k, stored_before):
                    rb = res[(k - 2) % 2]
                    v.wait_ge(log2_ready, i * 4 + (k - 1))
                    if stored_before:
                        v.wait_ge(out_stored[(k - 2) % 2], (i * 4 + (k - 2) - (k - 2) % 2 - 2) * 16 + 32)
                    v.wait_ge(pre_ready, i * 4 + (k - 1))
                    v.tensor_tensor(rb[:], pre[:], ab2[:], ALU.add).then_inc(soft_ready, 1)
                    v.wait_ge(soft_ready, i * 4 + (k - 1))
                    v.tensor_tensor(rb[:], rb[:], xb[(k - 2) % 4][:, 0:4, :].rearrange("p r w -> p (r w)"), ALU.add)\
                        .then_inc(out_ready, 1)

                par_m = [par[0][:, 8:10], par[1][:, 8:10]]

                def body(i, first):
                    for k in range(4):
                        b = k % 2
                        for n, (dr, dc) in enumerate(TAPS):
                            src = {-1: x_up, 0: x_mid, 1: x_down}[dr][b]
                            v.wait_ge(kern_done, i * 36 + (9 * k + n + 1))
                            if n == 0:
                                v.wait_ge(normed, i * 4 + (k + 1))
                            if n == 0 and not (first and k == 0):
                                v.wait_ge(sum_step, i * 20 + 5 * k)
                            if n < 4 and not (first and k == 0):
                                v.wait_ge(half_sum, i * 4 + k)
                            for h in range(2):
                                last = v.scalar_tensor_tensor(
                                    prod[n][:, 512 * h:512 * h + 512].rearrange("p (r w) -> p r w", w=W),
                                    b_kern[(9 * k + n) % 2][h][:].rearrange("p (r w) -> p r w", w=W), span_b[:, n:n + 1],
                                    src[:, 2 * h:2 * h + 2, 1 + dc:1 + dc + W], ALU.add, ALU.mult)
                            last.then_inc(prod_ready, 1)
                            if n == 2 and not (first and k == 0):
                                z_finish(i, k, not (first and k < 3))
                            if n == 3:
                                params(i * 4 + (k + 1), (k + 1) % 4)
                            if n == 8 and not (first and k < 2):
                                out_finish(i, k, not (first and k < 4))
                        for n in range(5):
                            a = prod[4] if n == 0 else inv
                            c = prod[n + 5] if n < 4 else prod[0]
                            if n == 0:
                                v.wait_ge(prod_ready, i * 36 + (9 * k + 9))
                                if not (first and k == 0):
                                    v.wait_ge(z_written, i * 8 + 2 * k)
                            else:
                                v.wait_ge(sum_step, i * 20 + (5 * k + n))
                            if n == 4:
                                v.wait_ge(half_sum, i * 4 + (k + 1))
                            v.tensor_tensor(inv[:], a[:], c[:], ALU.add).then_inc(sum_step, 1)

                v.wait_ge(zeroed, 1)
                v.wait_ge(w_loaded, 64)
                params(0, 0)
                run1(v, body)



def shape_constants(NI, S):
    NS, N1 = NI * S, strips_of_layer1(NI * S)
    out = {}
    m = np.arange(P)
    row, patch, col = m % 8, m // 64, m // 8 % 8
    real = [(0, 0), (0, 4), (4, 0), (4, 4)]
    pairs = [(u, w) for u in range(8) for w in range(8) if (u, w) not in real and (u, w) < ((-u) % 8, (-w) % 8)]
    assert len(pairs) == 30
    kinds = [(u, w, "r") for u, w in real] + [(u, w, "R") for u, w in pairs] + [(u, w, "I") for u, w in pairs]
    fq, fr, fi, gr, gi = (np.zeros((P, P)) for _ in range(5))
    for pt in range(2):
        on = patch == pt
        for j, (u, w, kind) in enumerate(kinds):
            f = 64 * pt + j
            th = 2 * np.pi * (u * row + w * col) / 8
            cos, sin = np.cos(th) * on, np.sin(th) * on
            fq[:, f] = -sin if kind == "I" else cos
            fr[:, f] = cos
            fi[:, f] = 0 if kind == "r" else -sin
            gr[f] = cos / 64 if kind == "r" else (2 * cos / 64 if kind == "R" else -2 * sin / 64)
            gi[f] = 0 if kind == "r" else (-2 * sin / 64 if kind == "R" else -2 * cos / 64)
    out["dft_q"], out["dft_kr"], out["dft_ki"], out["idft_r"], out["idft_i"] = fq, fr, fi, gr, gi
    out["center"] = np.eye(P) - 1.0 / P
    out["mean_w"] = np.full((P, C), 1.0 / P)
    ch = m % C
    out["pair_avg"] = (ch[:, None] // 2 == ch[None, :] // 2) / 4.0
    out["half_avg"] = (ch[:, None] == ch[None, :]) / 2.0
    tab0 = np.ones((P, NS + 2, 6))
    tap = (m - C) % 9
    for s in range(NS + 2):
        top, bottom = s % S == 0, s % S == S - 1
        tab0[:, s, 2], tab0[:, s, 3] = not top, not bottom
        tab0[:, s, 4] = np.where(tap < 3, not top, 1)
        tab0[:, s, 5] = np.where(tap >= 6, not bottom, 1)
    out["tab0"] = tab0
    tab1 = np.zeros((P, N1 + 2, 10))
    tab1[:, :, 8:10] = 1
    for u in range(0, N1 + 2):
        if u % S == 0:
            tab1[0:C, u, 8] = 0
            tab1[C:P, u, 9] = 0
    out["tab1"] = tab1
    b_sel = np.zeros((P, 2))
    b_sel[C:C + 9, 0] = 1
    b_sel[C + 9:C + 18, 1] = 1
    out["b_sel"] = b_sel
    out = {n: a.astype(np.float32) for n, a in out.items()}
    ind = np.zeros((P, W, R), np.float16)
    for part in range(2):
        for t, (dr, dc) in enumerate(TAPS):
            ind[C + 9 * part + t] = 1
            if dc == -1:
                ind[C + 9 * part + t, 0] = 0
            if dc == 1:
                ind[C + 9 * part + t, W - 1] = 0
    out["ind"] = ind
    return out


def two(a):
    return np.concatenate([a, a], axis=0)


def block_diagonal(a):
    out = np.zeros((P, P), a.dtype)
    out[0:C, 0:C] = a
    out[C:P, C:P] = a
    return out


def kernel(**inputs):
    import concourse.bacc as _bacc
    from concourse.bass_utils import run_bass_kernel_spmd as _run

    g = {n: np.asarray(a) for n, a in inputs.items()}
    x = g["x"]
    NI, _, H, _ = x.shape
    S = H // R
    NS, N1 = NI * S, strips_of_layer1(NI * S)
    arrays = shape_constants(NI, S)
    xt = np.zeros((C, 1 + NI * H + XTRA, W), x.dtype)
    xt[:, 1:1 + NI * H] = x.transpose(1, 0, 2, 3).reshape(C, NI * H, W)
    arrays["x"] = xt
    arrays["wh"] = two(g["L0_conv_w_hidden"].T)
    taps = g["L0_conv_w_dw"].reshape(HID, 9).T
    arrays["w_dw"] = np.broadcast_to(taps[None], (P, 9, HID))
    rows = np.zeros((P, HID), x.dtype)
    b_rows, d_rows = rows.copy(), rows.copy()
    for part in range(2):
        p0 = C + 9 * part
        rows[p0:p0 + 9] = taps
        b_rows[p0:p0 + 9] = g["L0_conv_b_hidden"]
        d_rows[p0 + 4] = g["L0_conv_b_dw"]
    arrays["w_dw_rows"], arrays["b_hidden_rows"], arrays["b_dw_rows"] = rows, b_rows, d_rows
    arrays["ln_wb"] = np.stack([g["L0_conv_ln_w"], g["L0_conv_ln_b"]], axis=1)
    arrays["w_projT"] = g["L0_conv_w_proj"].T
    arrays["b_proj"] = two(g["L0_conv_b_proj"])[:, None]
    arrays["w_reduceT"] = block_diagonal(g["L1_conv_w_reduce"].T)
    arrays["bn_vecs"] = two(np.stack([g["L1_conv_b_reduce"], g["L1_conv_bn_gamma"], g["L1_conv_bn_beta"]], axis=1))
    arrays["span_w"] = np.stack([block_diagonal(np.broadcast_to(g["L1_conv_w_span"][n][:, None], (C, C)))
                                 for n in range(9)], axis=1)
    arrays["span_b"] = np.broadcast_to(g["L1_conv_b_span"][None], (P, 9))
    w2 = g["L1_conv_w_conv2"]
    cw = np.zeros((P, 6, P), x.dtype)
    for dc in range(3):
        cw[0:C, dc, 0:C] = w2[:, :, 0, dc].T
        cw[C:P, dc, 0:C] = w2[:, :, 1, dc].T
        cw[C:P, dc, C:P] = w2[:, :, 0, dc].T
        cw[0:C, 3 + dc, 0:C] = w2[:, :, 2, dc].T
        cw[0:C, 3 + dc, C:P] = w2[:, :, 1, dc].T
        cw[C:P, 3 + dc, C:P] = w2[:, :, 2, dc].T
    arrays["conv_w"] = cw
    arrays["conv_b"] = two(g["L1_conv_b_conv2"])[:, None]
    arrays = {n: np.ascontiguousarray(a) for n, a in arrays.items()}

    nc = _bacc.Bacc("TRN2", target_bir_lowering=False, num_devices=1)
    A, feeds = {}, {}
    for name, a in arrays.items():
        feeds[f"in_{name}_dram"] = a
        A[name] = nc.dram_tensor(f"in_{name}_dram", a.shape, mybir.dt.from_np(a.dtype), kind="ExternalInput").ap()
    A["out"] = nc.dram_tensor("out_0_dram", (C, R * N1, W), F32, kind="ExternalOutput").ap()
    build_program(nc, A, NI, S)
    r = _run(nc, [feeds], core_ids=[0])
    out = np.asarray(r.results[0]["out_0_dram"])[:, R:R + NI * H]
    return np.ascontiguousarray(out.reshape(C, NI, H, W).transpose(1, 0, 2, 3))
```

```python
from contextlib import ExitStack

import numpy as np

import concourse.bass as bass
from concourse import mybir

ALU = mybir.AluOpType
ACT = mybir.ActivationFunctionType
AX_X = mybir.AxisListType.X
F32 = mybir.dt.float32
F16 = mybir.dt.float16
BF16 = mybir.dt.bfloat16
EXP_AND_LN = 6
RMAX = bass.bass_isa.ReduceOp.max

P = 128
C = 64
W = 256
WP = W + 2
PATCH = 8
R = 8
HID = 6 * C
KQ = 256
XTRA = 9
GN_EPS = 1e-5
LN_EPS = 1e-5
BN_EPS = 1e-5
WSCALE = 256.0
GCOL = 64
ORDER = [0, 2, 1, 3]
TAPS = [(dr, dc) for dr in (-1, 0, 1) for dc in (-1, 0, 1)]


def strips_of_layer1(strips):
    return (strips + 1 + 3) // 4 * 4


def build_program(nc, A, NI, S):
    NS = NI * S
    ROWS = NS * R
    NG = NS * 4
    NB = NS // 2
    N1 = strips_of_layer1(NS)
    Y1R = R * (N1 + 1) + 10
    y1 = nc.dram_tensor("y1_scratch", (C, Y1R, W), F32, kind="Internal").ap()
    y1_by_parity = y1.rearrange("c (r two) w -> c two r w", two=2)
    out_by_parity = A["out"].rearrange("c (r two) w -> c two r w", two=2)

    with ExitStack() as ctx:
        def sb(name, shape, dt=F32):
            return ctx.enter_context(nc.sbuf_tensor(name, shape, dt))

        def sem(name):
            return ctx.enter_context(nc.semaphore(name))

        bank_pair = [ctx.enter_context(nc.psum_tensor(f"banks{i}", [P, 2, 512], F32)) for i in range(4)]
        bank = [bank_pair[i // 2][:, i % 2, :] for i in range(8)]

        gn_scale = sb("gn_scale", [P, 2, NI])
        gn_bias = sb("gn_bias", [P, 2, NI])
        pair_avg = sb("pair_avg", [P, P])
        bn_alpha = sb("bn_alpha", [P, 1])
        bn_shift = sb("bn_shift", [P, 1])
        small = sb("small", [P, 64])

        w_hi = sb("w_hi", [P, 9, HID], F16)
        w_lo_pair = sb("w_lo_pair", [P, 3, HID], F16)
        w_lo_one = sb("w_lo_one", [P, 2, HID], F16)
        inv_wscale = sb("inv_wscale", [P, 1])
        dft = sb("dft", [P, P])
        idft_1 = sb("idft_1", [P, P])
        idft_2 = sb("idft_2", [P, P])
        mean_w = sb("mean_w", [P, P])
        ln_wb = sb("ln_wb", [P, 2])
        proj_w = sb("proj_w", [P, C])
        b_proj = sb("b_proj", [P, 1])
        tab0 = sb("tab0", [P, NS + 2, 6])

        with ExitStack() as ph:
            def tsb(name, shape, dt=F32):
                return ph.enter_context(nc.sbuf_tensor(name, shape, dt))

            wh = tsb("wh", [P, HID])
            w_dw = tsb("w_dw", [P, 9, HID])
            w_all = tsb("w_all", [P, 9, HID])
            bh = tsb("bh", [P, HID])
            bdw = tsb("bdw", [P, HID])
            bd = tsb("bd", [P, HID])
            btap = tsb("btap", [P, HID])
            b_hi = tsb("b_hi", [P, HID], F16)
            b_sel = tsb("b_sel", [P, 2])
            zrow = tsb("zrow", [C, 18, W])
            wmax = tsb("wmax", [P, 4])
            loaded = ph.enter_context(nc.semaphore("weights_loaded"))
            step = ph.enter_context(nc.semaphore("weight_step"))
            maxed = ph.enter_context(nc.semaphore("weight_max"))
            zeroed = ph.enter_context(nc.semaphore("zeros_made"))
            stored = ph.enter_context(nc.semaphore("zeros_stored"))
            blk = ph.enter_context(nc.Block())
            loads = [(wh[:], "wh"), (w_dw[:], "w_dw"), (bh[:], "b_hidden_rows"), (bdw[:], "w_dw_rows"),
                     (bd[:], "b_dw_rows"), (b_sel[:], "b_sel"), (ln_wb[:], "ln_wb"), (proj_w[:], "w_projT"),
                     (dft[:], "dft"), (idft_1[:], "idft_1"), (idft_2[:], "idft_2"),
                     (mean_w[:], "mean_w"), (b_proj[:], "b_proj"), (tab0[:], "tab0"), (pair_avg[:], "pair_avg")]

            @blk.sync
            def _(sp):
                for dst, name in loads:
                    sp.dma_start(dst, A[name]).then_inc(loaded, 16)
                sp.wait_ge(zeroed, 1)
                sp.dma_start(y1[:, 0:R, :], zrow[:, 0:R, :]).then_inc(stored, 16)
                n = 16
                for r0 in range(R + ROWS, Y1R, 18):
                    k = min(18, Y1R - r0)
                    sp.dma_start(y1[:, r0:r0 + k, :], zrow[:, 0:k, :]).then_inc(stored, 16)
                    n += 16
                sp.wait_ge(stored, n)

            @blk.gpsimd
            def _(pool):
                nc.gpsimd.memset(zrow[:], 0.0).then_inc(zeroed, 1)
                pool.wait_ge(maxed, 1)
                nc.gpsimd.partition_all_reduce(wmax[:, 2:3], wmax[:, 1:2], P, RMAX).then_inc(maxed, 1)

            @blk.vector
            def _(v):
                count = [0]

                def then(ins):
                    count[0] += 1
                    ins.then_inc(step, 1)
                    v.wait_ge(step, count[0])

                v.wait_ge(loaded, 16 * len(loads))
                for t in range(9):
                    then(v.tensor_tensor(w_all[:, t, :], w_dw[:, t, :], wh[:], ALU.mult))
                then(v.tensor_tensor(btap[:], bh[:], bdw[:], ALU.mult))
                then(v.tensor_tensor(btap[:], btap[:], bd[:], ALU.add))
                then(v.scalar_tensor_tensor(w_dw[:], w_all[:], -1.0, w_all[:], ALU.mult, ALU.max))
                then(v.tensor_reduce(wmax[:, 0:1], w_dw[:].rearrange("p t o -> p (t o)"), AX_X, ALU.max))
                then(v.scalar_tensor_tensor(bh[:], btap[:], -1.0, btap[:], ALU.mult, ALU.max))
                then(v.tensor_reduce(wmax[:, 3:4], bh[:], AX_X, ALU.max))
                v.tensor_tensor(wmax[:, 1:2], wmax[:, 0:1], wmax[:, 3:4], ALU.max).then_inc(maxed, 1)
                v.wait_ge(maxed, 2)
                then(v.tensor_scalar(wmax[:, 2:3], wmax[:, 2:3], 1e-30, None, ALU.max))
                then(v.tensor_scalar(inv_wscale[:], wmax[:, 2:3], 1.0 / WSCALE, None, ALU.mult))
                then(v.reciprocal(wmax[:, 0:1], inv_wscale[:]))
                then(v.tensor_scalar(w_all[:], w_all[:], wmax[:, 0:1], None, ALU.mult))
                then(v.tensor_copy(w_hi[:], w_all[:]))
                then(v.tensor_tensor(w_dw[:], w_all[:], w_hi[:], ALU.subtract))
                then(v.memset(w_lo_one[:], 0.0))
                then(v.tensor_copy(w_lo_pair[0:C], w_dw[0:C, 0:3, :]))
                then(v.tensor_copy(w_lo_pair[C:P], w_dw[C:P, 3:6, :]))
                then(v.tensor_copy(w_lo_one[0:C], w_dw[0:C, 6:8, :]))
                then(v.tensor_copy(w_lo_one[C:P, 0, :], w_dw[C:P, 8, :]))
                then(v.tensor_scalar(btap[:], btap[:], wmax[:, 0:1], None, ALU.mult))
                then(v.tensor_copy(b_hi[:], btap[:]))
                then(v.tensor_tensor(btap[:], btap[:], b_hi[:], ALU.subtract))
                then(v.tensor_scalar(btap[:], btap[:], b_sel[:, 1:2], None, ALU.mult))
                then(v.scalar_tensor_tensor(btap[:], b_hi[:], b_sel[:, 0:1], btap[:], ALU.mult, ALU.add))
                then(v.tensor_copy(w_lo_one[C:P, 1, :], btap[C:P]))

        def group_norm_params(blk_sems, v, layer, mv, tmp):
            step, asked, answered, count = blk_sems

            def then(ins):
                count[0] += 1
                ins.then_inc(step, 1)
                v.wait_ge(step, count[0])

            mean, var = mv[:, :, 0], mv[:, :, 1]
            then(v.tensor_tensor(tmp[:, 0, :], mean, mean, ALU.mult))
            then(v.tensor_tensor(tmp[:, 1, :], tmp[:, 0, :], var, ALU.add))
            then(v.tensor_copy(tmp[:, 0, :], mean))
            v.tensor_copy(tmp[:, 2, :], mean).then_inc(asked, 1)
            v.wait_ge(answered, 1)
            then(v.tensor_copy(tmp[:, 0:2, :], bank[0][:, 0:2 * NI].rearrange("p (a i) -> p a i", i=NI)))
            then(v.tensor_tensor(tmp[:, 2, :], tmp[:, 0, :], tmp[:, 0, :], ALU.mult))
            then(v.tensor_tensor(tmp[:, 2, :], tmp[:, 1, :], tmp[:, 2, :], ALU.subtract))
            v.tensor_scalar(tmp[:, 2, :], tmp[:, 2, :], 0.0, GN_EPS, ALU.max, ALU.add).then_inc(asked, 1)
            v.wait_ge(answered, 2)
            then(v.reciprocal(gn_scale[:, layer, :], tmp[:, 2, :]))
            then(v.scalar_tensor_tensor(gn_bias[:, layer, :], tmp[:, 0, :], -1.0, gn_scale[:, layer, :],
                                        ALU.mult, ALU.mult))
            return then

        def group_norm_root(act, asked, answered, tmp):
            act.wait_ge(asked, 2)
            act.activation(tmp[:, 2, :], tmp[:, 2, :], ACT.Sqrt).then_inc(answered, 1)

        with ExitStack() as ph:
            CH = 2 * R
            NC = ROWS // (2 * CH)
            PER = NC // NI
            NST = CH * W // 512
            xc = ph.enter_context(nc.sbuf_tensor("xc", [P, 2, CH * W], F32))
            st = ph.enter_context(nc.sbuf_tensor("st", [P, NC, NST * 6], F32))
            mv = ph.enter_context(nc.sbuf_tensor("mv", [P, NI, 2], F32))
            tmp = ph.enter_context(nc.sbuf_tensor("tmp", [P, 3, NI], F32))
            loaded = [ph.enter_context(nc.semaphore(f"chunk_loaded{i}")) for i in range(2)]
            used = ph.enter_context(nc.semaphore("chunk_used"))
            step = ph.enter_context(nc.semaphore("gn0_step"))
            asked = ph.enter_context(nc.semaphore("gn0_asked"))
            answered = ph.enter_context(nc.semaphore("gn0_answered"))
            blk = ph.enter_context(nc.Block())

            @blk.sync
            def _(sp):
                def load(i, b, first):
                    rows = [1 + (2 * CH) * (i * 2 + b) + CH * h for h in range(2)]
                    if not first:
                        rows = [sp.snap(row) for row in rows]
                        sp.wait_ge(used, i * 2 + b - 1)
                    for h, row in enumerate(rows):
                        sp.dma_start(xc[C * h:C * h + C, b, :].rearrange("p (r w) -> p r w", w=W),
                                     A["x"][:, bass.ds(row, CH), :]).then_inc(loaded[b], 16)

                load(0, 0, True)
                load(0, 1, True)
                if NC > 2:
                    with sp.Fori(1, NC // 2) as i:
                        load(i, 0, False)
                        load(i, 1, False)

            @blk.vector
            def _(v):
                with v.Fori(0, NC // 2) as i:
                    for b in range(2):
                        v.wait_ge(loaded[b], i * 32 + 32)
                        for n in range(NST):
                            last = v.bn_stats(st[:, bass.ds(i * 2 + b, 1), 6 * n:6 * n + 6].rearrange("p a k -> p (a k)"),
                                              xc[:, b, 512 * n:512 * n + 512])
                        last.then_inc(used, 1)
                v.wait_ge(used, NC)
                for i in range(NI):
                    last = v.bn_aggr(mv[:, i, :], st[:, PER * i:PER * i + PER, :].rearrange("p a k -> p (a k)"))
                last.then_inc(step, 1)
                v.wait_ge(step, 1)
                then = group_norm_params((step, asked, answered, [1]), v, 0, mv, tmp)
                for i in range(NI):
                    then(v.tensor_copy(tab0[:, S * i:S * i + S, 0:1],
                                       gn_scale[:, 0:1, i:i + 1].to_broadcast([P, S, 1])))
                    then(v.tensor_copy(tab0[:, S * i:S * i + S, 1:2],
                                       gn_bias[:, 0:1, i:i + 1].to_broadcast([P, S, 1])))

            @blk.scalar
            def _(act):
                group_norm_root(act, asked, answered, tmp)

            @blk.tensor
            def _(pe):
                pe.wait_ge(asked, 1)
                pe.matmul(bank[0][:, 0:2 * NI], pair_avg[:], tmp[:, 0:2, :].rearrange("p a i -> p (a i)"),
                          start=True, stop=True).then_inc(answered, 1)

        y_stats = sb("y_stats", [P, NS * 2, 6])

        with ExitStack() as ph:
            def tsb(name, shape, dt=F32):
                return ph.enter_context(nc.sbuf_tensor(name, shape, dt))

            def tsem(name):
                return ph.enter_context(nc.semaphore(name))

            SL = R + 3
            SLP = R + 4
            xr = [tsb(f"xr{b}", [P, SL, W]) for b in range(2)]
            xn = tsb("xn", [P, W, SLP])
            hi_all = tsb("hi_all", [P, WP, SLP], F16)
            hl_all = tsb("hl_all", [P, WP, SLP], F16)
            hi_lo = [[tsb(f"hi_lo{b}_{d}", [P, WP, R], F16) for d in range(3)] for b in range(2)]
            hi_pair = [tsb(f"hi_pair{b}", [P, WP, R], F16) for b in range(2)]
            hi_ind = [tsb(f"hi_ind{b}", [P, WP, R], F16) for b in range(2)]
            hi_side = [tsb(f"hi_side{b}", [P, WP, R], F16) for b in range(2)]
            par = [tsb(f"par{b}", [P, 6]) for b in range(2)]
            ind = tsb("ind", [P, W, R], F16)
            qk = tsb("qk", [P, 4, KQ])
            qf = tsb("qf", [P, 512])
            qs = tsb("qs", [P, 512])
            u = tsb("u", [P, 2, 512])
            u_mean = tsb("u_mean", [P, 8])
            v_s = [tsb(f"v_s{i}", [P, 512]) for i in range(4)]
            t_n = tsb("t_n", [P, 512])
            w_v = [tsb(f"w_v{i}", [P, 512]) for i in range(4)]
            sq = tsb("sq", [P, 512])
            rs = tsb("rs", [P, 512])
            eps = tsb("eps", [P, 1])
            ys = [tsb(f"ys{b}", [P, R, 2 * GCOL]) for b in range(2)]

            x_loaded = [tsem(f"x_loaded{b}") for b in range(2)]
            ind_loaded = tsem("ind_loaded")
            buffers_zeroed = tsem("buffers_zeroed")
            par_ready = tsem("par_ready")
            xn_made = tsem("xn_made")
            xn_masked = tsem("xn_masked")
            hi_made = tsem("hi_made")
            low_made = tsem("low_made")
            stacks_ready = tsem("stacks_ready")
            qk_conv = tsem("qk_conv")
            qk_copied = tsem("qk_copied")
            q_freq = tsem("q_freq")
            k_freq = tsem("k_freq")
            qf_copied = tsem("qf_copied")
            qs_copied = tsem("qs_copied")
            u_made = tsem("u_made")
            u_summed = tsem("u_summed")
            means_ready = tsem("means_ready")
            u_ready = tsem("u_ready")
            inv_done = tsem("inv_done")
            v_conv = tsem("v_conv")
            v_copied = tsem("v_copied")
            sq_ready = tsem("sq_ready")
            var_done = tsem("var_done")
            log_ready = tsem("log0_ready")
            rs_ready = tsem("rs_ready")
            t_ready = tsem("t_ready")
            affine_ready = tsem("affine_ready")
            w_ready = tsem("w_ready")
            fin_done = tsem("fin_done")
            fin_read = tsem("fin_read")
            pair_ready = tsem("pair_ready")
            y_stored = [tsem(f"y_stored{b}") for b in range(2)]
            blk = ph.enter_context(nc.Block())

            b_qk, b_v, b_q, b_k, b_o, b_var, b_y = (bank[0], bank[1]), bank[2], bank[3], bank[4], bank[5], bank[6], bank[7]

            def run(eng, body, tail=None):
                body(0, True)
                if NB > 1:
                    with eng.Fori(1, NB) as i:
                        body(i, False)
                if tail:
                    tail()

            @blk.sync
            def _(sp):
                def load(row, b):
                    sp.dma_start(xr[b][0:C, 1:SL, :], A["x"][:, bass.ds(row, R + 2), :]).then_inc(x_loaded[b], 16)
                    sp.dma_start(xr[b][C:P, 0:SL - 1, :], A["x"][:, bass.ds(row, R + 2), :]).then_inc(x_loaded[b], 16)

                def store(row, b):
                    for h in range(2):
                        sp.dma_start(y1[:, bass.ds(row, R), 2 * GCOL * h:2 * GCOL * h + 2 * GCOL],
                                     ys[b][C * h:C * h + C]).then_inc(y_stored[b], 16)

                def body(i, first):
                    for b in range(2):
                        if not (first and b == 0):
                            to, of = i * 2 * R + b * R, i * 2 * R + (b + 1) * R
                            if not first:
                                to, of = sp.snap(to), sp.snap(of)
                            sp.wait_ge(pair_ready, i * 4 + 2 * b)
                            store(to, 1 - b)
                            load(of, 1 - b)

                sp.dma_start(ind[:], A["ind"]).then_inc(ind_loaded, 16)
                sp.wait_ge(buffers_zeroed, 1)
                load(0, 0)
                load(R, 1)
                run(sp, body)
                sp.wait_ge(pair_ready, 2 * NS)
                store(NS * R, 1)
                sp.wait_ge(y_stored[0], 16 * NS)
                sp.wait_ge(y_stored[1], 16 * NS)
                sp.wait_ge(x_loaded[0], 32 * (NS // 2) + 32)

            @blk.gpsimd
            def _(pool):
                nc.gpsimd.memset(eps[:], LN_EPS)
                for t in xr + [xn, hi_all, hl_all] + hi_ind + hi_side:
                    last = nc.gpsimd.memset(t[:], 0.0)
                last.then_inc(buffers_zeroed, 1)

                def less_mean(i, k):
                    pool.wait_ge(means_ready, i * 8 + k)
                    u8 = u[:].rearrange("p f (t c) -> p (f t) c", t=4)
                    nc.gpsimd.tensor_tensor(u8, u8, u_mean[:].unsqueeze(2).to_broadcast([P, 8, P]), ALU.subtract)\
                        .then_inc(u_ready, 1)

                def times_v(i, k, ring_used):
                    pool.wait_ge(affine_ready, i * 8 + (k - 1))
                    if ring_used:
                        pool.wait_ge(fin_done, i * 4 + (k - 6) // 2 + 1)
                    nc.gpsimd.tensor_tensor(w_v[(k - 2) % 4][:], t_n[:], v_s[(k - 2) % 4][:], ALU.mult).then_inc(w_ready, 1)

                def body(i, first):
                    for k in range(8):
                        if not (first and k == 0):
                            less_mean(i, k)
                        if not (first and k < 2):
                            times_v(i, k, not (first and k < 6))

                def tail():
                    less_mean(NB, 0)
                    times_v(NB, 0, True)
                    times_v(NB, 1, True)

                run(pool, body, tail)

            @blk.tensor
            def _(pe):
                def conv(b, out, o0, o1, tile=None, group=None):
                    n = 0
                    def one(src, dc, w):
                        nonlocal n
                        c0, cols = (16 * tile, 16) if tile is not None else (GCOL * group, GCOL)
                        px = src[:, c0 + dc + 1:c0 + dc + 1 + cols, :].rearrange("p c r -> p (c r)")
                        a, m = (px, w[:, o0:o1]) if tile is not None else (w[:, o0:o1], px)
                        r = pe.matmul(out, a, m, start=n == 0, stop=n == 13)
                        n += 1
                        return r
                    for t, (dr, dc) in enumerate(TAPS):
                        one(hi_lo[b][dr + 1], dc, w_hi[:, t, :])
                    for j, dc in enumerate((-1, 0, 1)):
                        one(hi_pair[b], dc, w_lo_pair[:, j, :])
                    one(hi_side[b], -1, w_lo_one[:, 0, :])
                    return one(hi_ind[b], 0, w_lo_one[:, 1, :])

                def project(i, k, any_before):
                    pe.wait_ge(w_ready, i * 8 + (k - 1))
                    if any_before:
                        pe.wait_ge(fin_read, i * 4 + (k - 3) // 2)
                    for h in range(2):
                        last = pe.matmul(b_y[C * h:C * h + C, :], proj_w[:], w_v[(k - 3 + h) % 4][:], start=True, stop=True)
                    last.then_inc(fin_done, 1)

                def inverse(i, k, any_before):
                    pe.wait_ge(u_ready, i * 8 + k)
                    if any_before:
                        pe.wait_ge(t_ready, i * 8 + (k - 1))
                    for t in range(4):
                        px = slice(P * t, P * t + P)
                        pe.matmul(b_o[:, px], u[:, 0, px], idft_1[:], start=True, stop=False)
                        last = pe.matmul(b_o[:, px], u[:, 1, px], idft_2[:], start=False, stop=True)
                    last.then_inc(inv_done, 1)

                def variance(i, k, any_before):
                    pe.wait_ge(sq_ready, i * 8 + k)
                    if any_before:
                        pe.wait_ge(log_ready, i * 8 + (k - 1))
                    pe.matmul(b_var[:], mean_w[:], sq[:], start=True, stop=True).then_inc(var_done, 1)

                def body(i, first):
                    for k in range(8):
                        b = k // 4
                        cg = ORDER[k % 4]
                        if k % 4 == 0:
                            pe.wait_ge(stacks_ready, i * 2 + (b + 1))
                            pe.wait_ge(hi_made, i * 2 + (b + 1))
                        for t in range(4):
                            if t % 2 == 0 and not (first and k == 0):
                                pe.wait_ge(qk_copied, i * 16 + (2 * k - 1 + t // 2))
                            last = conv(b, b_qk[t // 2][:, KQ * (t % 2):KQ * (t % 2) + KQ], 0, KQ, tile=4 * cg + t)
                            if t % 2:
                                last.then_inc(qk_conv, 1)
                        if not (first and k == 0):
                            pe.wait_ge(v_copied, i * 8 + k)
                        conv(b, b_v[:], KQ, HID, group=cg).then_inc(v_conv, 1)
                        if k % 2 and not (first and k < 3):
                            project(i, k, not (first and k < 5))
                        if not (first and k == 0):
                            inverse(i, k, not (first and k == 1))
                        pe.wait_ge(qk_copied, i * 16 + (2 * k + 2))
                        if not (first and k == 0):
                            pe.wait_ge(u_made, i * 8 + k)
                            pe.wait_ge(qs_copied, i * 8 + k)
                        pe.matmul(b_q[:], dft[:], qk[:, :, 0:P], start=True, stop=True).then_inc(q_freq, 1)
                        pe.matmul(b_k[:], dft[:], qk[:, :, P:KQ], start=True, stop=True).then_inc(k_freq, 1)
                        if not (first and k == 0):
                            variance(i, k, not (first and k == 1))

                def tail():
                    inverse(NB, 0, True)
                    variance(NB, 0, True)
                    project(NB, 1, True)

                run(pe, body, tail)

            @blk.scalar
            def _(act):
                def normed(s, b):
                    act.wait_ge(x_loaded[b], (s - b) * 16 + 32)
                    act.wait_ge(par_ready, s + 1)
                    if not isinstance(s, int) or s >= 1:
                        act.wait_ge(stacks_ready, s + 0)
                        act.wait_ge(hi_made, s + 0)
                    act.activation(xn[:, :, 0:SL], xr[b][:].rearrange("p s w -> p w s"), ACT.Identity, bias=par[b][:, 1:2],
                                   scale=par[b][:, 0:1]).then_inc(xn_made, 1)

                def high_parts(s):
                    act.wait_ge(xn_masked, s + 1)
                    act.copy(hi_all[:, 1:W + 1, :], xn[:]).then_inc(hi_made, 1)

                def freq_copy(i, k, any_before):
                    act.wait_ge(q_freq, i * 8 + k)
                    if any_before:
                        act.wait_ge(u_made, i * 8 + (k - 1))
                    act.copy(qf[:], b_q[:]).then_inc(qf_copied, 1)
                    act.copy(qs[C:P, :], b_q[0:C, :])
                    act.copy(qs[0:C, :], b_q[C:P, :]).then_inc(qs_copied, 1)

                def root(i, k, any_before):
                    act.wait_ge(var_done, i * 8 + (k - 1))
                    if any_before:
                        act.wait_ge(t_ready, i * 8 + (k - 2))
                    act.activation(rs[:], b_var[:], ACT.Ln, bias=eps[:, 0:1]).then_inc(log_ready, 1)
                    act.wait_ge(log_ready, i * 8 + (k - 1))
                    act.activation(rs[:], rs[:], ACT.Exp, scale=-0.5).then_inc(rs_ready, 1)

                def affine(i, k):
                    act.wait_ge(t_ready, i * 8 + (k - 1))
                    act.activation(t_n[:], t_n[:], ACT.Identity, bias=ln_wb[:, 1:2], scale=ln_wb[:, 0:1]).then_inc(affine_ready, 1)

                def square(i, k, any_before):
                    act.wait_ge(inv_done, i * 8 + k)
                    if any_before:
                        act.wait_ge(var_done, i * 8 + (k - 1))
                    act.activation(sq[:], b_o[:], ACT.Square).then_inc(sq_ready, 1)

                def body(i, first):
                    for k in range(8):
                        if not (first and k == 0):
                            freq_copy(i, k, not (first and k == 1))
                        if not (first and k < 2):
                            root(i, k, not (first and k == 2))
                        if k % 4 == 3:
                            high_parts(i * 2 + (k // 4 + 1))
                        for h in range(2):
                            act.wait_ge(qk_conv, i * 16 + (2 * k + h + 1))
                            if not (first and k == 0):
                                act.wait_ge(k_freq, i * 8 + k)
                            act.activation(qk[:, 2 * h:2 * h + 2, :], b_qk[h][:].rearrange("p (t c) -> p t c", t=2),
                                           ACT.Copy, scale=inv_wscale[:, 0:1]).then_inc(qk_copied, 1)
                            if h == 0 and not (first and k < 2):
                                affine(i, k)
                        if k % 4 == 2:
                            normed(i * 2 + (k // 4 + 1), (k // 4 + 1) % 2)
                        act.wait_ge(v_conv, i * 8 + (k + 1))
                        if not (first and k < 4):
                            act.wait_ge(w_ready, i * 8 + (k - 3))
                        act.activation(v_s[k % 4][:], b_v[:], ACT.Copy,
                                       scale=inv_wscale[:, 0:1]).then_inc(v_copied, 1)
                        if not (first and k == 0):
                            square(i, k, not (first and k == 1))

                def tail():
                    freq_copy(NB, 0, True)
                    root(NB, 0, True)
                    affine(NB, 0)
                    square(NB, 0, True)
                    root(NB, 1, True)
                    affine(NB, 1)

                act.add_instruction(mybir.InstLoadActFuncSet(name=nc.get_next_instruction_name(),
                                                             act_func_set_id=EXP_AND_LN, engine=mybir.EngineType.Activation, ins=[], outs=[]))
                act.wait_ge(buffers_zeroed, 1)
                normed(0, 0)
                high_parts(0)
                run(act, body, tail)

            @blk.vector
            def _(v):
                def params(s, b):
                    if not isinstance(s, int) or s >= 2:
                        v.wait_ge(xn_masked, s - 1)
                    v.tensor_copy(par[b][:], tab0[:, bass.ds(s, 1), :].rearrange("p a k -> p (a k)")).then_inc(par_ready, 1)

                def masks(s, b):
                    v.wait_ge(xn_made, s + 1)
                    v.wait_ge(par_ready, s + 1)
                    for p0, top, bottom in ((0, 1, SL - 1), (C, 0, SL - 2)):
                        for slot, col in ((top, 2), (bottom, 3)):
                            last = v.tensor_scalar(xn[p0:p0 + C, :, slot], xn[p0:p0 + C, :, slot],
                                                   par[b][p0:p0 + C, col:col + 1], None, ALU.mult)
                    last.then_inc(xn_masked, 1)

                def stacks(s, b):
                    if not isinstance(s, int) or s >= 2:
                        v.wait_ge(qk_conv, s * 8 - 8)
                        v.wait_ge(v_conv, s * 4 - 4)
                    for row, col in ((0, 4), (R - 1, 5)):
                        v.tensor_scalar(hi_ind[b][C:P, 1:W + 1, row], ind[C:P, :, row], par[b][C:P, col:col + 1], None, ALU.mult)
                    if isinstance(s, int) and s < 2:
                        v.tensor_copy(hi_ind[b][C:P, 1:W + 1, 1:R - 1], ind[C:P, :, 1:R - 1])
                    v.wait_ge(hi_made, s + 1)
                    v.tensor_copy(hl_all[0:C, 1:W + 1, 0:SL], hi_all[0:C, 1:W + 1, 0:SL])
                    v.tensor_tensor(hl_all[C:P, 1:W + 1, 1:SL], xn[C:P, :, 0:SL - 1], hi_all[C:P, 1:W + 1, 0:SL - 1],
                                    ALU.subtract).then_inc(low_made, 1)
                    v.tensor_copy(hi_pair[b][:], hi_all[:, :, 1:1 + R])
                    v.tensor_copy(hi_ind[b][0:C], hi_all[0:C, :, 3:3 + R])
                    v.tensor_copy(hi_side[b][0:C], hi_all[0:C, :, 3:3 + R])
                    v.tensor_copy(hi_side[b][C:P, 0:W, :], hi_all[C:P, 2:W + 2, 2:2 + R])
                    v.wait_ge(low_made, s + 1)
                    for d in range(3):
                        last = v.tensor_copy(hi_lo[b][d][:], hl_all[:, :, 1 + d:1 + d + R])
                    last.then_inc(stacks_ready, 1)

                def products(i, k, any_before):
                    v.wait_ge(qf_copied, i * 8 + k)
                    v.wait_ge(k_freq, i * 8 + k)
                    if any_before:
                        v.wait_ge(inv_done, i * 8 + (k - 1))
                    v.tensor_tensor(u[:, 0, :], qf[:], b_k[:], ALU.mult)
                    v.wait_ge(qs_copied, i * 8 + k)
                    v.tensor_tensor(u[:, 1, :], qs[:], b_k[:], ALU.mult).then_inc(u_made, 1)
                    v.wait_ge(u_made, i * 8 + k)
                    v.tensor_reduce(u_mean[:], u[:].rearrange("p f (t c) -> p (f t) c", t=4), AX_X, ALU.add).then_inc(u_summed, 1)
                    v.wait_ge(u_summed, i * 8 + k)
                    v.tensor_scalar(u_mean[:], u_mean[:], 1.0 / P, None, ALU.mult).then_inc(means_ready, 1)

                def over_std(i, k, any_before):
                    v.wait_ge(rs_ready, i * 8 + (k - 1))
                    if any_before:
                        v.wait_ge(w_ready, i * 8 + (k - 2))
                    v.tensor_tensor(t_n[:], b_o[:], rs[:], ALU.mult).then_inc(t_ready, 1)

                def finish(i, k):
                    m = ((k - 3) % 4) // 2
                    sb_ = ((k - 3) // 4) % 2
                    done = i * 4 + (k - 1) // 2
                    v.wait_ge(fin_done, done)
                    strip_less_2 = i * 2 + ((k - 3) // 4 - 2)
                    if m == 0 and not (isinstance(i, int) and strip_less_2 < 0):
                        v.wait_ge(y_stored[sb_], (strip_less_2 - sb_) * 16 + 32)
                    y3 = b_y[:].rearrange("p (c r) -> p r c", r=R)
                    for h in range(2):
                        c0 = GCOL * (m + 2 * h)
                        slot = 2 - h
                        rows = slice(C * h, C * h + C)
                        last = v.scalar_tensor_tensor(ys[sb_][rows, :, GCOL * m:GCOL * m + GCOL], y3[rows], b_proj[rows, 0:1],
                                                      xr[sb_][rows, slot:slot + R, c0:c0 + GCOL], ALU.add, ALU.add)
                    last.then_inc(fin_read, 1)
                    v.wait_ge(fin_read, done)
                    v.bn_stats(y_stats[:, bass.ds(i * 4 + ((k - 1) // 2 - 1), 1), :].rearrange("p a k -> p (a k)"),
                               ys[sb_][:, :, GCOL * m:GCOL * m + GCOL]).then_inc(pair_ready, 1)

                def body(i, first):
                    for k in range(8):
                        s, b = i * 2 + (k // 4 + 1), (k // 4 + 1) % 2
                        if k % 4 == 1:
                            params(s, b)
                        if not (first and k == 0):
                            products(i, k, not (first and k == 1))
                        if not (first and k < 2):
                            over_std(i, k, not (first and k == 2))
                        if k % 4 == 3:
                            stacks(s, b)
                        if k % 2 and not (first and k < 3):
                            finish(i, k)
                        if k % 4 == 2:
                            masks(s, b)

                def tail():
                    products(NB, 0, True)
                    over_std(NB, 0, True)
                    over_std(NB, 1, True)
                    finish(NB, 1)

                v.wait_ge(buffers_zeroed, 1)
                v.wait_ge(ind_loaded, 16)
                params(0, 0)
                masks(0, 0)
                stacks(0, 0)
                run(v, body, tail)

        tab1 = sb("tab1", [P, N1 + 2, 10])
        wr = sb("wr", [P, P])
        with ExitStack() as ph:
            def tsb(name, shape, dt=F32):
                return ph.enter_context(nc.sbuf_tensor(name, shape, dt))

            def tsem(name):
                return ph.enter_context(nc.semaphore(name))

            mv = tsb("mv1", [P, NI, 2])
            tmp = tsb("tmp1", [P, 3, NI])
            wrs = tsb("wrs", [P, NI, P])
            yc = [tsb(f"yc{b}", [P, 4, W]) for b in range(4)]
            rst = tsb("rst", [P, NS, 12])
            rmv = tsb("rmv", [P, NI, 2])
            half_avg = tsb("half_avg", [P, P])
            const = tsb("const", [P, NI])
            vecs = tsb("vecs", [P, 3])
            acc = tsb("acc", [P, 8])
            w_loaded = tsem("w_loaded")
            y_loaded = [tsem(f"y_loaded{b}") for b in range(4)]
            r_made = tsem("r_made")
            r_read = tsem("r_read")
            step = tsem("gn1_step")
            asked = tsem("gn1_asked")
            answered = tsem("gn1_answered")
            scaled = tsem("wr_scaled")
            blk = ph.enter_context(nc.Block())
            NQ = NS // 4

            @blk.sync
            def _(sp):
                for dst, name in ((wr[:], "w_reduceT"), (half_avg[:], "half_avg"), (vecs[:], "bn_vecs"),
                                  (tab1[:], "tab1")):
                    sp.dma_start(dst, A[name]).then_inc(w_loaded, 16)

                def load(i, b, first):
                    rows = [(i * 4 + b) * R + (R + 4 * h) for h in range(2)]
                    if not first:
                        rows = [sp.snap(row) for row in rows]
                        sp.wait_ge(r_made, i * 8 + 2 * (b - 3))
                    for h, row in enumerate(rows):
                        sp.dma_start(yc[b][C * h:C * h + C], y1[:, bass.ds(row, 4), :]).then_inc(y_loaded[b], 16)

                for b in range(4):
                    load(0, b, True)
                if NQ > 1:
                    with sp.Fori(1, NQ) as i:
                        for b in range(4):
                            load(i, b, False)

            @blk.scalar
            def _(act):
                group_norm_root(act, asked, answered, tmp)
                act.wait_ge(asked, 4)
                act.activation(acc[:, 7:8], acc[:, 7:8], ACT.Sqrt).then_inc(answered, 1)

            @blk.tensor
            def _(pe):
                pe.wait_ge(asked, 1)
                pe.matmul(bank[0][:, 0:2 * NI], pair_avg[:], tmp[:, 0:2, :].rearrange("p a i -> p (a i)"),
                          start=True, stop=True).then_inc(answered, 1)
                pe.wait_ge(scaled, 1)
                pe.matmul(bank[1][:, 0:NI], wr[:], gn_bias[:, 1, :], start=True, stop=True).then_inc(answered, 1)

                def products(img, j, b, first):
                    i = img * (NQ // NI) + j
                    pe.wait_ge(y_loaded[b], i * 32 + 32)
                    for h in range(2):
                        bk = 2 + 2 * (b % 2) + h
                        if not (first and b < 2):
                            pe.wait_ge(r_read, i * 8 + (2 * b + h - 3))
                        last = pe.matmul(bank[bk][:], wrs[:, img, :], yc[b][:, 2 * h:2 * h + 2, :].rearrange("p r w -> p (r w)"),
                                         start=True, stop=True)
                        last.then_inc(r_made, 1)

                for img in range(NI):
                    if img == 0:
                        for b in range(4):
                            products(0, 0, b, True)
                    j0 = 1 if img == 0 else 0
                    if NQ // NI > j0:
                        with pe.Fori(j0, NQ // NI) as j:
                            for b in range(4):
                                products(img, j, b, False)
                pe.wait_ge(asked, 3)
                pe.matmul(bank[1][:, 0:2], half_avg[:], acc[:, 0:2], start=True, stop=True).then_inc(answered, 1)

            @blk.vector
            def _(v):
                PERI = 2 * NS // NI
                for i in range(NI):
                    last = v.bn_aggr(mv[:, i, :], y_stats[:, PERI * i:PERI * i + PERI, :].rearrange("p a k -> p (a k)"))
                last.then_inc(step, 1)
                v.wait_ge(step, 1)
                count = [1]
                then = group_norm_params((step, asked, answered, count), v, 1, mv, tmp)
                v.wait_ge(w_loaded, 64)
                for i in range(NI):
                    last = v.tensor_scalar(wrs[:, i, :], wr[:], gn_scale[:, 1, i:i + 1], None, ALU.mult)
                last.then_inc(scaled, 1)
                with v.Fori(0, NQ) as i:
                    for b in range(4):
                        for h in range(2):
                            v.wait_ge(r_made, i * 8 + (2 * b + h + 1))
                            v.bn_stats(rst[:, bass.ds(i * 4 + b, 1), 6 * h:6 * h + 6].rearrange("p a k -> p (a k)"),
                                       bank[2 + 2 * (b % 2) + h][:]).then_inc(r_read, 1)
                v.wait_ge(r_read, 2 * NS)
                for i in range(NI):
                    last = v.bn_aggr(rmv[:, i, :], rst[:, S * i:S * i + S, :].rearrange("p a k -> p (a k)"))
                then(last)
                v.wait_ge(answered, 3)
                then(v.tensor_copy(const[:], bank[1][:, 0:NI]))
                then(v.tensor_tensor(rmv[:, :, 0], rmv[:, :, 0], const[:], ALU.add))
                then(v.tensor_scalar(rmv[:, :, 0], rmv[:, :, 0], vecs[:, 0:1], None, ALU.add))
                then(v.tensor_tensor(const[:], rmv[:, :, 0], rmv[:, :, 0], ALU.mult))
                then(v.tensor_tensor(rmv[:, :, 1], rmv[:, :, 1], const[:], ALU.add))
                then(v.tensor_reduce(acc[:, 0:2], rmv[:].rearrange("p i k -> p k i"), AX_X, ALU.add))
                v.tensor_copy(acc[:, 2:4], acc[:, 0:2]).then_inc(asked, 1)
                v.wait_ge(answered, 4)
                then(v.tensor_scalar(acc[:, 4:6], bank[1][:, 0:2], 1.0 / NI, None, ALU.mult))
                then(v.tensor_tensor(acc[:, 6:7], acc[:, 4:5], acc[:, 4:5], ALU.mult))
                then(v.tensor_tensor(acc[:, 7:8], acc[:, 5:6], acc[:, 6:7], ALU.subtract))
                v.tensor_scalar(acc[:, 7:8], acc[:, 7:8], 0.0, BN_EPS, ALU.max, ALU.add).then_inc(asked, 1)
                v.wait_ge(answered, 5)
                then(v.reciprocal(acc[:, 7:8], acc[:, 7:8]))
                then(v.tensor_tensor(bn_alpha[:], acc[:, 7:8], vecs[:, 1:2], ALU.mult))
                then(v.tensor_tensor(acc[:, 6:7], vecs[:, 0:1], acc[:, 4:5], ALU.subtract))
                then(v.scalar_tensor_tensor(bn_shift[:], acc[:, 6:7], bn_alpha[:, 0:1], vecs[:, 2:3], ALU.mult, ALU.add))
                for kind, src in ((0, gn_scale), (4, gn_bias)):
                    for i in range(NI):
                        lo = S * i + 1
                        then(v.tensor_copy(tab1[:, lo:lo + S, kind:kind + 4],
                                           src[:, 1:2, i:i + 1].to_broadcast([P, S, 4])))
                    nxt = tab1[C:P, 0:S * (NI - 1) + 1:S, :] if NI > 1 else tab1[C:P, 0:1, :]
                    for col in (1, 3):
                        then(v.tensor_copy(nxt[:, :, kind + col], src[C:P, 1, :]))
                    then(v.memset(tab1[C:P, S:NS + 1:S, kind + 2:kind + 3], 0.0))
                    then(v.memset(tab1[0:C, S:NS + 1:S, kind + 3:kind + 4], 0.0))

        with ExitStack() as ph:
            def tsb(name, shape, dt=F32):
                return ph.enter_context(nc.sbuf_tensor(name, shape, dt))

            def tsem(name):
                return ph.enter_context(nc.semaphore(name))

            xa = [tsb(f"xa{b}", [P, 4, W]) for b in range(2)]
            xb = [tsb(f"xb{b}", [P, 5, W]) for b in range(4)]
            x_mid = [tsb(f"x_mid{b}", [P, 4, WP]) for b in range(2)]
            x_up = [tsb(f"x_up{b}", [P, 4, WP]) for b in range(2)]
            x_down = [tsb(f"x_down{b}", [P, 4, WP]) for b in range(2)]
            par = [tsb(f"par1_{b}", [P, 10]) for b in range(4)]
            rn = tsb("rn", [P, 1024])
            prod = [tsb(f"prod{k}", [P, 1024]) for k in range(9)]
            inv = tsb("inv", [P, 1024])
            ab = tsb("ab", [P, 1024])
            z = [tsb(f"z{b}", [P, 5, WP]) for b in range(2)]
            pre = tsb("pre", [P, 1024])
            ab2 = tsb("ab2", [P, 1024])
            res = [tsb(f"res{b}", [P, 1024]) for b in range(2)]
            kern = tsb("kern", [P, 1024])
            kern_rest = tsb("kern_rest", [P, 1024])
            kern_parts = [tsb(f"kern_parts{b}", [P, 1024], BF16) for b in range(2)]
            sel = tsb("sel", [P, 9, P], BF16)
            sel_f = tsb("sel_f", [P, 9, P])
            span_w = tsb("span_w", [P, P])
            span_b = tsb("span_b", [P, 1])
            conv_w = tsb("conv_w", [P, 6, P])
            conv_b = tsb("conv_b", [P, 1])

            w_loaded = tsem("w1_loaded")
            xa_loaded = [tsem(f"xa_loaded{b}") for b in range(2)]
            xb_loaded = [tsem(f"xb_loaded{b}") for b in range(4)]
            zeroed = tsem("zeroed1")
            par_ready = tsem("par1_ready")
            mid_normed = tsem("mid_normed")
            normed = tsem("normed")
            r_done = tsem("r_done")
            rn_ready = tsem("rn_ready")
            kern_made = tsem("kern_made")
            kern_copied = tsem("kern_copied")
            split_step = tsem("split_step")
            parts_ready = tsem("parts_ready")
            sel_ready = tsem("sel_ready")
            kern_done = tsem("kern_done")
            prod_ready = tsem("prod_ready")
            half_sum = tsem("half_sum")
            pool_step = tsem("pool_step")
            sum_step = tsem("sum_step")
            exp_step = tsem("exp_step")
            log_ready = tsem("log_ready")
            z_written = tsem("z_written")
            z_ready = tsem("z_ready")
            conv_done = [tsem(f"conv_done{h}") for h in range(2)]
            conv_copied = [tsem(f"conv_copied{h}") for h in range(2)]
            exp2_step = tsem("exp2_step")
            log2_ready = tsem("log2_ready")
            resid_added = tsem("resid_added")
            out_ready = tsem("out_ready")
            out_stored = [tsem(f"out_stored{b}") for b in range(2)]
            blk = ph.enter_context(nc.Block())

            b_kern = (bank_pair[0], bank_pair[1])
            b_r = bank_pair[2]
            b_c = bank_pair[3]
            flat = lambda t: t[:].rearrange("p a b -> p (a b)")
            NB1 = N1 // 4

            def run1(eng, body):
                body(0, True)
                if NB1 > 1:
                    with eng.Fori(1, NB1) as i:
                        body(i, False)

            @blk.sync
            def _(sp):
                def load_a(r, r1, b):
                    sp.dma_start(xa[b % 2][0:C], y1_by_parity[:, 1, bass.ds(r, 4), :]).then_inc(xa_loaded[b % 2], 16)
                    sp.dma_start(xa[b % 2][C:P], y1_by_parity[:, 0, bass.ds(r1, 4), :]).then_inc(xa_loaded[b % 2], 16)

                def load_b(r, b):
                    sp.dma_start(xb[b][0:C], y1_by_parity[:, 0, bass.ds(r, 5), :]).then_inc(xb_loaded[b], 16)
                    sp.dma_start(xb[b][C:P], y1_by_parity[:, 1, bass.ds(r, 5), :]).then_inc(xb_loaded[b], 16)

                def store(r, b):
                    for h in range(2):
                        sp.dma_start(out_by_parity[:, h, bass.ds(r, 4), :],
                                     res[b % 2][C * h:C * h + C].rearrange("p (r w) -> p r w", w=W)).then_inc(out_stored[b % 2], 16)

                def body(i, first):
                    for k in range(4):
                        to, of, of1 = (i * 16 + n for n in (4 * (k - 2), 4 * (k + 2), 4 * (k + 2) + 1))
                        strips_normed, strips_out = i * 4 + (k + 1), i * 4 + (k - 1)
                        if not first:
                            to, of, of1 = sp.snap(to), sp.snap(of), sp.snap(of1)
                            strips_normed, strips_out = sp.snap(strips_normed), sp.snap(strips_out)
                        if first and k < 2:
                            sp.wait_ge(normed, strips_normed)
                        else:
                            sp.wait_ge(resid_added, strips_out)
                        load_a(of, of1, (k + 2) % 4)
                        load_b(of, (k + 2) % 4)
                        if not (first and k < 2):
                            sp.wait_ge(out_ready, strips_out)
                            store(to, (k - 2) % 4)

                for dst, name in ((span_w[:], "span_w"), (span_b[:], "span_b"), (sel_f[:], "sel"), (conv_w[:], "conv_w"), (conv_b[:], "conv_b")):
                    sp.dma_start(dst, A[name]).then_inc(w_loaded, 16)
                for u in range(2):
                    load_a(4 * u, 4 * u + 1, u)
                    load_b(4 * u, u)
                run1(sp, body)
                for b in range(2):
                    sp.wait_ge(out_stored[b], 32 * ((N1 - 2) // 2))
                sp.wait_ge(xa_loaded[1], 32 * (N1 // 2 + 1))
                sp.wait_ge(xb_loaded[0], 32 * (N1 // 4 + 1))
                sp.wait_ge(xb_loaded[1], 32 * (N1 // 4 + 1))

            @blk.gpsimd
            def _(pool):
                for t in x_mid + x_up + x_down + z:
                    last = nc.gpsimd.memset(t[:], 0.0)
                last.then_inc(zeroed, 1)
                for t in kern_parts:
                    last = nc.gpsimd.memset(t[:], 0.0)
                last.then_inc(zeroed, 1)

                def body(i, first):
                    for k in range(4):
                        for n in range(5):
                            pool.wait_ge(prod_ready, i * 36 + (9 * k + n + 2))
                            if n:
                                pool.wait_ge(pool_step, i * 16 + (4 * k + n))
                            ins = nc.gpsimd.tensor_tensor(prod[0][:], prod[0][:], prod[n + 1][:], ALU.add)
                            ins.then_inc(pool_step if n < 4 else half_sum, 1)
                        if not (first and k < 2):
                            pool.wait_ge(conv_copied[0], i * 4 + (k - 1))
                            pool.wait_ge(conv_copied[1], i * 4 + (k - 1))
                            if not (first and k < 4):
                                pool.wait_ge(out_stored[k % 2], (i * 4 + (k - 2) - k % 2 - 2) * 16 + 32)
                            nc.gpsimd.tensor_tensor(res[k % 2][:], pre[:], flat(xb[(k - 2) % 4])[:, 0:1024], ALU.add)\
                                .then_inc(resid_added, 1)

                run1(pool, body)

            @blk.tensor
            def _(pe):
                def r_product(u, b, h, before):
                    if h == 0:
                        pe.wait_ge(mid_normed, u + 1)
                        if before:
                            pe.wait_ge(kern_copied, u + 0)
                    pe.matmul(b_r[:, h, :], wr[:], x_mid[b][:, 2 * h:2 * h + 2, 1:W + 1], start=True, stop=True)\
                        .then_inc(r_done, 1)

                def weights(u, h):
                    if h == 0:
                        pe.wait_ge(rn_ready, u + 1)
                    pe.matmul(b_r[:, h, :], span_w[:], rn[:, 512 * h:512 * h + 512], start=True, stop=True)\
                        .then_inc(kern_made, 1)

                def conv(k, h, products):
                    for n in products:
                        j, dc = n // 3, n % 3
                        last = pe.matmul(b_c[:, h, :], conv_w[:, n, :], z[k % 2][:, 2 * h + j:2 * h + j + 2, dc:dc + W],
                                         start=n == 0, stop=n == 5)
                    if n == 5:
                        last.then_inc(conv_done[h], 1)

                def body(i, first):
                    for k in range(4):
                        pe.wait_ge(parts_ready, i * 4 + (k + 1))
                        for n in range(9):
                            if not (first and 9 * k + n < 2):
                                pe.wait_ge(prod_ready, i * 36 + (9 * k + n - 1))
                            for h in range(2):
                                last = pe.matmul(b_kern[(9 * k + n) % 2][:, h, :], sel[:, n, :],
                                                 kern_parts[k % 2][:, 512 * h:512 * h + 512], start=True, stop=True)
                            last.then_inc(kern_done, 1)
                            if n < 5 and not (first and k < 2):
                                conv(k - 2, 1, (n + 1,))
                            if n in (4, 5):
                                r_product(i * 4 + (k + 1), (k + 1) % 2, n - 4, True)
                            if n >= 7:
                                weights(i * 4 + (k + 1), n - 7)
                        if not (first and k == 0):
                            pe.wait_ge(z_ready, i * 4 + k)
                            if not (first and k == 1):
                                pe.wait_ge(conv_copied[0], i * 4 + (k - 1))
                            conv(k - 1, 0, range(6))
                            if not (first and k == 1):
                                pe.wait_ge(conv_copied[1], i * 4 + (k - 1))
                            conv(k - 1, 1, (0,))

                pe.wait_ge(w_loaded, 80)
                pe.wait_ge(sel_ready, 1)
                for h in range(2):
                    r_product(0, 0, h, False)
                for h in range(2):
                    weights(0, h)
                run1(pe, body)

            @blk.scalar
            def _(act):
                def norm(u, b, src, s0, dst, col):
                    p = par[b]
                    act.activation(dst[b % 2][:, 0:3, 1:W + 1], src[:, s0:s0 + 3, :], ACT.Identity,
                                   bias=p[:, 4:5], scale=p[:, 0:1])
                    return act.activation(dst[b % 2][:, 3, 1:W + 1], src[:, s0 + 3, :], ACT.Identity,
                                          bias=p[:, 4 + col:5 + col], scale=p[:, col:col + 1])

                def norm_mid(u, b, before):
                    act.wait_ge(xa_loaded[b % 2], (u - b % 2) * 16 + 32)
                    act.wait_ge(par_ready, u + 1)
                    if before:
                        act.wait_ge(prod_ready, (u - 1) * 9)
                        act.wait_ge(r_done, (u - 1) * 2)
                    norm(u, b, xa[b % 2], 0, x_mid, 1).then_inc(mid_normed, 1)

                def norm_up(u, b):
                    act.wait_ge(xb_loaded[b], (u - b) * 8 + 32)
                    norm(u, b, xb[b], 0, x_up, 2)

                def norm_down(u, b):
                    norm(u, b, xb[b], 1, x_down, 3).then_inc(normed, 1)

                def bn_relu(u, before):
                    act.wait_ge(r_done, u * 2 + 2)
                    if before:
                        act.wait_ge(kern_made, u * 2)
                    act.activation(rn[:], flat(b_r), ACT.Relu, bias=bn_shift[:, 0:1],
                                   scale=bn_alpha[:, 0:1]).then_inc(rn_ready, 1)

                def weights_copy(u, b, before):
                    act.wait_ge(kern_made, u * 2 + 2)
                    if before:
                        act.wait_ge(split_step, u * 2)
                    if not isinstance(u, int) or u >= 2:
                        act.wait_ge(kern_done, (u - 1) * 9)
                    act.activation(kern[:], flat(b_r), ACT.Identity, bias=span_b[:, 0:1])
                    act.activation(kern_parts[b][:], flat(b_r), ACT.Identity, bias=span_b[:, 0:1]).then_inc(kern_copied, 1)

                def conv_copy(i, k, h):
                    act.wait_ge(conv_done[h], i * 4 + (k - 1))
                    part = slice(512 * h, 512 * h + 512)
                    act.activation(ab2[:, part], b_c[:, h, :], ACT.Abs, bias=conv_b[:, 0:1]).then_inc(exp2_step, 1)
                    act.activation(pre[:, part], b_c[:, h, :], ACT.Relu, bias=conv_b[:, 0:1]).then_inc(conv_copied[h], 1)

                def body(i, first):
                    for k in range(4):
                        if not (first and k == 0):
                            act.wait_ge(sum_step, i * 12 + 3 * k)
                            if not (first and k == 1):
                                act.wait_ge(z_written, i * 8 + (2 * k - 3))
                            act.activation(ab[:], inv[:], ACT.Abs).then_inc(exp_step, 1)
                            act.wait_ge(exp_step, i * 8 + (2 * k - 1))
                            act.activation(ab[:], ab[:], ACT.Exp, scale=-1.0).then_inc(exp_step, 1)
                            act.wait_ge(exp_step, i * 8 + 2 * k)
                            act.activation(ab[:], ab[:], ACT.Ln, bias=1.0).then_inc(log_ready, 1)
                        u1, b1 = i * 4 + (k + 1), (k + 1) % 4
                        norm_mid(u1, b1, not (first and k == 0))
                        norm_up(u1, b1)
                        bn_relu(u1, True)
                        norm_down(u1, b1)
                        if not (first and k < 2):
                            if not (first and k == 2):
                                act.wait_ge(out_ready, i * 4 + (k - 2))
                            conv_copy(i, k, 0)
                        weights_copy(u1, (k + 1) % 2, True)
                        if not (first and k < 2):
                            conv_copy(i, k, 1)
                        if not (first and k < 2):
                            act.wait_ge(exp2_step, i * 12 + (3 * (k - 1) - 1))
                            act.activation(ab2[:], ab2[:], ACT.Exp, scale=-1.0).then_inc(exp2_step, 1)
                            act.wait_ge(exp2_step, i * 12 + 3 * (k - 1))
                            act.activation(ab2[:], ab2[:], ACT.Ln, bias=1.0).then_inc(log2_ready, 1)

                act.add_instruction(mybir.InstLoadActFuncSet(name=nc.get_next_instruction_name(),
                                                             act_func_set_id=EXP_AND_LN, engine=mybir.EngineType.Activation, ins=[], outs=[]))
                act.wait_ge(zeroed, 2)
                act.wait_ge(w_loaded, 80)
                norm_mid(0, 0, False)
                norm_up(0, 0)
                norm_down(0, 0)
                bn_relu(0, False)
                weights_copy(0, 0, False)
                run1(act, body)

            @blk.vector
            def _(v):
                def params(u, b):
                    if not isinstance(u, int) or u >= 4:
                        v.wait_ge(normed, u - 3)
                        v.wait_ge(z_ready, u - 3)
                    v.tensor_copy(par[b][:], tab1[:, bass.ds(u, 1), :].rearrange("p a k -> p (a k)")).then_inc(par_ready, 1)

                def z_finish(i, k, third):
                    b = (k - 1) % 2
                    v.wait_ge(log_ready, i * 4 + k)
                    if third:
                        v.wait_ge(conv_done[1], i * 4 + (k - 2))
                    if not (isinstance(i, int) and k == 1):
                        v.wait_ge(conv_done[0], i * 4 + (k - 1))
                    v.scalar_tensor_tensor(z[b][:, 1:5, 1:W + 1], inv[:].rearrange("p (r w) -> p r w", w=W), 0.0,
                                           ab[:].rearrange("p (r w) -> p r w", w=W), ALU.max, ALU.add).then_inc(z_written, 1)
                    v.wait_ge(z_written, i * 8 + 2 * k - 1)
                    masks = par[(k - 1) % 4][:, 8:10]
                    v.tensor_scalar(z[1 - b][:, 0, 1:W + 1], z[b][:, 4, 1:W + 1], masks[:, 0:1], None, ALU.mult)\
                        .then_inc(z_written, 1)
                    v.wait_ge(z_written, i * 8 + 2 * k)
                    v.tensor_scalar(z[b][:, 4, 1:W + 1], z[b][:, 4, 1:W + 1], masks[:, 1:2], None, ALU.mult).then_inc(z_ready, 1)

                def out_finish(i, k):
                    v.wait_ge(log2_ready, i * 4 + (k - 1))
                    v.wait_ge(resid_added, i * 4 + (k - 1))
                    v.tensor_tensor(res[k % 2][:], res[k % 2][:], ab2[:], ALU.add).then_inc(out_ready, 1)

                def split(u, b):
                    v.wait_ge(kern_copied, u + 1)
                    v.tensor_tensor(kern_rest[C:P], kern[C:P], kern_parts[b][C:P], ALU.subtract).then_inc(split_step, 1)
                    v.wait_ge(split_step, u * 2 + 1)
                    v.tensor_copy(kern_parts[b][C:P], kern_rest[C:P]).then_inc(split_step, 1)
                    v.wait_ge(split_step, u * 2 + 2)
                    v.tensor_tensor(kern_parts[b][96:P], kern_rest[96:P], kern_parts[b][96:P], ALU.subtract).then_inc(parts_ready, 1)

                def body(i, first):
                    for k in range(4):
                        b = k % 2
                        for n, (dr, dc) in enumerate(TAPS):
                            src = {-1: x_up, 0: x_mid, 1: x_down}[dr][b]
                            v.wait_ge(kern_done, i * 36 + (9 * k + n + 1))
                            if n == 0:
                                v.wait_ge(normed, i * 4 + (k + 1))
                            if n == 0 and not (first and k == 0):
                                v.wait_ge(sum_step, i * 12 + 3 * k)
                            if n < 6 and not (first and k == 0):
                                v.wait_ge(half_sum, i * 4 + k)
                            v.tensor_tensor(prod[n][:].rearrange("p (r w) -> p r w", w=W),
                                            flat(b_kern[(9 * k + n) % 2]).rearrange("p (r w) -> p r w", w=W),
                                            src[:, :, 1 + dc:1 + dc + W], ALU.mult).then_inc(prod_ready, 1)
                            if n == 2 and not (first and k == 0):
                                z_finish(i, k, not (first and k < 3))
                            if n == 3:
                                params(i * 4 + (k + 2), (k + 2) % 4)
                        for n, (a, c) in enumerate(((prod[6], prod[7]), (inv, prod[8]), (inv, prod[0]))):
                            if n == 0:
                                v.wait_ge(prod_ready, i * 36 + (9 * k + 9))
                                if not (first and k == 0):
                                    v.wait_ge(z_written, i * 8 + 2 * k)
                            else:
                                v.wait_ge(sum_step, i * 12 + (3 * k + n))
                            if n == 2:
                                split(i * 4 + (k + 1), (k + 1) % 2)
                                v.wait_ge(half_sum, i * 4 + (k + 1))
                            v.tensor_tensor(inv[:], a[:], c[:], ALU.add).then_inc(sum_step, 1)
                        if not (first and k < 2):
                            out_finish(i, k)

                v.wait_ge(zeroed, 1)
                v.wait_ge(w_loaded, 80)
                nc.vector.tensor_copy(sel[:], sel_f[:]).then_inc(sel_ready, 1)
                params(0, 0)
                params(1, 1)
                split(0, 0)
                run1(v, body)



def shape_constants(NI, S):
    NS, N1 = NI * S, strips_of_layer1(NI * S)
    out = {}
    m = np.arange(P)
    row, patch, col = m % 8, m // 64, m // 8 % 8
    real = [(0, 0), (0, 4), (4, 0), (4, 4)]
    pairs = [(u, w) for u in range(8) for w in range(8) if (u, w) not in real and (u, w) < ((-u) % 8, (-w) % 8)]
    assert len(pairs) == 30
    slots = [(half, pt, u, w, "RI"[half]) for half in range(2) for pt in range(2) for u, w in pairs]
    slots = slots[:60] + [(0, pt, u, w, "r") for pt in range(2) for u, w in real[:2]] \
        + slots[60:] + [(1, pt, u, w, "r") for pt in range(2) for u, w in real[2:]]
    f_all, g1, g2 = (np.zeros((P, P)) for _ in range(3))
    for f, (half, pt, u, w, kind) in enumerate(slots):
        on = patch == pt
        th = 2 * np.pi * (u * row + w * col) / 8
        cos, sin = np.cos(th) * on, np.sin(th) * on
        f_all[:, f] = -sin if kind == "I" else cos
        g1[f] = cos / 64 if kind == "r" else (2 * cos / 64 if kind == "R" else -2 * cos / 64)
        g2[f] = 0 if kind == "r" else -2 * sin / 64
    out["dft"], out["idft_1"], out["idft_2"] = f_all, g1, g2
    out["mean_w"] = np.full((P, P), 1.0 / P)
    ch = m % C
    out["pair_avg"] = (ch[:, None] // 2 == ch[None, :] // 2) / 4.0
    out["half_avg"] = (ch[:, None] == ch[None, :]) / 2.0
    tab0 = np.ones((P, NS + 2, 6))
    tap = (m - C) % 9
    for s in range(NS + 2):
        top, bottom = s % S == 0, s % S == S - 1
        tab0[:, s, 2], tab0[:, s, 3] = not top, not bottom
        tab0[:, s, 4] = np.where(tap < 3, not top, 1)
        tab0[:, s, 5] = np.where(tap >= 6, not bottom, 1)
    out["tab0"] = tab0
    tab1 = np.zeros((P, N1 + 2, 10))
    tab1[:, :, 8:10] = 1
    for u in range(0, N1 + 2):
        if u % S == 0:
            tab1[0:C, u, 8] = 0
            tab1[C:P, u, 9] = 0
    out["tab1"] = tab1
    b_sel = np.zeros((P, 2))
    b_sel[C:C + 9, 0] = 1
    b_sel[C + 9:C + 18, 1] = 1
    out["b_sel"] = b_sel
    out = {n: a.astype(np.float32) for n, a in out.items()}
    ind = np.zeros((P, W, R), np.float16)
    for part in range(2):
        for t, (dr, dc) in enumerate(TAPS):
            ind[C + 9 * part + t] = 1
            if dc == -1:
                ind[C + 9 * part + t, 0] = 0
            if dc == 1:
                ind[C + 9 * part + t, W - 1] = 0
    out["ind"] = ind
    return out


def two(a):
    return np.concatenate([a, a], axis=0)


def block_diagonal(a):
    out = np.zeros((P, P), a.dtype)
    out[0:C, 0:C] = a
    out[C:P, C:P] = a
    return out


def kernel(**inputs):
    import concourse.bacc as _bacc
    from concourse.bass_utils import run_bass_kernel_spmd as _run

    g = {n: np.asarray(a) for n, a in inputs.items()}
    x = g["x"]
    NI, _, H, _ = x.shape
    S = H // R
    NS, N1 = NI * S, strips_of_layer1(NI * S)
    arrays = shape_constants(NI, S)
    xt = np.zeros((C, 1 + NI * H + XTRA, W), x.dtype)
    xt[:, 1:1 + NI * H] = x.transpose(1, 0, 2, 3).reshape(C, NI * H, W)
    arrays["x"] = xt
    arrays["wh"] = two(g["L0_conv_w_hidden"].T)
    taps = g["L0_conv_w_dw"].reshape(HID, 9).T
    arrays["w_dw"] = np.broadcast_to(taps[None], (P, 9, HID))
    rows = np.zeros((P, HID), x.dtype)
    b_rows, d_rows = rows.copy(), rows.copy()
    for part in range(2):
        p0 = C + 9 * part
        rows[p0:p0 + 9] = taps
        b_rows[p0:p0 + 9] = g["L0_conv_b_hidden"]
        d_rows[p0 + 4] = g["L0_conv_b_dw"]
    arrays["w_dw_rows"], arrays["b_hidden_rows"], arrays["b_dw_rows"] = rows, b_rows, d_rows
    arrays["ln_wb"] = np.stack([g["L0_conv_ln_w"], g["L0_conv_ln_b"]], axis=1)
    arrays["w_projT"] = g["L0_conv_w_proj"].T
    arrays["b_proj"] = two(g["L0_conv_b_proj"])[:, None]
    arrays["w_reduceT"] = block_diagonal(g["L1_conv_w_reduce"].T)
    arrays["bn_vecs"] = two(np.stack([g["L1_conv_b_reduce"], g["L1_conv_bn_gamma"], g["L1_conv_bn_beta"]], axis=1))
    span, span_b, sel = np.zeros((P, P), x.dtype), np.zeros((P, 1), x.dtype), np.zeros((P, 9, P), np.float32)
    for part in (0, 64, 96):
        for p in range(2):
            rows = slice(part + 9 * p, part + 9 * p + 9)
            span[C * p:C * p + C, rows] = g["L1_conv_w_span"].T
            span_b[rows, 0] = g["L1_conv_b_span"]
            for n in range(9):
                sel[part + 9 * p + n, n, C * p:C * p + C] = 1
    arrays["span_w"], arrays["span_b"], arrays["sel"] = span, span_b, sel
    w2 = g["L1_conv_w_conv2"]
    cw = np.zeros((P, 6, P), x.dtype)
    for dc in range(3):
        cw[0:C, dc, 0:C] = w2[:, :, 0, dc].T
        cw[C:P, dc, 0:C] = w2[:, :, 1, dc].T
        cw[C:P, dc, C:P] = w2[:, :, 0, dc].T
        cw[0:C, 3 + dc, 0:C] = w2[:, :, 2, dc].T
        cw[0:C, 3 + dc, C:P] = w2[:, :, 1, dc].T
        cw[C:P, 3 + dc, C:P] = w2[:, :, 2, dc].T
    arrays["conv_w"] = cw
    arrays["conv_b"] = two(g["L1_conv_b_conv2"])[:, None]
    arrays = {n: np.ascontiguousarray(a) for n, a in arrays.items()}

    nc = _bacc.Bacc("TRN2", target_bir_lowering=False, num_devices=1)
    A, feeds = {}, {}
    for name, a in arrays.items():
        feeds[f"in_{name}_dram"] = a
        A[name] = nc.dram_tensor(f"in_{name}_dram", a.shape, mybir.dt.from_np(a.dtype), kind="ExternalInput").ap()
    A["out"] = nc.dram_tensor("out_0_dram", (C, R * N1, W), F32, kind="ExternalOutput").ap()
    build_program(nc, A, NI, S)
    r = _run(nc, [feeds], core_ids=[0])
    out = np.asarray(r.results[0]["out_0_dram"])[:, R:R + NI * H]
    return np.ascontiguousarray(out.reshape(C, NI, H, W).transpose(1, 0, 2, 3))
```

```python
from contextlib import ExitStack

import numpy as np

import concourse.bass as bass
from concourse import mybir

ALU = mybir.AluOpType
ACT = mybir.ActivationFunctionType
AX_X = mybir.AxisListType.X
F32 = mybir.dt.float32
F16 = mybir.dt.float16
BF16 = mybir.dt.bfloat16
EXP_AND_LN = 6
RMAX = bass.bass_isa.ReduceOp.max

P = 128
C = 64
W = 256
WP = W + 2
PATCH = 8
R = 8
KQ = 4 * C
XTRA = 9
GN_EPS = 1e-5
LN_EPS = 1e-5
BN_EPS = 1e-5
WSCALE = 256.0
GCOL = 64
ORDER = [0, 2, 1, 3]
TAPS = [(dr, dc) for dr in (-1, 0, 1) for dc in (-1, 0, 1)]


def strips_of_layer1(strips):
    return (strips + 1 + 3) // 4 * 4


def build_program(nc, A, NI, S):
    NS = NI * S
    ROWS = NS * R
    NG = NS * 4
    NB = NS // 2
    N1 = strips_of_layer1(NS)
    Y1R = R * (N1 + 1) + 10
    y1 = nc.dram_tensor("y1_scratch", (C, Y1R, W), F32, kind="Internal").ap()
    y1_by_parity = y1.rearrange("c (r two) w -> c two r w", two=2)
    out_by_parity = A["out"].rearrange("c (r two) w -> c two r w", two=2)

    with ExitStack() as ctx:
        def sb(name, shape, dt=F32):
            return ctx.enter_context(nc.sbuf_tensor(name, shape, dt))

        def sem(name):
            return ctx.enter_context(nc.semaphore(name))

        bank_pair = [ctx.enter_context(nc.psum_tensor(f"banks{i}", [P, 2, 512], F32)) for i in range(4)]
        bank = [bank_pair[i // 2][:, i % 2, :] for i in range(8)]

        gn_scale = sb("gn_scale", [P, 2, NI])
        gn_bias = sb("gn_bias", [P, 2, NI])
        pair_avg = sb("pair_avg", [P, P])
        bn_alpha = sb("bn_alpha", [P, 1])
        bn_shift = sb("bn_shift", [P, 1])
        small = sb("small", [P, 64])

        w_hi = sb("w_hi", [P, 9, KQ], F16)
        w_lo_pair = sb("w_lo_pair", [P, 3, KQ], F16)
        w_lo_one = sb("w_lo_one", [P, 2, KQ], F16)
        inv_wscale = sb("inv_wscale", [P, 1])
        dft = sb("dft", [P, P])
        idft = sb("idft", [P, P])
        imag_sign = sb("imag_sign", [P, 2])
        mean_w = sb("mean_w", [P, P])
        ln_wb = sb("ln_wb", [P, 2])
        proj_w = sb("proj_w", [P, C])
        v_hidden = sb("v_hidden", [C, P])
        v_vecs = sb("v_vecs", [P, 11])
        b_proj = sb("b_proj", [P, 1])
        tab0 = sb("tab0", [P, NS + 2, 6])

        with ExitStack() as ph:
            def tsb(name, shape, dt=F32):
                return ph.enter_context(nc.sbuf_tensor(name, shape, dt))

            wh = tsb("wh", [P, KQ])
            w_dw = tsb("w_dw", [P, 9, KQ])
            w_all = tsb("w_all", [P, 9, KQ])
            bh = tsb("bh", [P, KQ])
            bdw = tsb("bdw", [P, KQ])
            bd = tsb("bd", [P, KQ])
            btap = tsb("btap", [P, KQ])
            b_hi = tsb("b_hi", [P, KQ], F16)
            b_sel = tsb("b_sel", [P, 2])
            zrow = tsb("zrow", [C, 18, W])
            wmax = tsb("wmax", [P, 4])
            loaded = ph.enter_context(nc.semaphore("weights_loaded"))
            step = ph.enter_context(nc.semaphore("weight_step"))
            maxed = ph.enter_context(nc.semaphore("weight_max"))
            zeroed = ph.enter_context(nc.semaphore("zeros_made"))
            stored = ph.enter_context(nc.semaphore("zeros_stored"))
            blk = ph.enter_context(nc.Block())
            loads = [(wh[:], "wh"), (w_dw[:], "w_dw"), (bh[:], "b_hidden_rows"), (bdw[:], "w_dw_rows"),
                     (bd[:], "b_dw_rows"), (b_sel[:], "b_sel"), (ln_wb[:], "ln_wb"), (proj_w[:], "w_projT"),
                     (v_hidden[:], "v_hiddenT"), (v_vecs[:], "v_vecs"),
                     (dft[:], "dft"), (idft[:], "idft"), (imag_sign[:], "imag_sign"),
                     (mean_w[:], "mean_w"), (b_proj[:], "b_proj"), (tab0[:], "tab0"), (pair_avg[:], "pair_avg")]

            @blk.sync
            def _(sp):
                for dst, name in loads:
                    sp.dma_start(dst, A[name]).then_inc(loaded, 16)
                sp.wait_ge(zeroed, 1)
                sp.dma_start(y1[:, 0:R, :], zrow[:, 0:R, :]).then_inc(stored, 16)
                n = 16
                for r0 in range(R + ROWS, Y1R, 18):
                    k = min(18, Y1R - r0)
                    sp.dma_start(y1[:, r0:r0 + k, :], zrow[:, 0:k, :]).then_inc(stored, 16)
                    n += 16
                sp.wait_ge(stored, n)

            @blk.gpsimd
            def _(pool):
                nc.gpsimd.memset(zrow[:], 0.0).then_inc(zeroed, 1)
                pool.wait_ge(maxed, 1)
                nc.gpsimd.partition_all_reduce(wmax[:, 2:3], wmax[:, 1:2], P, RMAX).then_inc(maxed, 1)

            @blk.vector
            def _(v):
                count = [0]

                def then(ins):
                    count[0] += 1
                    ins.then_inc(step, 1)
                    v.wait_ge(step, count[0])

                v.wait_ge(loaded, 16 * len(loads))
                for t in range(9):
                    then(v.tensor_tensor(w_all[:, t, :], w_dw[:, t, :], wh[:], ALU.mult))
                then(v.tensor_tensor(btap[:], bh[:], bdw[:], ALU.mult))
                then(v.tensor_tensor(btap[:], btap[:], bd[:], ALU.add))
                then(v.scalar_tensor_tensor(w_dw[:], w_all[:], -1.0, w_all[:], ALU.mult, ALU.max))
                then(v.tensor_reduce(wmax[:, 0:1], w_dw[:].rearrange("p t o -> p (t o)"), AX_X, ALU.max))
                then(v.scalar_tensor_tensor(bh[:], btap[:], -1.0, btap[:], ALU.mult, ALU.max))
                then(v.tensor_reduce(wmax[:, 3:4], bh[:], AX_X, ALU.max))
                v.tensor_tensor(wmax[:, 1:2], wmax[:, 0:1], wmax[:, 3:4], ALU.max).then_inc(maxed, 1)
                v.wait_ge(maxed, 2)
                then(v.tensor_scalar(wmax[:, 2:3], wmax[:, 2:3], 1e-30, None, ALU.max))
                then(v.tensor_scalar(inv_wscale[:], wmax[:, 2:3], 1.0 / WSCALE, None, ALU.mult))
                then(v.reciprocal(wmax[:, 0:1], inv_wscale[:]))
                then(v.tensor_scalar(w_all[:], w_all[:], wmax[:, 0:1], None, ALU.mult))
                then(v.tensor_copy(w_hi[:], w_all[:]))
                then(v.tensor_tensor(w_dw[:], w_all[:], w_hi[:], ALU.subtract))
                then(v.memset(w_lo_one[:], 0.0))
                then(v.tensor_copy(w_lo_pair[0:C], w_dw[0:C, 0:3, :]))
                then(v.tensor_copy(w_lo_pair[C:P], w_dw[C:P, 3:6, :]))
                then(v.tensor_copy(w_lo_one[0:C], w_dw[0:C, 6:8, :]))
                then(v.tensor_copy(w_lo_one[C:P, 0, :], w_dw[C:P, 8, :]))
                then(v.tensor_scalar(btap[:], btap[:], wmax[:, 0:1], None, ALU.mult))
                then(v.tensor_copy(b_hi[:], btap[:]))
                then(v.tensor_tensor(btap[:], btap[:], b_hi[:], ALU.subtract))
                then(v.tensor_scalar(btap[:], btap[:], b_sel[:, 1:2], None, ALU.mult))
                then(v.scalar_tensor_tensor(btap[:], b_hi[:], b_sel[:, 0:1], btap[:], ALU.mult, ALU.add))
                then(v.tensor_copy(w_lo_one[C:P, 1, :], btap[C:P]))

        def group_norm_params(blk_sems, v, layer, mv, tmp):
            step, asked, answered, count = blk_sems

            def then(ins):
                count[0] += 1
                ins.then_inc(step, 1)
                v.wait_ge(step, count[0])

            mean, var = mv[:, :, 0], mv[:, :, 1]
            then(v.tensor_tensor(tmp[:, 0, :], mean, mean, ALU.mult))
            then(v.tensor_tensor(tmp[:, 1, :], tmp[:, 0, :], var, ALU.add))
            then(v.tensor_copy(tmp[:, 0, :], mean))
            v.tensor_copy(tmp[:, 2, :], mean).then_inc(asked, 1)
            v.wait_ge(answered, 1)
            then(v.tensor_copy(tmp[:, 0:2, :], bank[0][:, 0:2 * NI].rearrange("p (a i) -> p a i", i=NI)))
            then(v.tensor_tensor(tmp[:, 2, :], tmp[:, 0, :], tmp[:, 0, :], ALU.mult))
            then(v.tensor_tensor(tmp[:, 2, :], tmp[:, 1, :], tmp[:, 2, :], ALU.subtract))
            v.tensor_scalar(tmp[:, 2, :], tmp[:, 2, :], 0.0, GN_EPS, ALU.max, ALU.add).then_inc(asked, 1)
            v.wait_ge(answered, 2)
            then(v.reciprocal(gn_scale[:, layer, :], tmp[:, 2, :]))
            then(v.scalar_tensor_tensor(gn_bias[:, layer, :], tmp[:, 0, :], -1.0, gn_scale[:, layer, :],
                                        ALU.mult, ALU.mult))
            return then

        def group_norm_root(act, asked, answered, tmp):
            act.wait_ge(asked, 2)
            act.activation(tmp[:, 2, :], tmp[:, 2, :], ACT.Sqrt).then_inc(answered, 1)

        with ExitStack() as ph:
            CH = 2 * R
            NC = ROWS // (2 * CH)
            PER = NC // NI
            NST = CH * W // 512
            xc = ph.enter_context(nc.sbuf_tensor("xc", [P, 2, CH * W], F32))
            st = ph.enter_context(nc.sbuf_tensor("st", [P, NC, NST * 6], F32))
            mv = ph.enter_context(nc.sbuf_tensor("mv", [P, NI, 2], F32))
            tmp = ph.enter_context(nc.sbuf_tensor("tmp", [P, 3, NI], F32))
            loaded = [ph.enter_context(nc.semaphore(f"chunk_loaded{i}")) for i in range(2)]
            used = ph.enter_context(nc.semaphore("chunk_used"))
            step = ph.enter_context(nc.semaphore("gn0_step"))
            asked = ph.enter_context(nc.semaphore("gn0_asked"))
            answered = ph.enter_context(nc.semaphore("gn0_answered"))
            blk = ph.enter_context(nc.Block())

            @blk.sync
            def _(sp):
                def load(i, b, first):
                    rows = [1 + (2 * CH) * (i * 2 + b) + CH * h for h in range(2)]
                    if not first:
                        rows = [sp.snap(row) for row in rows]
                        sp.wait_ge(used, i * 2 + b - 1)
                    for h, row in enumerate(rows):
                        sp.dma_start(xc[C * h:C * h + C, b, :].rearrange("p (r w) -> p r w", w=W),
                                     A["x"][:, bass.ds(row, CH), :]).then_inc(loaded[b], 16)

                load(0, 0, True)
                load(0, 1, True)
                if NC > 2:
                    with sp.Fori(1, NC // 2) as i:
                        load(i, 0, False)
                        load(i, 1, False)

            @blk.vector
            def _(v):
                with v.Fori(0, NC // 2) as i:
                    for b in range(2):
                        v.wait_ge(loaded[b], i * 32 + 32)
                        for n in range(NST):
                            last = v.bn_stats(st[:, bass.ds(i * 2 + b, 1), 6 * n:6 * n + 6].rearrange("p a k -> p (a k)"),
                                              xc[:, b, 512 * n:512 * n + 512])
                        last.then_inc(used, 1)
                v.wait_ge(used, NC)
                for i in range(NI):
                    last = v.bn_aggr(mv[:, i, :], st[:, PER * i:PER * i + PER, :].rearrange("p a k -> p (a k)"))
                last.then_inc(step, 1)
                v.wait_ge(step, 1)
                then = group_norm_params((step, asked, answered, [1]), v, 0, mv, tmp)
                for i in range(NI):
                    then(v.tensor_copy(tab0[:, S * i:S * i + S, 0:1],
                                       gn_scale[:, 0:1, i:i + 1].to_broadcast([P, S, 1])))
                    then(v.tensor_copy(tab0[:, S * i:S * i + S, 1:2],
                                       gn_bias[:, 0:1, i:i + 1].to_broadcast([P, S, 1])))

            @blk.scalar
            def _(act):
                group_norm_root(act, asked, answered, tmp)

            @blk.tensor
            def _(pe):
                pe.wait_ge(asked, 1)
                pe.matmul(bank[0][:, 0:2 * NI], pair_avg[:], tmp[:, 0:2, :].rearrange("p a i -> p (a i)"),
                          start=True, stop=True).then_inc(answered, 1)

        y_stats = sb("y_stats", [P, NS * 2, 6])

        with ExitStack() as ph:
            def tsb(name, shape, dt=F32):
                return ph.enter_context(nc.sbuf_tensor(name, shape, dt))

            def tsem(name):
                return ph.enter_context(nc.semaphore(name))

            SL = R + 3
            SLP = R + 4
            xr = [tsb(f"xr{b}", [P, SL, W]) for b in range(2)]
            x_res = [tsb(f"x_res{b}", [P, R, 2 * GCOL]) for b in range(2)]
            xn = tsb("xn", [P, W, SLP])
            hi_all = tsb("hi_all", [P, WP, SLP], F16)
            hl_all = tsb("hl_all", [P, WP, SLP], F16)
            hi_lo = [[tsb(f"hi_lo{b}_{d}", [P, WP, R], F16) for d in range(3)] for b in range(2)]
            hi_pair = [tsb(f"hi_pair{b}", [P, WP, R], F16) for b in range(2)]
            hi_ind = [tsb(f"hi_ind{b}", [P, WP, R], F16) for b in range(2)]
            hi_side = [tsb(f"hi_side{b}", [P, WP, R], F16) for b in range(2)]
            par = [tsb(f"par{b}", [P, 6]) for b in range(2)]
            ind = tsb("ind", [P, W, R], F16)
            qk = tsb("qk", [P, 4, KQ])
            q_re = tsb("q_re", [P, 512])
            q_im = tsb("q_im", [P, 512])
            k_swap = tsb("k_swap", [P, 512])
            u = tsb("u", [P, 512])
            u_im = tsb("u_im", [P, 512])
            u_mean = tsb("u_mean", [P, 4])
            hv = [tsb(f"hv{b}", [P, WP, R + 2]) for b in range(2)]
            v_s = [tsb(f"v_s{i}", [P, 512]) for i in range(4)]
            t_n = tsb("t_n", [P, 512])
            w_v = [tsb(f"w_v{i}", [P, 512]) for i in range(4)]
            sq = tsb("sq", [P, 512])
            rs = tsb("rs", [P, 512])
            eps = tsb("eps", [P, 1])
            ys = [tsb(f"ys{b}", [P, R, 2 * GCOL]) for b in range(2)]

            x_loaded = [tsem(f"x_loaded{b}") for b in range(2)]
            res_loaded = [tsem(f"res_loaded{b}") for b in range(2)]
            ind_loaded = tsem("ind_loaded")
            buffers_zeroed = tsem("buffers_zeroed")
            par_ready = tsem("par_ready")
            xn_made = tsem("xn_made")
            xn_masked = tsem("xn_masked")
            hi_made = tsem("hi_made")
            below_copied = tsem("below_copied")
            low_made = tsem("low_made")
            stacks_ready = tsem("stacks_ready")
            qk_conv = tsem("qk_conv")
            qk_copied = tsem("qk_copied")
            k_freq = tsem("k_freq")
            k_swapped = tsem("k_swapped")
            q_copied = tsem("q_copied")
            q_split = tsem("q_split")
            q_im_ready = tsem("q_im_ready")
            k_read = tsem("k_read")
            u_made = tsem("u_made")
            u_step = tsem("u_step")
            u_summed = tsem("u_summed")
            means_ready = tsem("means_ready")
            u_ready = tsem("u_ready")
            inv_done = tsem("inv_done")
            h_done = tsem("h_done")
            h_copied = tsem("h_copied")
            h_ready = tsem("h_ready")
            v_begun = tsem("v_begun")
            tap_step = tsem("tap_step")
            sq_ready = tsem("sq_ready")
            var_done = tsem("var_done")
            log_ready = tsem("log0_ready")
            rs_ready = tsem("rs_ready")
            t_ready = tsem("t_ready")
            affine_ready = tsem("affine_ready")
            w_ready = tsem("w_ready")
            fin_done = tsem("fin_done")
            fin_read = tsem("fin_read")
            pair_ready = tsem("pair_ready")
            y_stored = [tsem(f"y_stored{b}") for b in range(2)]
            blk = ph.enter_context(nc.Block())

            b_qk, b_h, b_q, b_k, b_o, b_var, b_y = (bank[0], bank[1]), bank[2], bank[3], bank[4], bank[5], bank[6], bank[7]

            CHUNKS = {0: (), 1: ((0, 0), (1, 2), (2, 3)), 2: ((3, 0), (4, 2), (5, 3)), 3: ((6, 2), (7, 3))}

            def run(eng, body, tail=None):
                body(0, True)
                if NB > 1:
                    with eng.Fori(1, NB) as i:
                        body(i, False)
                if tail:
                    tail()

            @blk.sync
            def _(sp):
                def load(row, b):
                    sp.dma_start(xr[b][0:C, 1:SL, :], A["x"][:, bass.ds(row, R + 2), :]).then_inc(x_loaded[b], 16)
                    sp.dma_start(xr[b][C:P, 0:SL - 1, :], A["x"][:, bass.ds(row, R + 2), :]).then_inc(x_loaded[b], 16)

                def load_res(row, b):
                    for h in range(2):
                        sp.dma_start(x_res[b][C * h:C * h + C],
                                     A["x"][:, bass.ds(row, R), 2 * GCOL * h:2 * GCOL * h + 2 * GCOL]).then_inc(res_loaded[b], 16)

                def store(row, b):
                    for h in range(2):
                        sp.dma_start(y1[:, bass.ds(row, R), 2 * GCOL * h:2 * GCOL * h + 2 * GCOL],
                                     ys[b][C * h:C * h + C]).then_inc(y_stored[b], 16)

                def body(i, first):
                    for b in range(2):
                        if not (first and b == 0):
                            to, of, of_res = i * 2 * R + b * R, i * 2 * R + (b + 1) * R, i * 2 * R + (b + 1) * R + 1
                            normed_before, pairs_before = i * 2 + b, i * 4 + 2 * b
                            if not first:
                                to, of, of_res = sp.snap(to), sp.snap(of), sp.snap(of_res)
                                normed_before, pairs_before = sp.snap(normed_before), sp.snap(pairs_before)
                            sp.wait_ge(xn_made, normed_before)
                            load(of, 1 - b)
                            sp.wait_ge(pair_ready, pairs_before)
                            load_res(of_res, 1 - b)
                            store(to, 1 - b)

                sp.dma_start(ind[:], A["ind"]).then_inc(ind_loaded, 16)
                sp.wait_ge(buffers_zeroed, 1)
                for b in range(2):
                    load(R * b, b)
                    load_res(R * b + 1, b)
                run(sp, body)
                sp.wait_ge(pair_ready, 2 * NS)
                store(NS * R, 1)
                sp.wait_ge(y_stored[0], 16 * NS)
                sp.wait_ge(y_stored[1], 16 * NS)
                sp.wait_ge(x_loaded[0], 32 * (NS // 2) + 32)
                sp.wait_ge(res_loaded[0], 32 * (NS // 2) + 32)

            @blk.gpsimd
            def _(pool):
                nc.gpsimd.memset(eps[:], LN_EPS)
                for t in xr + [xn, hi_all, hl_all] + hi_ind + hi_side + hv:
                    last = nc.gpsimd.memset(t[:], 0.0)
                last.then_inc(buffers_zeroed, 1)

                def edge_rows(i, strip, first_chunk, chunks):
                    pool.wait_ge(h_copied, i * 16 + (8 * strip + first_chunk + chunks))
                    cols = slice(1 + 32 * first_chunk, 1 + 32 * (first_chunk + chunks))
                    for slot, col in ((0, 2), (R + 1, 3)):
                        rows = hv[strip % 2][:, cols, slot]
                        last = nc.gpsimd.tensor_tensor(rows, rows, par[strip % 2][:, col:col + 1].to_broadcast([P, 32 * chunks]),
                                                       ALU.mult)
                    last.then_inc(h_ready, 1)

                def low_parts(s, half):
                    pool.wait_ge(hi_made, s + 1)
                    if not isinstance(s, int) or s >= 1:
                        pool.wait_ge(stacks_ready, s + 0)
                    c0, c1 = W // 2 * half, W // 2 * half + W // 2
                    nc.gpsimd.tensor_tensor(hl_all[C:P, 1 + c0:1 + c1, 1:SL], xn[C:P, c0:c1, 0:SL - 1],
                                            hi_all[C:P, 1 + c0:1 + c1, 0:SL - 1], ALU.subtract).then_inc(low_made, 1)
                    pool.wait_ge(low_made, s * 2 + (half + 1))

                def imaginary(i, k, any_before):
                    pool.wait_ge(q_im_ready, i * 8 + k)
                    if any_before:
                        pool.wait_ge(u_step, i * 8 + (k - 1))
                    nc.gpsimd.tensor_tensor(u_im[:], q_im[:], k_swap[:], ALU.mult).then_inc(u_made, 1)
                    pool.wait_ge(u_made, i * 8 + k)
                    pool.wait_ge(k_read, i * 8 + k)
                    nc.gpsimd.tensor_tensor(u[:], u[:], u_im[:], ALU.add).then_inc(u_step, 1)

                def less_mean(i, k):
                    pool.wait_ge(means_ready, i * 8 + k)
                    u4 = u[:].rearrange("p (t c) -> p t c", t=4)
                    nc.gpsimd.tensor_tensor(u4, u4, u_mean[:].unsqueeze(2).to_broadcast([P, 4, P]), ALU.subtract)\
                        .then_inc(u_ready, 1)

                def times_v(i, k, ring_used):
                    pool.wait_ge(affine_ready, i * 8 + (k - 1))
                    pool.wait_ge(tap_step, i * 64 + 8 * (k - 1))
                    if ring_used:
                        pool.wait_ge(fin_done, i * 4 + (k - 6) // 2 + 1)
                    nc.gpsimd.tensor_tensor(w_v[(k - 2) % 4][:], t_n[:], v_s[(k - 2) % 4][:], ALU.mult).then_inc(w_ready, 1)

                def body(i, first):
                    for k in range(8):
                        if k % 4 == 2:
                            pool.wait_ge(h_ready, i * 6 + (3 * (k // 4) + 4))
                            low_parts(i * 2 + (k // 4 + 1), 0)
                        if not (first and k == 0):
                            imaginary(i, k, not (first and k == 1))
                            less_mean(i, k)
                        if not (first and k < 2):
                            times_v(i, k, not (first and k < 6))
                        if k % 4 == 2:
                            pool.wait_ge(w_ready, i * 8 + (k - 1))
                            low_parts(i * 2 + (k // 4 + 1), 1)
                        if k % 4:
                            edge_rows(i, k // 4 + 1, CHUNKS[k % 4][0][0], len(CHUNKS[k % 4]))

                def tail():
                    imaginary(NB, 0, True)
                    less_mean(NB, 0)
                    times_v(NB, 0, True)
                    times_v(NB, 1, True)

                for half in range(2):
                    low_parts(0, half)
                pool.wait_ge(par_ready, 1)
                for k in range(1, 4):
                    edge_rows(0, 0, CHUNKS[k][0][0], len(CHUNKS[k]))
                run(pool, body, tail)

            @blk.tensor
            def _(pe):
                def conv(b, out, tile):
                    n = 0
                    def one(src, dc, w):
                        nonlocal n
                        px = src[:, 16 * tile + dc + 1:16 * tile + dc + 17, :].rearrange("p c r -> p (c r)")
                        r = pe.matmul(out, px, w, start=n == 0, stop=n == 13)
                        n += 1
                        return r
                    for t, (dr, dc) in enumerate(TAPS):
                        one(hi_lo[b][dr + 1], dc, w_hi[:, t, :])
                    for j, dc in enumerate((-1, 0, 1)):
                        one(hi_pair[b], dc, w_lo_pair[:, j, :])
                    one(hi_side[b], -1, w_lo_one[:, 0, :])
                    return one(hi_ind[b], 0, w_lo_one[:, 1, :])

                def hidden(i, strip, chunk, before):
                    if before:
                        pe.wait_ge(h_copied, i * 16 + (8 * strip + chunk))
                    pe.matmul(b_h[:, 0:320], v_hidden[:], xn[0:C, 32 * chunk:32 * chunk + 32, 1:R + 3],
                              start=True, stop=True).then_inc(h_done, 1)

                def project(i, k, any_before):
                    pe.wait_ge(w_ready, i * 8 + (k - 2))
                    if any_before:
                        pe.wait_ge(fin_read, i * 4 + (k - 4) // 2)
                    for h in range(2):
                        last = pe.matmul(b_y[C * h:C * h + C, :], proj_w[:], w_v[(k - 4 + h) % 4][:], start=True, stop=True)
                    last.then_inc(fin_done, 1)

                def inverse(i, k, any_before):
                    pe.wait_ge(u_ready, i * 8 + k)
                    if any_before:
                        pe.wait_ge(t_ready, i * 8 + (k - 1))
                    for t in range(4):
                        px = slice(P * t, P * t + P)
                        last = pe.matmul(b_o[:, px], u[:, px], idft[:], start=True, stop=True)
                    last.then_inc(inv_done, 1)

                def variance(i, k, any_before):
                    pe.wait_ge(sq_ready, i * 8 + (k - 1))
                    if any_before:
                        pe.wait_ge(log_ready, i * 8 + (k - 2))
                    pe.matmul(b_var[:], mean_w[:], sq[:], start=True, stop=True).then_inc(var_done, 1)

                def body(i, first):
                    for k in range(8):
                        b = k // 4
                        cg = ORDER[k % 4]
                        if k % 4 == 0:
                            pe.wait_ge(stacks_ready, i * 2 + (b + 1))
                            pe.wait_ge(hi_made, i * 2 + (b + 1))
                        for t in range(4):
                            if t % 2 == 0 and not (first and k == 0):
                                pe.wait_ge(qk_copied, i * 16 + (2 * k - 1 + t // 2))
                            last = conv(b, b_qk[t // 2][:, KQ * (t % 2):KQ * (t % 2) + KQ], 4 * cg + t)
                            if t % 2:
                                last.then_inc(qk_conv, 1)
                            if t == 0 and not (first and k < 2):
                                variance(i, k, not (first and k == 2))
                            if t == 3 and k % 2 == 0 and not (first and k < 4):
                                project(i, k, not (first and k < 6))
                            for chunk, tile in CHUNKS[k % 4]:
                                if tile == t:
                                    if chunk == 0:
                                        pe.wait_ge(xn_masked, i * 2 + (b + 2))
                                    hidden(i, b + 1, chunk, True)
                        pe.wait_ge(qk_copied, i * 16 + (2 * k + 2))
                        if not (first and k == 0):
                            pe.wait_ge(k_read, i * 8 + k)
                            pe.wait_ge(q_split, i * 8 + k)
                        pe.matmul(b_q[:], dft[:], qk[:, :, 0:P], start=True, stop=True)
                        pe.matmul(b_k[:], dft[:], qk[:, :, P:KQ], start=True, stop=True).then_inc(k_freq, 1)
                        if not (first and k == 0):
                            inverse(i, k, not (first and k == 1))

                def tail():
                    variance(NB, 0, True)
                    project(NB, 0, True)
                    inverse(NB, 0, True)
                    variance(NB, 1, True)
                    project(NB, 2, True)

                pe.wait_ge(xn_masked, 1)
                for chunk in range(8):
                    hidden(0, 0, chunk, chunk > 0)
                run(pe, body, tail)

            @blk.scalar
            def _(act):
                def normed(s, b):
                    act.wait_ge(x_loaded[b], (s - b) * 16 + 32)
                    act.wait_ge(par_ready, s + 1)
                    if not isinstance(s, int) or s >= 1:
                        act.wait_ge(stacks_ready, s + 0)
                        act.wait_ge(hi_made, s + 0)
                        act.wait_ge(h_done, s * 8)
                    act.activation(xn[:, :, 0:SL], xr[b][:].rearrange("p s w -> p w s"), ACT.Identity, bias=par[b][:, 1:2],
                                   scale=par[b][:, 0:1]).then_inc(xn_made, 1)

                def hidden_copy(i, strip, chunk):
                    act.wait_ge(h_done, i * 16 + (8 * strip + chunk + 1))
                    if chunk == 0 and not (isinstance(i, int) and i == 0 and strip < 2):
                        act.wait_ge(tap_step, i * 64 + 32 * (strip - 1))
                    act.activation(hv[strip % 2][:, 1 + 32 * chunk:33 + 32 * chunk, :],
                                   b_h[:, 0:320].rearrange("p (c r) -> p c r", r=R + 2), ACT.Identity,
                                   bias=v_vecs[:, 9:10]).then_inc(h_copied, 1)

                def v_begin(i, k, any_before):
                    b, c0 = ((k - 1) // 4) % 2, GCOL * ORDER[(k - 1) % 4]
                    act.wait_ge(h_ready, i * 6 + 3 * ((k - 1) // 4 + 1))
                    if any_before:
                        act.wait_ge(w_ready, i * 8 + (k - 4))
                    act.activation(v_s[(k - 1) % 4][:].rearrange("p (c r) -> p c r", r=R), hv[b][:, c0 + 1:c0 + 1 + GCOL, 1:R + 1],
                                   ACT.Identity, bias=v_vecs[:, 10:11], scale=v_vecs[:, 4:5]).then_inc(v_begun, 1)

                def high_parts(s):
                    act.wait_ge(xn_masked, s + 1)
                    act.copy(hi_all[:, 1:W + 1, :], xn[:]).then_inc(hi_made, 1)

                def freq_copy(i, k, any_before):
                    act.wait_ge(k_freq, i * 8 + k)
                    if any_before:
                        act.wait_ge(u_step, i * 8 + (k - 1))
                    act.copy(k_swap[C:P, :], b_k[0:C, :])
                    act.copy(k_swap[0:C, :], b_k[C:P, :]).then_inc(k_swapped, 1)
                    act.activation(q_im[0:C, :], b_q[C:P, :], ACT.Copy, scale=imag_sign[0:C, 0:1])
                    act.activation(q_im[C:P, :], b_q[C:P, :], ACT.Copy, scale=imag_sign[C:P, 1:2]).then_inc(q_im_ready, 1)
                    act.copy(q_re[0:C, :], b_q[0:C, :])
                    act.copy(q_re[C:P, :], b_q[0:C, :]).then_inc(q_copied, 1)
                    act.wait_ge(q_copied, i * 8 + k)
                    act.copy(q_re[C:C + 4, :], b_q[C:C + 4, :]).then_inc(q_split, 1)

                def root(i, k, any_before):
                    act.wait_ge(var_done, i * 8 + (k - 1))
                    if any_before:
                        act.wait_ge(t_ready, i * 8 + (k - 2))
                    act.activation(rs[:], b_var[:], ACT.Ln, bias=eps[:, 0:1]).then_inc(log_ready, 1)
                    act.wait_ge(log_ready, i * 8 + (k - 1))
                    act.activation(rs[:], rs[:], ACT.Exp, scale=-0.5).then_inc(rs_ready, 1)

                def affine(i, k):
                    act.wait_ge(t_ready, i * 8 + (k - 1))
                    act.activation(t_n[:], t_n[:], ACT.Identity, bias=ln_wb[:, 1:2], scale=ln_wb[:, 0:1]).then_inc(affine_ready, 1)

                def square(i, k, any_before):
                    act.wait_ge(inv_done, i * 8 + k)
                    if any_before:
                        act.wait_ge(var_done, i * 8 + (k - 1))
                    act.activation(sq[:], b_o[:], ACT.Square).then_inc(sq_ready, 1)

                def body(i, first):
                    for k in range(8):
                        if not (first and k == 0):
                            v_begin(i, k, not (first and k < 5))
                            freq_copy(i, k, not (first and k == 1))
                        if len(CHUNKS[k % 4]) == 3:
                            hidden_copy(i, k // 4 + 1, CHUNKS[k % 4][0][0])
                        if not (first and k < 2):
                            root(i, k, not (first and k == 2))
                        for h in range(2):
                            act.wait_ge(qk_conv, i * 16 + (2 * k + h + 1))
                            if not (first and k == 0):
                                act.wait_ge(k_freq, i * 8 + k)
                            act.activation(qk[:, 2 * h:2 * h + 2, :], b_qk[h][:].rearrange("p (t c) -> p t c", t=2),
                                           ACT.Copy, scale=inv_wscale[:, 0:1]).then_inc(qk_copied, 1)
                            if k % 4:
                                hidden_copy(i, k // 4 + 1, CHUNKS[k % 4][h - 2][0])
                        if k % 4 == 0:
                            normed(i * 2 + (k // 4 + 1), (k // 4 + 1) % 2)
                        if k % 4 == 1:
                            high_parts(i * 2 + (k // 4 + 1))
                        if not (first and k < 2):
                            affine(i, k)
                        if not (first and k == 0):
                            square(i, k, not (first and k == 1))

                def tail():
                    v_begin(NB, 0, True)
                    freq_copy(NB, 0, True)
                    root(NB, 0, True)
                    affine(NB, 0)
                    square(NB, 0, True)
                    root(NB, 1, True)
                    affine(NB, 1)

                act.add_instruction(mybir.InstLoadActFuncSet(name=nc.get_next_instruction_name(),
                                                             act_func_set_id=EXP_AND_LN, engine=mybir.EngineType.Activation, ins=[], outs=[]))
                act.wait_ge(buffers_zeroed, 1)
                normed(0, 0)
                act.wait_ge(buffers_zeroed, 1)
                for chunk in range(8):
                    hidden_copy(0, 0, chunk)
                high_parts(0)
                run(act, body, tail)

            @blk.vector
            def _(v):
                def params(s, b):
                    if not isinstance(s, int) or s >= 2:
                        v.wait_ge(xn_masked, s - 1)
                        v.wait_ge(h_ready, s * 3 - 3)
                    v.tensor_copy(par[b][:], tab0[:, bass.ds(s, 1), :].rearrange("p a k -> p (a k)")).then_inc(par_ready, 1)

                def masks(s, b):
                    v.wait_ge(xn_made, s + 1)
                    v.wait_ge(par_ready, s + 1)
                    for p0, top, bottom in ((0, 1, SL - 1), (C, 0, SL - 2)):
                        for slot, col in ((top, 2), (bottom, 3)):
                            last = v.tensor_scalar(xn[p0:p0 + C, :, slot], xn[p0:p0 + C, :, slot],
                                                   par[b][p0:p0 + C, col:col + 1], None, ALU.mult)
                    last.then_inc(xn_masked, 1)

                def high_stacks(s, b):
                    if not isinstance(s, int) or s >= 2:
                        v.wait_ge(qk_conv, s * 8 - 8)
                    for row, col in ((0, 4), (R - 1, 5)):
                        v.tensor_scalar(hi_ind[b][C:P, 1:W + 1, row], ind[C:P, :, row], par[b][C:P, col:col + 1], None, ALU.mult)
                    if isinstance(s, int) and s < 2:
                        v.tensor_copy(hi_ind[b][C:P, 1:W + 1, 1:R - 1], ind[C:P, :, 1:R - 1])
                    v.wait_ge(hi_made, s + 1)
                    v.tensor_copy(hi_pair[b][:], hi_all[:, :, 1:1 + R])
                    v.tensor_copy(hi_ind[b][0:C], hi_all[0:C, :, 3:3 + R])
                    v.tensor_copy(hi_side[b][0:C], hi_all[0:C, :, 3:3 + R])
                    v.tensor_copy(hi_side[b][C:P, 0:W, :], hi_all[C:P, 2:W + 2, 2:2 + R])

                def high_below(s, b):
                    v.tensor_copy(hl_all[0:C, 1:W + 1, 0:SL], hi_all[0:C, 1:W + 1, 0:SL]).then_inc(below_copied, 1)

                def both_stacks(s, b):
                    v.wait_ge(below_copied, s + 1)
                    v.wait_ge(low_made, s * 2 + 2)
                    for d in range(3):
                        last = v.tensor_copy(hi_lo[b][d][:], hl_all[:, :, 1 + d:1 + d + R])
                    last.then_inc(stacks_ready, 1)

                EARLY = {0: 5, 1: 5, 2: 5, 3: 3}

                def taps(i, k, some):
                    b, c0 = ((k - 1) // 4) % 2, GCOL * ORDER[(k - 1) % 4]
                    v3 = v_s[(k - 1) % 4][:].rearrange("p (c r) -> p c r", r=R)
                    for n in some:
                        t = n if n < 4 else n + 1
                        dr, dc = TAPS[t]
                        if n == 0:
                            v.wait_ge(v_begun, i * 8 + k)
                        else:
                            v.wait_ge(tap_step, i * 64 + (8 * (k - 1) + n))
                        v.scalar_tensor_tensor(v3, hv[b][:, c0 + dc + 1:c0 + dc + 1 + GCOL, dr + 1:dr + 1 + R],
                                               v_vecs[:, t:t + 1], v3, ALU.mult, ALU.add).then_inc(tap_step, 1)

                def over_std(i, k, any_before):
                    v.wait_ge(rs_ready, i * 8 + (k - 1))
                    if any_before:
                        v.wait_ge(w_ready, i * 8 + (k - 2))
                    v.tensor_tensor(t_n[:], b_o[:], rs[:], ALU.mult).then_inc(t_ready, 1)

                def products(i, k, any_before, before_last):
                    v.wait_ge(k_swapped, i * 8 + k)
                    v.wait_ge(q_split, i * 8 + k)
                    if any_before:
                        v.wait_ge(inv_done, i * 8 + (k - 1))
                    v.tensor_tensor(u[:], q_re[:], b_k[:], ALU.mult).then_inc(k_read, 1)
                    n = EARLY[k % 4]
                    taps(i, k, (n,))
                    if before_last is not None:
                        over_std(i, k, before_last)
                    taps(i, k, (n + 1,))
                    v.wait_ge(u_step, i * 8 + k)
                    v.tensor_reduce(u_mean[:], u[:].rearrange("p (t c) -> p t c", t=4), AX_X, ALU.add).then_inc(u_summed, 1)
                    v.wait_ge(u_summed, i * 8 + k)
                    v.tensor_scalar(u_mean[:], u_mean[:], 1.0 / P, None, ALU.mult).then_inc(means_ready, 1)
                    taps(i, k, (n + 2,))

                def finish(i, k):
                    m = ((k - 4) % 4) // 2
                    sb_ = ((k - 4) // 4) % 2
                    done = i * 4 + (k - 2) // 2
                    v.wait_ge(fin_done, done)
                    strip_less_2 = i * 2 + ((k - 4) // 4 - 2)
                    if m == 0:
                        v.wait_ge(res_loaded[sb_], (i * 2 + (k - 4) // 4 - sb_) * 16 + 32)
                    if m == 0 and not (isinstance(i, int) and strip_less_2 < 0):
                        v.wait_ge(y_stored[sb_], (strip_less_2 - sb_) * 16 + 32)
                    y3 = b_y[:].rearrange("p (c r) -> p r c", r=R)
                    for h in range(2):
                        rows = slice(C * h, C * h + C)
                        last = v.scalar_tensor_tensor(ys[sb_][rows, :, GCOL * m:GCOL * m + GCOL], y3[rows], b_proj[rows, 0:1],
                                                      x_res[sb_][rows, :, GCOL * m:GCOL * m + GCOL], ALU.add, ALU.add)
                    last.then_inc(fin_read, 1)
                    v.wait_ge(fin_read, done)
                    v.bn_stats(y_stats[:, bass.ds(i * 4 + ((k - 2) // 2 - 1), 1), :].rearrange("p a k -> p (a k)"),
                               ys[sb_][:, :, GCOL * m:GCOL * m + GCOL]).then_inc(pair_ready, 1)

                def body(i, first):
                    for k in range(8):
                        s, b = i * 2 + (k // 4 + 1), (k // 4 + 1) % 2
                        if k % 4 == 3:
                            params(i * 2 + (k // 4 + 2), k // 4)
                        if k % 4 == 2:
                            high_stacks(s, b)
                        if not (first and k == 0):
                            taps(i, k, range(EARLY[k % 4]))
                            products(i, k, not (first and k == 1), None if first and k < 2 else not (first and k == 2))
                        if k % 4 == 2:
                            high_below(s, b)
                        if k % 4 == 3:
                            both_stacks(s, b)
                        if not (first and k == 0):
                            taps(i, k, range(EARLY[k % 4] + 3, 8))
                        if k % 2 == 0 and not (first and k < 4):
                            finish(i, k)
                        if k % 4 == 0:
                            masks(s, b)

                def tail():
                    taps(NB, 0, range(EARLY[0]))
                    products(NB, 0, True, True)
                    taps(NB, 0, range(EARLY[0] + 3, 8))
                    finish(NB, 0)
                    over_std(NB, 1, True)
                    finish(NB, 2)

                v.wait_ge(buffers_zeroed, 1)
                v.wait_ge(ind_loaded, 16)
                params(0, 0)
                params(1, 1)
                masks(0, 0)
                high_stacks(0, 0)
                high_below(0, 0)
                both_stacks(0, 0)
                run(v, body, tail)

        tab1 = sb("tab1", [P, N1 + 2, 10])
        wr = sb("wr", [P, P])
        with ExitStack() as ph:
            def tsb(name, shape, dt=F32):
                return ph.enter_context(nc.sbuf_tensor(name, shape, dt))

            def tsem(name):
                return ph.enter_context(nc.semaphore(name))

            mv = tsb("mv1", [P, NI, 2])
            tmp = tsb("tmp1", [P, 3, NI])
            wrs = tsb("wrs", [P, NI, P])
            yc = [tsb(f"yc{b}", [P, 4, W]) for b in range(4)]
            rst = tsb("rst", [P, NS, 12])
            rmv = tsb("rmv", [P, NI, 2])
            half_avg = tsb("half_avg", [P, P])
            const = tsb("const", [P, NI])
            vecs = tsb("vecs", [P, 3])
            acc = tsb("acc", [P, 8])
            w_loaded = tsem("w_loaded")
            y_loaded = [tsem(f"y_loaded{b}") for b in range(4)]
            r_made = tsem("r_made")
            r_read = tsem("r_read")
            step = tsem("gn1_step")
            asked = tsem("gn1_asked")
            answered = tsem("gn1_answered")
            scaled = tsem("wr_scaled")
            blk = ph.enter_context(nc.Block())
            NQ = NS // 4

            @blk.sync
            def _(sp):
                for dst, name in ((wr[:], "w_reduceT"), (half_avg[:], "half_avg"), (vecs[:], "bn_vecs"),
                                  (tab1[:], "tab1")):
                    sp.dma_start(dst, A[name]).then_inc(w_loaded, 16)

                def load(i, b, first):
                    rows = [(i * 4 + b) * R + (R + 4 * h) for h in range(2)]
                    if not first:
                        rows = [sp.snap(row) for row in rows]
                        sp.wait_ge(r_made, i * 8 + 2 * (b - 3))
                    for h, row in enumerate(rows):
                        sp.dma_start(yc[b][C * h:C * h + C], y1[:, bass.ds(row, 4), :]).then_inc(y_loaded[b], 16)

                for b in range(4):
                    load(0, b, True)
                if NQ > 1:
                    with sp.Fori(1, NQ) as i:
                        for b in range(4):
                            load(i, b, False)

            @blk.scalar
            def _(act):
                group_norm_root(act, asked, answered, tmp)
                act.wait_ge(asked, 4)
                act.activation(acc[:, 7:8], acc[:, 7:8], ACT.Sqrt).then_inc(answered, 1)

            @blk.tensor
            def _(pe):
                pe.wait_ge(asked, 1)
                pe.matmul(bank[0][:, 0:2 * NI], pair_avg[:], tmp[:, 0:2, :].rearrange("p a i -> p (a i)"),
                          start=True, stop=True).then_inc(answered, 1)
                pe.wait_ge(scaled, 1)
                pe.matmul(bank[1][:, 0:NI], wr[:], gn_bias[:, 1, :], start=True, stop=True).then_inc(answered, 1)

                def products(img, j, b, first):
                    i = img * (NQ // NI) + j
                    pe.wait_ge(y_loaded[b], i * 32 + 32)
                    for h in range(2):
                        bk = 2 + 2 * (b % 2) + h
                        if not (first and b < 2):
                            pe.wait_ge(r_read, i * 8 + (2 * b + h - 3))
                        last = pe.matmul(bank[bk][:], wrs[:, img, :], yc[b][:, 2 * h:2 * h + 2, :].rearrange("p r w -> p (r w)"),
                                         start=True, stop=True)
                        last.then_inc(r_made, 1)

                for img in range(NI):
                    if img == 0:
                        for b in range(4):
                            products(0, 0, b, True)
                    j0 = 1 if img == 0 else 0
                    if NQ // NI > j0:
                        with pe.Fori(j0, NQ // NI) as j:
                            for b in range(4):
                                products(img, j, b, False)
                pe.wait_ge(asked, 3)
                pe.matmul(bank[1][:, 0:2], half_avg[:], acc[:, 0:2], start=True, stop=True).then_inc(answered, 1)

            @blk.vector
            def _(v):
                PERI = 2 * NS // NI
                for i in range(NI):
                    last = v.bn_aggr(mv[:, i, :], y_stats[:, PERI * i:PERI * i + PERI, :].rearrange("p a k -> p (a k)"))
                last.then_inc(step, 1)
                v.wait_ge(step, 1)
                count = [1]
                then = group_norm_params((step, asked, answered, count), v, 1, mv, tmp)
                v.wait_ge(w_loaded, 64)
                for i in range(NI):
                    last = v.tensor_scalar(wrs[:, i, :], wr[:], gn_scale[:, 1, i:i + 1], None, ALU.mult)
                last.then_inc(scaled, 1)
                with v.Fori(0, NQ) as i:
                    for b in range(4):
                        for h in range(2):
                            v.wait_ge(r_made, i * 8 + (2 * b + h + 1))
                            v.bn_stats(rst[:, bass.ds(i * 4 + b, 1), 6 * h:6 * h + 6].rearrange("p a k -> p (a k)"),
                                       bank[2 + 2 * (b % 2) + h][:]).then_inc(r_read, 1)
                v.wait_ge(r_read, 2 * NS)
                for i in range(NI):
                    last = v.bn_aggr(rmv[:, i, :], rst[:, S * i:S * i + S, :].rearrange("p a k -> p (a k)"))
                then(last)
                v.wait_ge(answered, 3)
                then(v.tensor_copy(const[:], bank[1][:, 0:NI]))
                then(v.tensor_tensor(rmv[:, :, 0], rmv[:, :, 0], const[:], ALU.add))
                then(v.tensor_scalar(rmv[:, :, 0], rmv[:, :, 0], vecs[:, 0:1], None, ALU.add))
                then(v.tensor_tensor(const[:], rmv[:, :, 0], rmv[:, :, 0], ALU.mult))
                then(v.tensor_tensor(rmv[:, :, 1], rmv[:, :, 1], const[:], ALU.add))
                then(v.tensor_reduce(acc[:, 0:2], rmv[:].rearrange("p i k -> p k i"), AX_X, ALU.add))
                v.tensor_copy(acc[:, 2:4], acc[:, 0:2]).then_inc(asked, 1)
                v.wait_ge(answered, 4)
                then(v.tensor_scalar(acc[:, 4:6], bank[1][:, 0:2], 1.0 / NI, None, ALU.mult))
                then(v.tensor_tensor(acc[:, 6:7], acc[:, 4:5], acc[:, 4:5], ALU.mult))
                then(v.tensor_tensor(acc[:, 7:8], acc[:, 5:6], acc[:, 6:7], ALU.subtract))
                v.tensor_scalar(acc[:, 7:8], acc[:, 7:8], 0.0, BN_EPS, ALU.max, ALU.add).then_inc(asked, 1)
                v.wait_ge(answered, 5)
                then(v.reciprocal(acc[:, 7:8], acc[:, 7:8]))
                then(v.tensor_tensor(bn_alpha[:], acc[:, 7:8], vecs[:, 1:2], ALU.mult))
                then(v.tensor_tensor(acc[:, 6:7], vecs[:, 0:1], acc[:, 4:5], ALU.subtract))
                then(v.scalar_tensor_tensor(bn_shift[:], acc[:, 6:7], bn_alpha[:, 0:1], vecs[:, 2:3], ALU.mult, ALU.add))
                for kind, src in ((0, gn_scale), (4, gn_bias)):
                    for i in range(NI):
                        lo = S * i + 1
                        then(v.tensor_copy(tab1[:, lo:lo + S, kind:kind + 4],
                                           src[:, 1:2, i:i + 1].to_broadcast([P, S, 4])))
                    nxt = tab1[C:P, 0:S * (NI - 1) + 1:S, :] if NI > 1 else tab1[C:P, 0:1, :]
                    for col in (1, 3):
                        then(v.tensor_copy(nxt[:, :, kind + col], src[C:P, 1, :]))
                    then(v.memset(tab1[C:P, S:NS + 1:S, kind + 2:kind + 3], 0.0))
                    then(v.memset(tab1[0:C, S:NS + 1:S, kind + 3:kind + 4], 0.0))

        with ExitStack() as ph:
            def tsb(name, shape, dt=F32):
                return ph.enter_context(nc.sbuf_tensor(name, shape, dt))

            def tsem(name):
                return ph.enter_context(nc.semaphore(name))

            xa = [tsb(f"xa{b}", [P, 4, W]) for b in range(2)]
            xb = [tsb(f"xb{b}", [P, 5, W]) for b in range(4)]
            x_mid = [tsb(f"x_mid{b}", [P, 4, WP]) for b in range(2)]
            x_up = [tsb(f"x_up{b}", [P, 4, WP]) for b in range(2)]
            x_down = [tsb(f"x_down{b}", [P, 4, WP]) for b in range(2)]
            par = [tsb(f"par1_{b}", [P, 10]) for b in range(4)]
            rn = tsb("rn", [P, 1024])
            prod = [tsb(f"prod{k}", [P, 1024]) for k in range(9)]
            inv = tsb("inv", [P, 1024])
            ab = tsb("ab", [P, 1024])
            z = [tsb(f"z{b}", [P, 5, WP]) for b in range(2)]
            pre = tsb("pre", [P, 1024])
            ab2 = tsb("ab2", [P, 1024])
            res = [tsb(f"res{b}", [P, 1024]) for b in range(2)]
            kern = tsb("kern", [P, 1024])
            kern_rest = tsb("kern_rest", [P, 1024])
            kern_parts = [tsb(f"kern_parts{b}", [P, 1024], BF16) for b in range(2)]
            sel = tsb("sel", [P, 9, P], BF16)
            sel_f = tsb("sel_f", [P, 9, P])
            span_w = tsb("span_w", [P, P])
            span_b = tsb("span_b", [P, 1])
            conv_w = tsb("conv_w", [P, 6, P])
            conv_b = tsb("conv_b", [P, 1])

            w_loaded = tsem("w1_loaded")
            xa_loaded = [tsem(f"xa_loaded{b}") for b in range(2)]
            xb_loaded = [tsem(f"xb_loaded{b}") for b in range(4)]
            zeroed = tsem("zeroed1")
            par_ready = tsem("par1_ready")
            mid_normed = tsem("mid_normed")
            normed = tsem("normed")
            r_done = tsem("r_done")
            rn_ready = tsem("rn_ready")
            kern_made = tsem("kern_made")
            kern_copied = tsem("kern_copied")
            rest_made = tsem("rest_made")
            second_made = tsem("second_made")
            parts_ready = tsem("parts_ready")
            sel_ready = tsem("sel_ready")
            kern_done = tsem("kern_done")
            prod_ready = tsem("prod_ready")
            half_sum = tsem("half_sum")
            pool_step = tsem("pool_step")
            sum_step = tsem("sum_step")
            exp_step = tsem("exp_step")
            log_ready = tsem("log_ready")
            z_written = tsem("z_written")
            row_copied = tsem("row_copied")
            z_ready = tsem("z_ready")
            conv_done = [tsem(f"conv_done{h}") for h in range(2)]
            conv_copied = [tsem(f"conv_copied{h}") for h in range(2)]
            exp2_step = tsem("exp2_step")
            log2_ready = tsem("log2_ready")
            resid_added = tsem("resid_added")
            out_ready = tsem("out_ready")
            out_stored = [tsem(f"out_stored{b}") for b in range(2)]
            blk = ph.enter_context(nc.Block())

            b_kern = (bank_pair[0], bank_pair[1])
            b_r = bank_pair[2]
            b_c = bank_pair[3]
            flat = lambda t: t[:].rearrange("p a b -> p (a b)")
            NB1 = N1 // 4

            def run1(eng, body):
                body(0, True)
                if NB1 > 1:
                    with eng.Fori(1, NB1) as i:
                        body(i, False)

            @blk.sync
            def _(sp):
                def load_a(r, r1, b):
                    sp.dma_start(xa[b % 2][0:C], y1_by_parity[:, 1, bass.ds(r, 4), :]).then_inc(xa_loaded[b % 2], 16)
                    sp.dma_start(xa[b % 2][C:P], y1_by_parity[:, 0, bass.ds(r1, 4), :]).then_inc(xa_loaded[b % 2], 16)

                def load_b(r, b):
                    sp.dma_start(xb[b][0:C], y1_by_parity[:, 0, bass.ds(r, 5), :]).then_inc(xb_loaded[b], 16)
                    sp.dma_start(xb[b][C:P], y1_by_parity[:, 1, bass.ds(r, 5), :]).then_inc(xb_loaded[b], 16)

                def store(r, b):
                    for h in range(2):
                        sp.dma_start(out_by_parity[:, h, bass.ds(r, 4), :],
                                     res[b % 2][C * h:C * h + C].rearrange("p (r w) -> p r w", w=W)).then_inc(out_stored[b % 2], 16)

                def body(i, first):
                    for k in range(4):
                        to, of, of1 = (i * 16 + n for n in (4 * (k - 2), 4 * (k + 2), 4 * (k + 2) + 1))
                        strips_normed, strips_out = i * 4 + (k + 1), i * 4 + (k - 1)
                        if not first:
                            to, of, of1 = sp.snap(to), sp.snap(of), sp.snap(of1)
                            strips_normed, strips_out = sp.snap(strips_normed), sp.snap(strips_out)
                        if first and k < 2:
                            sp.wait_ge(normed, strips_normed)
                        else:
                            sp.wait_ge(resid_added, strips_out)
                        load_a(of, of1, (k + 2) % 4)
                        load_b(of, (k + 2) % 4)
                        if not (first and k < 2):
                            sp.wait_ge(out_ready, strips_out)
                            store(to, (k - 2) % 4)

                for dst, name in ((span_w[:], "span_w"), (span_b[:], "span_b"), (sel_f[:], "sel"), (conv_w[:], "conv_w"), (conv_b[:], "conv_b")):
                    sp.dma_start(dst, A[name]).then_inc(w_loaded, 16)
                for u in range(2):
                    load_a(4 * u, 4 * u + 1, u)
                    load_b(4 * u, u)
                run1(sp, body)
                for b in range(2):
                    sp.wait_ge(out_stored[b], 32 * ((N1 - 2) // 2))
                sp.wait_ge(xa_loaded[1], 32 * (N1 // 2 + 1))
                sp.wait_ge(xb_loaded[0], 32 * (N1 // 4 + 1))
                sp.wait_ge(xb_loaded[1], 32 * (N1 // 4 + 1))

            @blk.gpsimd
            def _(pool):
                for t in x_mid + x_up + x_down + z:
                    last = nc.gpsimd.memset(t[:], 0.0)
                last.then_inc(zeroed, 1)
                for t in kern_parts:
                    last = nc.gpsimd.memset(t[:], 0.0)
                last.then_inc(zeroed, 1)

                def body(i, first):
                    for k in range(4):
                        for n in range(5):
                            pool.wait_ge(prod_ready, i * 36 + (9 * k + n + 2))
                            if n:
                                pool.wait_ge(pool_step, i * 16 + (4 * k + n))
                            ins = nc.gpsimd.tensor_tensor(prod[0][:], prod[0][:], prod[n + 1][:], ALU.add)
                            ins.then_inc(pool_step if n < 4 else half_sum, 1)
                        if not (first and k < 2):
                            pool.wait_ge(conv_copied[0], i * 4 + (k - 1))
                            pool.wait_ge(conv_copied[1], i * 4 + (k - 1))
                            if not (first and k < 4):
                                pool.wait_ge(out_stored[k % 2], (i * 4 + (k - 2) - k % 2 - 2) * 16 + 32)
                            nc.gpsimd.tensor_tensor(res[k % 2][:], pre[:], flat(xb[(k - 2) % 4])[:, 0:1024], ALU.add)\
                                .then_inc(resid_added, 1)
                            pool.wait_ge(resid_added, i * 4 + (k - 1))
                            pool.wait_ge(log2_ready, i * 4 + (k - 1))
                            nc.gpsimd.tensor_tensor(res[k % 2][:], res[k % 2][:], ab2[:], ALU.add).then_inc(out_ready, 1)

                run1(pool, body)

            @blk.tensor
            def _(pe):
                def r_product(u, b, h, before):
                    if h == 0:
                        pe.wait_ge(mid_normed, u + 1)
                        if before:
                            pe.wait_ge(kern_copied, u + 0)
                    pe.matmul(b_r[:, h, :], wr[:], x_mid[b][:, 2 * h:2 * h + 2, 1:W + 1], start=True, stop=True)\
                        .then_inc(r_done, 1)

                def weights(u, h):
                    if h == 0:
                        pe.wait_ge(rn_ready, u + 1)
                    pe.matmul(b_r[:, h, :], span_w[:], rn[:, 512 * h:512 * h + 512], start=True, stop=True)\
                        .then_inc(kern_made, 1)

                def conv(k, h, products):
                    for n in products:
                        j, dc = n // 3, n % 3
                        last = pe.matmul(b_c[:, h, :], conv_w[:, n, :], z[k % 2][:, 2 * h + j:2 * h + j + 2, dc:dc + W],
                                         start=n == 0, stop=n == 5)
                    if n == 5:
                        last.then_inc(conv_done[h], 1)

                def body(i, first):
                    for k in range(4):
                        pe.wait_ge(parts_ready, i * 4 + (k + 1))
                        for n in range(9):
                            if not (first and 9 * k + n < 2):
                                pe.wait_ge(prod_ready, i * 36 + (9 * k + n - 1))
                            for h in range(2):
                                last = pe.matmul(b_kern[(9 * k + n) % 2][:, h, :], sel[:, n, :],
                                                 kern_parts[k % 2][:, 512 * h:512 * h + 512], start=True, stop=True)
                            last.then_inc(kern_done, 1)
                            if n < 5 and not (first and k < 2):
                                conv(k - 2, 1, (n + 1,))
                            if n in (4, 5):
                                r_product(i * 4 + (k + 1), (k + 1) % 2, n - 4, True)
                            if n >= 7:
                                weights(i * 4 + (k + 1), n - 7)
                        if not (first and k == 0):
                            pe.wait_ge(z_ready, i * 4 + k)
                            if not (first and k == 1):
                                pe.wait_ge(conv_copied[0], i * 4 + (k - 1))
                            conv(k - 1, 0, range(6))
                            if not (first and k == 1):
                                pe.wait_ge(conv_copied[1], i * 4 + (k - 1))
                            conv(k - 1, 1, (0,))

                pe.wait_ge(w_loaded, 80)
                pe.wait_ge(sel_ready, 1)
                for h in range(2):
                    r_product(0, 0, h, False)
                for h in range(2):
                    weights(0, h)
                run1(pe, body)

            @blk.scalar
            def _(act):
                def norm(u, b, src, s0, dst, col):
                    p = par[b]
                    act.activation(dst[b % 2][:, 0:3, 1:W + 1], src[:, s0:s0 + 3, :], ACT.Identity,
                                   bias=p[:, 4:5], scale=p[:, 0:1])
                    return act.activation(dst[b % 2][:, 3, 1:W + 1], src[:, s0 + 3, :], ACT.Identity,
                                          bias=p[:, 4 + col:5 + col], scale=p[:, col:col + 1])

                def norm_mid(u, b, before):
                    act.wait_ge(xa_loaded[b % 2], (u - b % 2) * 16 + 32)
                    act.wait_ge(par_ready, u + 1)
                    if before:
                        act.wait_ge(prod_ready, (u - 1) * 9)
                        act.wait_ge(r_done, (u - 1) * 2)
                    norm(u, b, xa[b % 2], 0, x_mid, 1).then_inc(mid_normed, 1)

                def norm_up(u, b):
                    act.wait_ge(xb_loaded[b], (u - b) * 8 + 32)
                    norm(u, b, xb[b], 0, x_up, 2)

                def norm_down(u, b):
                    norm(u, b, xb[b], 1, x_down, 3).then_inc(normed, 1)

                def edge_rows(i, k):
                    b, masks = (k - 1) % 2, par[(k - 1) % 4][:, 8:10]
                    act.wait_ge(z_written, i * 4 + k)
                    act.activation(z[1 - b][:, 0, 1:W + 1], z[b][:, 4, 1:W + 1], ACT.Copy, scale=masks[:, 0:1]).then_inc(row_copied, 1)
                    act.wait_ge(row_copied, i * 4 + k)
                    act.activation(z[b][:, 4, 1:W + 1], z[b][:, 4, 1:W + 1], ACT.Copy, scale=masks[:, 1:2]).then_inc(z_ready, 1)

                def second_parts(u, b):
                    act.wait_ge(rest_made, u + 1)
                    act.copy(kern_parts[b][C:P], kern_rest[C:P]).then_inc(second_made, 1)

                def bn_relu(u, before):
                    act.wait_ge(r_done, u * 2 + 2)
                    if before:
                        act.wait_ge(kern_made, u * 2)
                    act.activation(rn[:], flat(b_r), ACT.Relu, bias=bn_shift[:, 0:1],
                                   scale=bn_alpha[:, 0:1]).then_inc(rn_ready, 1)

                def weights_copy(u, b, before):
                    act.wait_ge(kern_made, u * 2 + 2)
                    if before:
                        act.wait_ge(rest_made, u + 0)
                    if not isinstance(u, int) or u >= 2:
                        act.wait_ge(kern_done, (u - 1) * 9)
                    act.activation(kern[:], flat(b_r), ACT.Identity, bias=span_b[:, 0:1])
                    act.activation(kern_parts[b][:], flat(b_r), ACT.Identity, bias=span_b[:, 0:1]).then_inc(kern_copied, 1)

                def conv_copy(i, k, h):
                    act.wait_ge(conv_done[h], i * 4 + (k - 1))
                    part = slice(512 * h, 512 * h + 512)
                    act.activation(ab2[:, part], b_c[:, h, :], ACT.Abs, bias=conv_b[:, 0:1]).then_inc(exp2_step, 1)
                    act.activation(pre[:, part], b_c[:, h, :], ACT.Relu, bias=conv_b[:, 0:1]).then_inc(conv_copied[h], 1)

                def body(i, first):
                    for k in range(4):
                        if not (first and k == 0):
                            act.wait_ge(sum_step, i * 12 + 3 * k)
                            if not (first and k == 1):
                                act.wait_ge(z_written, i * 4 + (k - 1))
                            act.activation(ab[:], inv[:], ACT.Abs).then_inc(exp_step, 1)
                            act.wait_ge(exp_step, i * 8 + (2 * k - 1))
                            act.activation(ab[:], ab[:], ACT.Exp, scale=-1.0).then_inc(exp_step, 1)
                            act.wait_ge(exp_step, i * 8 + 2 * k)
                            act.activation(ab[:], ab[:], ACT.Ln, bias=1.0).then_inc(log_ready, 1)
                        u1, b1 = i * 4 + (k + 1), (k + 1) % 4
                        norm_mid(u1, b1, not (first and k == 0))
                        norm_up(u1, b1)
                        if not (first and k == 0):
                            edge_rows(i, k)
                        bn_relu(u1, True)
                        norm_down(u1, b1)
                        if not (first and k < 2):
                            if not (first and k == 2):
                                act.wait_ge(out_ready, i * 4 + (k - 2))
                            conv_copy(i, k, 0)
                        weights_copy(u1, (k + 1) % 2, True)
                        if not (first and k < 2):
                            conv_copy(i, k, 1)
                        second_parts(u1, (k + 1) % 2)
                        if not (first and k < 2):
                            act.wait_ge(exp2_step, i * 12 + (3 * (k - 1) - 1))
                            act.activation(ab2[:], ab2[:], ACT.Exp, scale=-1.0).then_inc(exp2_step, 1)
                            act.wait_ge(exp2_step, i * 12 + 3 * (k - 1))
                            act.activation(ab2[:], ab2[:], ACT.Ln, bias=1.0).then_inc(log2_ready, 1)

                act.add_instruction(mybir.InstLoadActFuncSet(name=nc.get_next_instruction_name(),
                                                             act_func_set_id=EXP_AND_LN, engine=mybir.EngineType.Activation, ins=[], outs=[]))
                act.wait_ge(zeroed, 2)
                act.wait_ge(w_loaded, 80)
                norm_mid(0, 0, False)
                norm_up(0, 0)
                norm_down(0, 0)
                bn_relu(0, False)
                weights_copy(0, 0, False)
                second_parts(0, 0)
                run1(act, body)

            @blk.vector
            def _(v):
                def params(u, b):
                    if not isinstance(u, int) or u >= 4:
                        v.wait_ge(normed, u - 3)
                        v.wait_ge(z_ready, u - 3)
                    v.tensor_copy(par[b][:], tab1[:, bass.ds(u, 1), :].rearrange("p a k -> p (a k)")).then_inc(par_ready, 1)

                def z_finish(i, k, third):
                    b = (k - 1) % 2
                    v.wait_ge(log_ready, i * 4 + k)
                    if third:
                        v.wait_ge(conv_done[1], i * 4 + (k - 2))
                    if not (isinstance(i, int) and k == 1):
                        v.wait_ge(conv_done[0], i * 4 + (k - 1))
                    v.scalar_tensor_tensor(z[b][:, 1:5, 1:W + 1], inv[:].rearrange("p (r w) -> p r w", w=W), 0.0,
                                           ab[:].rearrange("p (r w) -> p r w", w=W), ALU.max, ALU.add).then_inc(z_written, 1)

                def rest(u, b):
                    v.wait_ge(kern_copied, u + 1)
                    v.tensor_tensor(kern_rest[C:P], kern[C:P], kern_parts[b][C:P], ALU.subtract).then_inc(rest_made, 1)

                def third_parts(u, b):
                    v.wait_ge(second_made, u + 1)
                    v.tensor_tensor(kern_parts[b][96:P], kern_rest[96:P], kern_parts[b][96:P], ALU.subtract).then_inc(parts_ready, 1)

                def body(i, first):
                    for k in range(4):
                        b = k % 2
                        for n, (dr, dc) in enumerate(TAPS):
                            src = {-1: x_up, 0: x_mid, 1: x_down}[dr][b]
                            v.wait_ge(kern_done, i * 36 + (9 * k + n + 1))
                            if n == 0:
                                v.wait_ge(normed, i * 4 + (k + 1))
                            if n == 0 and not (first and k == 0):
                                v.wait_ge(sum_step, i * 12 + 3 * k)
                            if n < 6 and not (first and k == 0):
                                v.wait_ge(half_sum, i * 4 + k)
                            v.tensor_tensor(prod[n][:].rearrange("p (r w) -> p r w", w=W),
                                            flat(b_kern[(9 * k + n) % 2]).rearrange("p (r w) -> p r w", w=W),
                                            src[:, :, 1 + dc:1 + dc + W], ALU.mult).then_inc(prod_ready, 1)
                            if n == 2 and not (first and k == 0):
                                z_finish(i, k, not (first and k < 3))
                            if n == 3:
                                params(i * 4 + (k + 2), (k + 2) % 4)
                        for n, (a, c) in enumerate(((prod[6], prod[7]), (inv, prod[8]), (inv, prod[0]))):
                            if n == 0:
                                v.wait_ge(prod_ready, i * 36 + (9 * k + 9))
                                if not (first and k == 0):
                                    v.wait_ge(z_written, i * 4 + k)
                            else:
                                v.wait_ge(sum_step, i * 12 + (3 * k + n))
                            if n == 1:
                                rest(i * 4 + (k + 1), (k + 1) % 2)
                            if n == 2:
                                third_parts(i * 4 + (k + 1), (k + 1) % 2)
                                v.wait_ge(half_sum, i * 4 + (k + 1))
                            v.tensor_tensor(inv[:], a[:], c[:], ALU.add).then_inc(sum_step, 1)

                v.wait_ge(zeroed, 1)
                v.wait_ge(w_loaded, 80)
                nc.vector.tensor_copy(sel[:], sel_f[:]).then_inc(sel_ready, 1)
                params(0, 0)
                params(1, 1)
                rest(0, 0)
                third_parts(0, 0)
                run1(v, body)



def shape_constants(NI, S):
    NS, N1 = NI * S, strips_of_layer1(NI * S)
    out = {}
    m = np.arange(P)
    row, patch, col = m % 8, m // 64, m // 8 % 8
    real = [(0, 0), (0, 4), (4, 0), (4, 4)]
    pairs = [(u, w) for u in range(8) for w in range(8) if (u, w) not in real and (u, w) < ((-u) % 8, (-w) % 8)]
    assert len(pairs) == 30
    slots = []
    for half in range(2):
        slots += [(pt, u, w, "r") for pt in range(2) for u, w in real[2 * half:2 * half + 2]]
        slots += [(pt, u, w, "RI"[half]) for pt in range(2) for u, w in pairs]
    f_all, g_all = np.zeros((P, P)), np.zeros((P, P))
    for f, (pt, u, w, kind) in enumerate(slots):
        th = 2 * np.pi * (u * row + w * col) / 8
        wave = (-np.sin(th) if kind == "I" else np.cos(th)) * (patch == pt)
        f_all[:, f] = wave
        g_all[f] = wave * (1 if kind == "r" else 2) / 64
    out["dft"], out["idft"] = f_all, g_all
    out["imag_sign"] = np.stack([-1.0 * (m % C >= 4), 1.0 * (m % C >= 4)], axis=1)
    out["mean_w"] = np.full((P, P), 1.0 / P)
    ch = m % C
    out["pair_avg"] = (ch[:, None] // 2 == ch[None, :] // 2) / 4.0
    out["half_avg"] = (ch[:, None] == ch[None, :]) / 2.0
    tab0 = np.ones((P, NS + 2, 6))
    tap = (m - C) % 9
    for s in range(NS + 2):
        top, bottom = s % S == 0, s % S == S - 1
        tab0[:, s, 2], tab0[:, s, 3] = not top, not bottom
        tab0[:, s, 4] = np.where(tap < 3, not top, 1)
        tab0[:, s, 5] = np.where(tap >= 6, not bottom, 1)
    out["tab0"] = tab0
    tab1 = np.zeros((P, N1 + 2, 10))
    tab1[:, :, 8:10] = 1
    for u in range(0, N1 + 2):
        if u % S == 0:
            tab1[0:C, u, 8] = 0
            tab1[C:P, u, 9] = 0
    out["tab1"] = tab1
    b_sel = np.zeros((P, 2))
    b_sel[C:C + 9, 0] = 1
    b_sel[C + 9:C + 18, 1] = 1
    out["b_sel"] = b_sel
    out = {n: a.astype(np.float32) for n, a in out.items()}
    ind = np.zeros((P, W, R), np.float16)
    for part in range(2):
        for t, (dr, dc) in enumerate(TAPS):
            ind[C + 9 * part + t] = 1
            if dc == -1:
                ind[C + 9 * part + t, 0] = 0
            if dc == 1:
                ind[C + 9 * part + t, W - 1] = 0
    out["ind"] = ind
    return out


def two(a):
    return np.concatenate([a, a], axis=0)


def block_diagonal(a):
    out = np.zeros((P, P), a.dtype)
    out[0:C, 0:C] = a
    out[C:P, C:P] = a
    return out


def kernel(**inputs):
    import concourse.bacc as _bacc
    from concourse.bass_utils import run_bass_kernel_spmd as _run

    g = {n: np.asarray(a) for n, a in inputs.items()}
    x = g["x"]
    NI, _, H, _ = x.shape
    S = H // R
    NS, N1 = NI * S, strips_of_layer1(NI * S)
    arrays = shape_constants(NI, S)
    xt = np.zeros((C, 1 + NI * H + XTRA, W), x.dtype)
    xt[:, 1:1 + NI * H] = x.transpose(1, 0, 2, 3).reshape(C, NI * H, W)
    arrays["x"] = xt
    arrays["wh"] = two(g["L0_conv_w_hidden"][:KQ].T)
    taps = g["L0_conv_w_dw"][:KQ].reshape(KQ, 9).T
    arrays["v_hiddenT"] = g["L0_conv_w_hidden"][KQ:].T
    arrays["v_vecs"] = np.concatenate([g["L0_conv_w_dw"][KQ:].reshape(P, 9), g["L0_conv_b_hidden"][KQ:, None],
                                       g["L0_conv_b_dw"][KQ:, None]], axis=1)
    arrays["w_dw"] = np.broadcast_to(taps[None], (P, 9, KQ))
    rows = np.zeros((P, KQ), x.dtype)
    b_rows, d_rows = rows.copy(), rows.copy()
    for part in range(2):
        p0 = C + 9 * part
        rows[p0:p0 + 9] = taps
        b_rows[p0:p0 + 9] = g["L0_conv_b_hidden"][:KQ]
        d_rows[p0 + 4] = g["L0_conv_b_dw"][:KQ]
    arrays["w_dw_rows"], arrays["b_hidden_rows"], arrays["b_dw_rows"] = rows, b_rows, d_rows
    arrays["ln_wb"] = np.stack([g["L0_conv_ln_w"], g["L0_conv_ln_b"]], axis=1)
    arrays["w_projT"] = g["L0_conv_w_proj"].T
    arrays["b_proj"] = two(g["L0_conv_b_proj"])[:, None]
    arrays["w_reduceT"] = block_diagonal(g["L1_conv_w_reduce"].T)
    arrays["bn_vecs"] = two(np.stack([g["L1_conv_b_reduce"], g["L1_conv_bn_gamma"], g["L1_conv_bn_beta"]], axis=1))
    span, span_b, sel = np.zeros((P, P), x.dtype), np.zeros((P, 1), x.dtype), np.zeros((P, 9, P), np.float32)
    for part in (0, 64, 96):
        for p in range(2):
            rows = slice(part + 9 * p, part + 9 * p + 9)
            span[C * p:C * p + C, rows] = g["L1_conv_w_span"].T
            span_b[rows, 0] = g["L1_conv_b_span"]
            for n in range(9):
                sel[part + 9 * p + n, n, C * p:C * p + C] = 1
    arrays["span_w"], arrays["span_b"], arrays["sel"] = span, span_b, sel
    w2 = g["L1_conv_w_conv2"]
    cw = np.zeros((P, 6, P), x.dtype)
    for dc in range(3):
        cw[0:C, dc, 0:C] = w2[:, :, 0, dc].T
        cw[C:P, dc, 0:C] = w2[:, :, 1, dc].T
        cw[C:P, dc, C:P] = w2[:, :, 0, dc].T
        cw[0:C, 3 + dc, 0:C] = w2[:, :, 2, dc].T
        cw[0:C, 3 + dc, C:P] = w2[:, :, 1, dc].T
        cw[C:P, 3 + dc, C:P] = w2[:, :, 2, dc].T
    arrays["conv_w"] = cw
    arrays["conv_b"] = two(g["L1_conv_b_conv2"])[:, None]
    arrays = {n: np.ascontiguousarray(a) for n, a in arrays.items()}

    nc = _bacc.Bacc("TRN2", target_bir_lowering=False, num_devices=1)
    A, feeds = {}, {}
    for name, a in arrays.items():
        feeds[f"in_{name}_dram"] = a
        A[name] = nc.dram_tensor(f"in_{name}_dram", a.shape, mybir.dt.from_np(a.dtype), kind="ExternalInput").ap()
    A["out"] = nc.dram_tensor("out_0_dram", (C, R * N1, W), F32, kind="ExternalOutput").ap()
    build_program(nc, A, NI, S)
    r = _run(nc, [feeds], core_ids=[0])
    out = np.asarray(r.results[0]["out_0_dram"])[:, R:R + NI * H]
    return np.ascontiguousarray(out.reshape(C, NI, H, W).transpose(1, 0, 2, 3))
```
